# Optimizing a Trainium2 kernel written in Bass

```python
import numpy as np
import jax
import jax.numpy as jnp

def _softmax(x, axis=-1):
    return jax.nn.softmax(x, axis=axis)

def _gelu(x):
    return jax.nn.gelu(x, approximate=True)

def _silu(x):
    return jax.nn.silu(x)

def _sigmoid(x):
    return jax.nn.sigmoid(x)

def _layernorm(x, axis=-1, eps=1e-05):
    m = jnp.mean(x, axis=axis, keepdims=True)
    v = jnp.var(x, axis=axis, keepdims=True)
    return (x - m) / jnp.sqrt(v + eps)

def _scatter_add(tgt, idx, src, axis=0):
    return tgt.at[idx].add(src)

def _segment_sum(src, seg, n):
    return jax.ops.segment_sum(src, seg, n)
kernel_name = 'mk_gnn_resnorm_d4_gnn_r8_a44f54'

def setup_inputs(seed: int=0):
    np.random.seed(seed)
    _w = jnp.asarray

    def _rec_inputs():
        import jax
        import jax.numpy as jnp
        _gk = jax.random.key(seed)
        x = -0.000202 + 1 * jax.random.normal(jax.random.fold_in(_gk, 1), (6250, 128), jnp.float32)
        _s = jax.random.randint(jax.random.fold_in(_gk, 2), (100000,), 0, 6250, jnp.int32)
        _d = jax.random.randint(jax.random.fold_in(_gk, 3), (100000,), 0, 6250, jnp.int32)
        _loop = jnp.arange(6250, dtype=jnp.int32)
        src = jnp.concatenate([_s, _d, _loop])
        dst = jnp.concatenate([_d, _s, _loop])
        _o = jnp.argsort(dst, stable=True)
        src = src[_o]
        dst = dst[_o]
        edge_attr_64 = 0.000189758 + 1.00013 * jax.random.normal(jax.random.fold_in(_gk, 12), (206250, 64), jnp.float32)
        return (x, src, dst, edge_attr_64)
    x, src, dst, edge_attr_64 = _rec_inputs()

    def _L0_gnn_setup():
        import jax, jax.numpy as jnp
        import numpy as np
        N_NODES = 6250
        N_EDGES = 100000
        NODE_DIM = 128
        EDGE_DIM = 64
        HIDDEN = 128
        EPS = 1e-05

        def _glorot(key, shape):
            fan_in, fan_out = (shape[0], shape[1])
            lim = (6.0 / (fan_in + fan_out)) ** 0.5
            return jax.random.uniform(key, shape, jnp.float32, -lim, lim)
        key = jax.random.key(seed)
        ks = jax.random.split(key, 12)
        node_features = jax.random.normal(ks[0], (N_NODES, NODE_DIM), jnp.float32)
        edge_index = jax.random.randint(ks[1], (2, N_EDGES), 0, N_NODES, jnp.int64)
        edge_features = jax.random.normal(ks[2], (N_EDGES, EDGE_DIM), jnp.float32)
        W1 = _glorot(ks[3], (2 * NODE_DIM + EDGE_DIM, HIDDEN))
        b1 = jnp.zeros((HIDDEN,), jnp.float32)
        W2 = _glorot(ks[4], (HIDDEN, HIDDEN))
        b2 = jnp.zeros((HIDDEN,), jnp.float32)
        U1 = _glorot(ks[5], (NODE_DIM + HIDDEN, HIDDEN))
        c1 = jnp.zeros((HIDDEN,), jnp.float32)
        U2 = _glorot(ks[6], (HIDDEN, NODE_DIM))
        c2 = jnp.zeros((NODE_DIM,), jnp.float32)
        gamma = jnp.ones((NODE_DIM,), jnp.float32)
        beta = jnp.zeros((NODE_DIM,), jnp.float32)
        return {'node_features': node_features, 'edge_index': edge_index, 'edge_features': edge_features, 'W1': W1, 'b1': b1, 'W2': W2, 'b2': b2, 'U1': U1, 'c1': c1, 'U2': U2, 'c2': c2, 'gamma': gamma, 'beta': beta}
    _L0_gnn_all = _L0_gnn_setup()
    _L0_gnn_in = {k: v for k, v in _L0_gnn_all.items() if k in ('W1', 'b1', 'W2', 'b2', 'U1', 'c1', 'U2', 'c2', 'gamma', 'beta')}
    del _L0_gnn_all

    def _L1_gnn_setup():
        import jax, jax.numpy as jnp
        import numpy as np
        N = 12500
        E = 200000
        D_IN = 128
        D_OUT = 128
        HEADS = 4
        C = D_OUT // HEADS
        NEG_SLOPE = 0.2
        EPS_SOFTMAX = 1e-16
        EPS_LN = 1e-05

        def _gat_edge_conv(x, src, dst, W, att_src, att_dst, gat_bias, skip_W, skip_b, ln_g, ln_b):
            n = x.shape[0]
            h = (x @ W).reshape(n, HEADS, C)
            a_s = jnp.einsum('nhc,hc->nh', h, att_src)
            a_d = jnp.einsum('nhc,hc->nh', h, att_dst)
            e = jax.nn.leaky_relu(a_s[src] + a_d[dst], NEG_SLOPE)
            m = jax.ops.segment_max(e, dst, num_segments=n)
            p = jnp.exp(e - m[dst])
            z = jax.ops.segment_sum(p, dst, num_segments=n)
            alpha = p / (z[dst] + EPS_SOFTMAX)
            msg = h[src] * alpha[:, :, None]
            out = jax.ops.segment_sum(msg, dst, num_segments=n)
            out = out.reshape(n, HEADS * C) + gat_bias
            out = out + x @ skip_W + skip_b
            mu = out.mean(-1, keepdims=True)
            var = ((out - mu) ** 2).mean(-1, keepdims=True)
            return (out - mu) * jax.lax.rsqrt(var + EPS_LN) * ln_g + ln_b
        key = jax.random.key(seed)
        ks = jax.random.split(key, 10)
        x = jax.random.normal(ks[0], (N, D_IN), dtype=jnp.float32)
        edge_index = jax.random.randint(ks[1], (2, E), 0, N, dtype=jnp.int64)
        s = 1.0 / np.sqrt(D_IN)
        W = jax.random.normal(ks[2], (D_IN, HEADS * C), dtype=jnp.float32) * s
        att_src = jax.random.normal(ks[3], (HEADS, C), dtype=jnp.float32) * (1.0 / np.sqrt(C))
        att_dst = jax.random.normal(ks[4], (HEADS, C), dtype=jnp.float32) * (1.0 / np.sqrt(C))
        gat_bias = jax.random.normal(ks[5], (D_OUT,), dtype=jnp.float32) * 0.02
        skip_W = jax.random.normal(ks[6], (D_IN, D_OUT), dtype=jnp.float32) * s
        skip_b = jax.random.normal(ks[7], (D_OUT,), dtype=jnp.float32) * 0.02
        ln_g = jnp.ones((D_OUT,), dtype=jnp.float32)
        ln_b = jnp.zeros((D_OUT,), dtype=jnp.float32)
        return {'x': x, 'edge_index': edge_index, 'W': W, 'att_src': att_src, 'att_dst': att_dst, 'gat_bias': gat_bias, 'skip_W': skip_W, 'skip_b': skip_b, 'ln_g': ln_g, 'ln_b': ln_b}
    _L1_gnn_all = _L1_gnn_setup()
    _L1_gnn_in = {k: v for k, v in _L1_gnn_all.items() if k in ('W', 'att_src', 'att_dst', 'gat_bias', 'skip_W', 'skip_b', 'ln_g', 'ln_b')}
    del _L1_gnn_all

    def _L2_gnn_setup():
        import jax, jax.numpy as jnp
        import numpy as np
        from jax import lax
        N = 6250
        E = 100000
        IN = 128
        H = 4
        D = 32
        SLOPE = 0.2
        key = jax.random.key(seed)
        ks = jax.random.split(key, 12)
        feat = jax.random.normal(ks[0], (N, IN), jnp.float32)
        s_in = 1.0 / np.sqrt(IN)
        W_src = jax.random.normal(ks[1], (IN, H * D), jnp.float32) * s_in
        b_src = jnp.zeros((H * D,), jnp.float32)
        W_dst = jax.random.normal(ks[2], (IN, H * D), jnp.float32) * s_in
        b_dst = jnp.zeros((H * D,), jnp.float32)
        W_val = jax.random.normal(ks[3], (IN, H * D), jnp.float32) * s_in
        b_val = jnp.zeros((H * D,), jnp.float32)
        attn_l = jax.random.normal(ks[4], (H, D), jnp.float32) * (1.0 / np.sqrt(D))
        attn_r = jax.random.normal(ks[5], (H, D), jnp.float32) * (1.0 / np.sqrt(D))
        src = jax.random.randint(ks[6], (E,), 0, N, dtype=jnp.int32)
        dst = jax.random.randint(ks[7], (E,), 0, N, dtype=jnp.int32)
        return {'feat': feat, 'W_src': W_src, 'b_src': b_src, 'W_dst': W_dst, 'b_dst': b_dst, 'W_val': W_val, 'b_val': b_val, 'attn_l': attn_l, 'attn_r': attn_r, 'src': src, 'dst': dst}
    _L2_gnn_all = _L2_gnn_setup()
    _L2_gnn_in = {k: v for k, v in _L2_gnn_all.items() if k in ('W_src', 'b_src', 'W_dst', 'b_dst', 'W_val', 'b_val', 'attn_l', 'attn_r')}
    del _L2_gnn_all

    def _L3_gnn_setup():
        import jax, jax.numpy as jnp
        import numpy as np
        N_NODES = 6250
        N_EDGES = 200000
        IN_DIM = 128
        HEADS = 8
        OUT_C = 16
        NEG_SLOPE = 0.2
        BN_EPS = 1e-05
        key = jax.random.key(seed)
        ks = jax.random.split(key, 8)
        x = jax.random.normal(ks[0], (N_NODES, IN_DIM), dtype=jnp.float32)
        edge_index = jax.random.randint(ks[1], (2, N_EDGES), 0, N_NODES, dtype=jnp.int64)
        W = jax.random.normal(ks[2], (IN_DIM, HEADS * OUT_C), dtype=jnp.float32) / np.sqrt(IN_DIM)
        att_src = jax.random.normal(ks[3], (HEADS, OUT_C), dtype=jnp.float32) / np.sqrt(OUT_C)
        att_dst = jax.random.normal(ks[4], (HEADS, OUT_C), dtype=jnp.float32) / np.sqrt(OUT_C)
        bias = jnp.zeros((HEADS * OUT_C,), dtype=jnp.float32)
        gamma = jnp.ones((HEADS * OUT_C,), dtype=jnp.float32)
        beta = jnp.zeros((HEADS * OUT_C,), dtype=jnp.float32)
        return {'x': x, 'edge_index': edge_index, 'W': W, 'att_src': att_src, 'att_dst': att_dst, 'bias': bias, 'gamma': gamma, 'beta': beta}
    _L3_gnn_all = _L3_gnn_setup()
    _L3_gnn_in = {k: v for k, v in _L3_gnn_all.items() if k in ('W', 'att_src', 'att_dst', 'bias', 'gamma', 'beta')}
    del _L3_gnn_all
    return {'x': x, 'src': src, 'dst': dst, 'edge_attr_64': edge_attr_64, 'L0_gnn_W1': _L0_gnn_in['W1'], 'L0_gnn_b1': _L0_gnn_in['b1'], 'L0_gnn_W2': _L0_gnn_in['W2'], 'L0_gnn_b2': _L0_gnn_in['b2'], 'L0_gnn_U1': _L0_gnn_in['U1'], 'L0_gnn_c1': _L0_gnn_in['c1'], 'L0_gnn_U2': _L0_gnn_in['U2'], 'L0_gnn_c2': _L0_gnn_in['c2'], 'L0_gnn_gamma': _L0_gnn_in['gamma'], 'L0_gnn_beta': _L0_gnn_in['beta'], 'L1_gnn_W': _L1_gnn_in['W'], 'L1_gnn_att_src': _L1_gnn_in['att_src'], 'L1_gnn_att_dst': _L1_gnn_in['att_dst'], 'L1_gnn_gat_bias': _L1_gnn_in['gat_bias'], 'L1_gnn_skip_W': _L1_gnn_in['skip_W'], 'L1_gnn_skip_b': _L1_gnn_in['skip_b'], 'L1_gnn_ln_g': _L1_gnn_in['ln_g'], 'L1_gnn_ln_b': _L1_gnn_in['ln_b'], 'L2_gnn_W_src': _L2_gnn_in['W_src'], 'L2_gnn_b_src': _L2_gnn_in['b_src'], 'L2_gnn_W_dst': _L2_gnn_in['W_dst'], 'L2_gnn_b_dst': _L2_gnn_in['b_dst'], 'L2_gnn_W_val': _L2_gnn_in['W_val'], 'L2_gnn_b_val': _L2_gnn_in['b_val'], 'L2_gnn_attn_l': _L2_gnn_in['attn_l'], 'L2_gnn_attn_r': _L2_gnn_in['attn_r'], 'L3_gnn_W': _L3_gnn_in['W'], 'L3_gnn_att_src': _L3_gnn_in['att_src'], 'L3_gnn_att_dst': _L3_gnn_in['att_dst'], 'L3_gnn_bias': _L3_gnn_in['bias'], 'L3_gnn_gamma': _L3_gnn_in['gamma'], 'L3_gnn_beta': _L3_gnn_in['beta']}

def reference(x, src, dst, edge_attr_64, L0_gnn_W1, L0_gnn_b1, L0_gnn_W2, L0_gnn_b2, L0_gnn_U1, L0_gnn_c1, L0_gnn_U2, L0_gnn_c2, L0_gnn_gamma, L0_gnn_beta, L1_gnn_W, L1_gnn_att_src, L1_gnn_att_dst, L1_gnn_gat_bias, L1_gnn_skip_W, L1_gnn_skip_b, L1_gnn_ln_g, L1_gnn_ln_b, L2_gnn_W_src, L2_gnn_b_src, L2_gnn_W_dst, L2_gnn_b_dst, L2_gnn_W_val, L2_gnn_b_val, L2_gnn_attn_l, L2_gnn_attn_r, L3_gnn_W, L3_gnn_att_src, L3_gnn_att_dst, L3_gnn_bias, L3_gnn_gamma, L3_gnn_beta):
    import jax
    import jax.numpy as jnp

    def _L0_gnn_ref(node_features, edge_index, edge_features, W1, b1, W2, b2, U1, c1, U2, c2, gamma, beta):
        import jax, jax.numpy as jnp
        import numpy as np
        N_NODES = 6250
        N_EDGES = 100000
        NODE_DIM = 128
        EDGE_DIM = 64
        HIDDEN = 128
        EPS = 1e-05

        def _glorot(key, shape):
            fan_in, fan_out = (shape[0], shape[1])
            lim = (6.0 / (fan_in + fan_out)) ** 0.5
            return jax.random.uniform(key, shape, jnp.float32, -lim, lim)
        src, tgt = (edge_index[0], edge_index[1])
        msg_in = jnp.concatenate([node_features[src], node_features[tgt], edge_features], axis=-1)
        messages = jax.nn.relu(msg_in @ W1 + b1) @ W2 + b2
        agg = jax.ops.segment_sum(messages, tgt, num_segments=N_NODES)
        counts = jax.ops.segment_sum(jnp.ones((messages.shape[0],), jnp.float32), tgt, num_segments=N_NODES)
        agg = agg / jnp.clip(counts, 1.0)[:, None]
        upd_in = jnp.concatenate([node_features, agg], axis=-1)
        updated = jax.nn.relu(upd_in @ U1 + c1) @ U2 + c2
        x = node_features + updated
        mu = jnp.mean(x, axis=-1, keepdims=True)
        var = jnp.mean((x - mu) ** 2, axis=-1, keepdims=True)
        return (x - mu) / jnp.sqrt(var + EPS) * gamma + beta

    def _L1_gnn_ref(x, edge_index, W, att_src, att_dst, gat_bias, skip_W, skip_b, ln_g, ln_b):
        import jax, jax.numpy as jnp
        import numpy as np
        N = 12500
        E = 200000
        D_IN = 128
        D_OUT = 128
        HEADS = 4
        C = D_OUT // HEADS
        NEG_SLOPE = 0.2
        EPS_SOFTMAX = 1e-16
        EPS_LN = 1e-05

        def _gat_edge_conv(x, src, dst, W, att_src, att_dst, gat_bias, skip_W, skip_b, ln_g, ln_b):
            n = x.shape[0]
            h = (x @ W).reshape(n, HEADS, C)
            a_s = jnp.einsum('nhc,hc->nh', h, att_src)
            a_d = jnp.einsum('nhc,hc->nh', h, att_dst)
            e = jax.nn.leaky_relu(a_s[src] + a_d[dst], NEG_SLOPE)
            m = jax.ops.segment_max(e, dst, num_segments=n)
            p = jnp.exp(e - m[dst])
            z = jax.ops.segment_sum(p, dst, num_segments=n)
            alpha = p / (z[dst] + EPS_SOFTMAX)
            msg = h[src] * alpha[:, :, None]
            out = jax.ops.segment_sum(msg, dst, num_segments=n)
            out = out.reshape(n, HEADS * C) + gat_bias
            out = out + x @ skip_W + skip_b
            mu = out.mean(-1, keepdims=True)
            var = ((out - mu) ** 2).mean(-1, keepdims=True)
            return (out - mu) * jax.lax.rsqrt(var + EPS_LN) * ln_g + ln_b
        n = x.shape[0]
        loops = jnp.arange(n, dtype=edge_index.dtype)
        src = jnp.concatenate([edge_index[0], loops])
        dst = jnp.concatenate([edge_index[1], loops])
        return _gat_edge_conv(x, src, dst, W, att_src, att_dst, gat_bias, skip_W, skip_b, ln_g, ln_b)

    def _L2_gnn_ref(feat, W_src, b_src, W_dst, b_dst, W_val, b_val, attn_l, attn_r, src, dst):
        import jax, jax.numpy as jnp
        import numpy as np
        from jax import lax
        N = 6250
        E = 100000
        IN = 128
        H = 4
        D = 32
        SLOPE = 0.2
        n = feat.shape[0]
        fs = (feat @ W_src + b_src).reshape(n, H, D)
        fd = (feat @ W_dst + b_dst).reshape(n, H, D)
        fv = (feat @ W_val + b_val).reshape(n, H, D)
        el = jnp.einsum('nhd,hd->nh', fs, attn_l)
        er = jnp.einsum('nhd,hd->nh', fd, attn_r)
        e = el[src] + er[dst]
        e = jnp.where(e >= 0, e, SLOPE * e)
        emax = lax.stop_gradient(jax.ops.segment_max(e, dst, num_segments=n))
        ee = jnp.exp(e - emax[dst])
        denom = jax.ops.segment_sum(ee, dst, num_segments=n)
        a = ee / denom[dst]
        msg = fv[src] * a[:, :, None]
        out = jax.ops.segment_sum(msg, dst, num_segments=n)
        return out.reshape(n, H * D)

    def _L3_gnn_ref(x, edge_index, W, att_src, att_dst, bias, gamma, beta):
        import jax, jax.numpy as jnp
        import numpy as np
        N_NODES = 6250
        N_EDGES = 200000
        IN_DIM = 128
        HEADS = 8
        OUT_C = 16
        NEG_SLOPE = 0.2
        BN_EPS = 1e-05
        N = x.shape[0]
        H, C = att_src.shape
        src, dst = (edge_index[0], edge_index[1])
        xl = (x @ W).reshape(N, H, C)
        a_src = jnp.sum(xl * att_src[None], axis=-1)
        a_dst = jnp.sum(xl * att_dst[None], axis=-1)
        e = jax.nn.leaky_relu(a_src[src] + a_dst[dst], NEG_SLOPE)
        m = jax.ops.segment_max(e, dst, num_segments=N)
        m = jnp.where(jnp.isfinite(m), m, 0.0)
        ex = jnp.exp(e - m[dst])
        denom = jax.ops.segment_sum(ex, dst, num_segments=N)
        alpha = ex / (denom[dst] + 1e-16)
        out = jax.ops.segment_sum(alpha[:, :, None] * xl[src], dst, num_segments=N)
        h = out.reshape(N, H * C) + bias
        mean = jnp.mean(h, axis=0)
        var = jnp.mean((h - mean) ** 2, axis=0)
        h = (h - mean) * jax.lax.rsqrt(var + BN_EPS) * gamma + beta
        h = jax.nn.relu(h)
        return x + h
    edge_index = jnp.stack([src, dst])
    x = _layernorm(x + _L0_gnn_ref(x, edge_index, edge_attr_64, L0_gnn_W1, L0_gnn_b1, L0_gnn_W2, L0_gnn_b2, L0_gnn_U1, L0_gnn_c1, L0_gnn_U2, L0_gnn_c2, L0_gnn_gamma, L0_gnn_beta), axis=-1)
    x = _layernorm(x + _L1_gnn_ref(x, edge_index, L1_gnn_W, L1_gnn_att_src, L1_gnn_att_dst, L1_gnn_gat_bias, L1_gnn_skip_W, L1_gnn_skip_b, L1_gnn_ln_g, L1_gnn_ln_b), axis=-1)
    x = _layernorm(x + _L2_gnn_ref(x, L2_gnn_W_src, L2_gnn_b_src, L2_gnn_W_dst, L2_gnn_b_dst, L2_gnn_W_val, L2_gnn_b_val, L2_gnn_attn_l, L2_gnn_attn_r, src, dst), axis=-1)
    x = _layernorm(x + _L3_gnn_ref(x, edge_index, L3_gnn_W, L3_gnn_att_src, L3_gnn_att_dst, L3_gnn_bias, L3_gnn_gamma, L3_gnn_beta), axis=-1)
    return x

_drawn_inputs = setup_inputs


def setup_inputs(seed=0):
    import zlib

    import numpy as np

    out = dict(_drawn_inputs(seed))
    spreads = {'L0_gnn_b1': (0.0, 0.447),
     'L0_gnn_b2': (0.0, 0.31),
     'L0_gnn_c1': (0.0, 0.1),
     'L0_gnn_c2': (0.0, 0.1),
     'L0_gnn_gamma': (1.0, 0.2),
     'L0_gnn_beta': (0.0, 0.1),
     'L1_gnn_ln_g': (1.0, 0.2),
     'L1_gnn_ln_b': (0.0, 0.1),
     'L2_gnn_b_src': (0.0, 2.0),
     'L2_gnn_b_dst': (0.0, 2.0),
     'L2_gnn_b_val': (0.0, 0.1),
     'L3_gnn_bias': (0.0, 2.0),
     'L3_gnn_gamma': (1.0, 0.2),
     'L3_gnn_beta': (0.0, 0.271)}
    factors = {'edge_attr_64': 3.545, 'L1_gnn_skip_b': 3.284, 'L1_gnn_gat_bias': 2.667}
    for name, (base, spread) in spreads.items():
        noise = np.random.default_rng([zlib.crc32(name.encode()), seed]).standard_normal(out[name].shape)
        drawn = base * np.exp(spread * noise) if base else spread * noise
        out[name] = jnp.asarray(drawn.astype(out[name].dtype))
    for name, factor in factors.items():
        out[name] = (out[name] * factor).astype(out[name].dtype)
    return out
```

```python
import concourse.bass as bass
from concourse import mybir
from contextlib import ExitStack


def gnn_program(nc, A, out):
    fp32 = mybir.dt.float32
    i32 = mybir.dt.int32
    ALU = mybir.AluOpType
    ACT = mybir.ActivationFunctionType
    AX = mybir.AxisListType

    P = 128
    N = out.shape[0]
    E = A["edge_attr_64"].shape[1]
    ED = A["edge_attr_64"].shape[0]
    K = A["src"].shape[2]
    CH = A["src"].shape[0]
    TILES = K * CH
    PAIRS = CH // 2
    PIECES = 4
    PIECE = TILES // PIECES
    WIN = 32
    BLK = 512
    NP = A["x"].shape[0]
    NBLK = NP // BLK
    Q = BLK // P
    GR = -(-K // 4)
    LAYERS = 4
    HEADS = [1, 4, 4, 8]
    HM = max(HEADS)
    BIG = float(2 ** 100)
    SLOPE = 0.2
    EPS_LN = 1e-5
    ROW = P + HM

    def tiles_of(g):
        return min(4, K - 4 * g)

    ctx = ExitStack()
    with ctx:
        def sb(name, shape, dt=fp32):
            return ctx.enter_context(nc.sbuf_tensor(name, shape, dt))

        def sem(name):
            return ctx.enter_context(nc.semaphore(name))

        def pair(name):
            return [sem(f"{name}{b}") for b in range(2)]

        def dram(name, shape, dt=fp32):
            return nc.dram_tensor(name, shape, dt, kind="Internal").ap()

        width = [P] + [P + h for h in HEADS[1:]]
        rows = [dram(f"rows{l}", (NP, width[l])) for l in range(LAYERS)]
        wins = [dram(f"wins{l}", (NP, P if l == 0 else HEADS[l])) for l in range(LAYERS)]
        breaks = dram("breaks", (TILES, P))
        joins = dram("joins", (2, TILES))

        acc = sb("acc", [P, NP])
        hacc = sb("hacc", [WIN + HM, NP])
        xn = sb("xn", [P, NP // P, P])
        base_i = sb("base_i", [P, TILES], i32)
        rel = sb("rel", [P, TILES])
        ident = sb("ident", [P, P])
        spread = sb("spread", [HM, 2, P])
        masks = {4: sb("masks4", [P, 2, 4]), 8: sb("masks8", [P, 2, 8])}
        ones = sb("ones", [P, P])
        win_iota = sb("win_iota", [P, WIN])
        head_of = {4: sb("head4", [P, 4]), 8: sb("head8", [P, 8])}
        row_head = {h: sb(f"row_head{h}", [P, h]) for h in (4, 8)}
        row_tile = {h: sb(f"row_tile{h}", [P, K]) for h in (4, 8)}

        G = sb("G", [P, 2, K, ROW])
        idx = sb("idx", [P, 2, K], i32)
        msg = sb("msg", [P, 2, K, P])
        prob = sb("prob", [P, 2, K * HM])
        memb = sb("memb", [P, 2, K * WIN])
        membT = sb("membT", [P, GR * P])
        brk = sb("brk", [P, 2, P])
        join = sb("join", [HM, 2, 2, K])
        wtab = sb("wtab", [P, 2, K * P])
        sflat = sb("sflat", [P, P])
        segm = sb("segm", [P, P])
        lastm = sb("lastm", [P, HM])
        runmax = sb("runmax", [HM, K + 1])
        carry = sb("carry", [HM, K])
        cdiag = sb("cdiag", [HM, HM * K])
        notfirst = sb("notfirst", [P, K])
        scores = sb("scores", [P, 3, K * HM])
        diff = sb("diff", [P, 2, K * HM])
        prow = sb("prow", [1, K * HM])
        maxf = sb("maxf", [P, 2, K * HM])
        facm = sb("facm", [P, 2, K * HM])
        fac = sb("fac", [P, 2, 2, K])

        share = sb("share", [P, max(12 * BLK, 4 * TILES)])
        lhs = share[0:ED + WIN, 0:2 * K * P].rearrange("p (b n) -> p b n", b=2)
        xt, f1, f2, f3, f4, f5, feat, old, tmp, new = (share[:, k * BLK:(k + 1) * BLK] for k in range(10))
        tab = share[:, 10 * BLK:12 * BLK].rearrange("p (q n) -> p q n", q=Q)

        def rowsof(a):
            return a.rearrange("p (q f) -> p q f", q=Q)

        hst = sb("hst", [HM, 2, BLK])
        minus_half = sb("minus_half", [P, Q])
        paced = sb("paced", [1, 2])
        varn = sb("varn", [P, Q])
        stats = sb("stats", [P, Q, 6])
        mv = sb("mv", [P, Q, 2])
        rstd = sb("rstd", [P, Q])
        bnst = sb("bnst", [P, NBLK, 6])
        bnmv = sb("bnmv", [P, 2])
        bnsc = sb("bnsc", [P, 3])

        w1 = sb("w1", [P, 2 * P])
        w1e = sb("w1e", [ED, P])
        w2 = sb("w2", [P, P])
        u1 = sb("u1", [P, 2, P])
        u2 = sb("u2", [P, P])
        wsk = sb("wsk", [P, P])
        wext = [None] + [sb(f"wext{l}", [P, P + 2 * HEADS[l]]) for l in (1, 2, 3)]
        wside = sb("wside", [P, 2, P])
        wexp = sb("wexp", [P, 2, P])
        wT = sb("wT", [P, 4, P])
        att = sb("att", [P, 6, HM])
        rowv = sb("rowv", [1, 7, P])
        brow = sb("brow", [1, 2, 2 * P])
        bc = sb("bc", [P, 4, P])
        COL = {n: k for k, n in enumerate(
            ["L0_gnn_c1", "L0_gnn_c2", "L1_gnn_gat_bias", "L1_gnn_skip_b", "L3_gnn_bias", "L3_gnn_gamma",
             "L3_gnn_beta", "L1_gnn_att_src", "L1_gnn_att_dst", "L2_gnn_attn_l", "L2_gnn_attn_r",
             "L3_gnn_att_src", "L3_gnn_att_dst", "L2_gnn_b_src", "L2_gnn_b_dst"])}
        RW = {n: k for k, n in enumerate(
            ["L0_gnn_gamma", "L0_gnn_beta", "L1_gnn_ln_g", "L1_gnn_ln_b", "L0_gnn_b1", "L0_gnn_b2", "L2_gnn_b_val"])}
        cols = sb("cols", [P, len(COL)])
        skipb = sb("skipb", [P, 1])

        def col(name):
            return cols[:, COL[name]:COL[name] + 1]

        ps = ctx.enter_context(nc.psum_tensor("ps", [P, 8, BLK], fp32))
        ps_msg, ps_wgt = [ps[:, 0, :], ps[:, 2, :]], [ps[:, 1, :], ps[:, 3, :]]
        ps_mT, ps_e, ps_t, ps_max = (ps[:, k, :] for k in (4, 5, 6, 7))
        ps_pre = [ps[:, 6, :], ps[:, 7, :]]
        O_DST, O_CAR, O_FAC, O_SEG = (k * K * HM for k in range(4))
        ps_last = ps[:, 6, 2 * P:2 * P + K]
        pn_tab = ps[:, 0:2, :].rearrange("p a n -> p (a n)").rearrange("p (q n) -> p q n", q=Q)
        pn_max = ps[:, 0, :]
        pn_a, pn_b, pn_c, pn_d, pn_n, pn_t = (ps[:, k, :] for k in range(2, 8))

        loaded = sem("inputs_loaded")
        built = sem("constants_built")
        norm_paced, gather_paced = sem("norm_paced"), sem("gather_paced")
        step = sem("vector_setup_step")
        setup_pe = sem("setup_products_ready")
        setup_copied = sem("setup_products_copied")
        tables_in = sem("edge_tables_stored")
        gathered = [pair(f"gathered_l{l}_") for l in range(LAYERS)]
        win_loaded = [pair(f"windows_loaded_l{l}_") for l in range(LAYERS)]
        idx_loaded = pair("indices_loaded")
        ef_loaded = pair("edge_features_loaded")
        brk_loaded = pair("breaks_loaded")
        messages = pair("messages_ready")
        memb_ready, memb_turned, memb_copied = (sem(f"membership_{w}") for w in ("ready", "turned", "copied"))
        summed = pair("window_sums_ready")
        added = pair("window_sums_added")
        weighed = pair("window_weights_added")
        wtab_clear = sem("window_blocks_cleared")
        maxed = sem("window_maxima_kept")
        pre_ready = pair("preactivation_ready")
        pre_added = pair("preactivation_added")
        hidden = sem("hidden_ready")
        sc_copied, sc_turned = sem("scores_copied"), sem("scores_turned")
        seg_fwd, seg_all, seg_turned = (sem(f"segment_maxima_{w}") for w in ("scanned_forward", "ready", "turned"))
        last_masked, last_ready = sem("last_maxima_masked"), sem("last_maxima_ready")
        run_ready, carry_ready, run_kept = sem("running_maxima_ready"), sem("carry_ready"), sem("running_maximum_kept")
        cdiag_ready, carry_spread = sem("carry_diagonal_ready"), sem("carry_spread")
        dst_ready = pair("target_scores_ready")
        vec = sem("vector_score_step")
        diff_ready = sem("score_differences_ready")
        factor_ready, prob_ready = sem("carry_factors_ready"), sem("weights_ready")
        fac_spread, fac_masked, fac_ready = (sem(f"carry_factors_{w}") for w in ("spread", "masked", "by_feature"))
        brkT_ready, maxf_ready = sem("first_flags_turned"), sem("first_maxima_ready")
        nvec = sem("node_vector_step")
        x_in = sem("node_rows_copied")
        old_turned, old_copied = sem("old_features_turned"), sem("old_features_copied")
        agg_in, agg_out, agg_copied = (sem(f"aggregate_{w}") for w in ("ready", "multiplied", "copied"))
        hid_out, hid_ready, upd_out = sem("update_hidden_multiplied"), sem("update_hidden_ready"), sem("update_multiplied")
        self_out, self_diff, self_exp = (sem(f"self_loop_{w}") for w in ("products_ready", "differences_ready", "weights_ready"))
        var_ready, rstd_ready = sem("variances_ready"), sem("inverse_deviations_ready")
        wide_out = sem("head_sums_spread")
        bn_in, bn_wide, bn_done = sem("batch_head_sums_copied"), sem("batch_head_sums_spread"), sem("batch_block_ready")
        bn_var, bn_rstd = sem("batch_variance_ready"), sem("batch_inverse_deviation_ready")
        bn_ready = sem("batch_statistics_ready")
        feat_ready, feat_turned = sem("layer_output_ready"), sem("layer_output_turned")
        new_ready, new_kept = sem("new_features_ready"), sem("new_features_kept")
        new_turned, new_copied = sem("new_features_turned"), sem("new_features_copied")
        tab_out, tab_ready, stored = sem("table_rows_multiplied"), sem("table_rows_ready"), sem("table_rows_stored")
        final = sem("output_stored")

        block = ctx.enter_context(nc.Block())

        N_LOADS = 17 + len(COL) + len(RW)
        N_BUILT = 10
        STEP_FIRST, STEP_ATT, STEP_TABLES, STEP_END = 1, 3, 13, 22
        VEC = 6

        def chunks(l, i, b):
            return l * CH + 2 * i + b

        def gchunks(l, i, b):
            return (l - 1) * CH + 2 * i + b

        def is_last(i, b):
            return isinstance(i, int) and i == PAIRS - 1 and b == 1

        def uses(l, i):
            return l * PAIRS + i

        def guses(l, i):
            return (l - 1) * PAIRS + i

        def blocks(layers, l, k):
            return NBLK * sum(m < l for m in layers) + k

        NORMS = {0: 2, 1: 2, 2: 1, 3: 1}

        def norms_before(l, k):
            return NBLK * sum(NORMS[m] for m in range(l)) + NORMS[l] * k

        ALL, SOME, MID, MORE = (-1, 0, 1, 2, 3), (0, 1), (0, 1, 2, 3), (-1, 0, 1, 2)

        @block.sync
        def _(sp):
            n_in = [0]

            def load(dst, src):
                sp.dma_start(dst, src).then_inc(loaded, 16)
                n_in[0] += 1

            load(base_i[:, :], A["dst_cols"])
            load(share[0:1, 0:TILES].bitcast(i32), A["dst_cols"][P - 1:P, :])
            load(msg[0:CH, 0, :, :].rearrange("p k n -> p (k n)").bitcast(i32), A["dst_rows"])
            load(w1[:, 0:P], A["L0_gnn_W1"][0:P, :])
            load(w1[:, P:2 * P], A["L0_gnn_W1"][P:2 * P, :])
            load(w1e[:, :], A["L0_gnn_W1"][2 * P:2 * P + ED, :])
            load(w2[:, :], A["L0_gnn_W2"])
            load(u1[:, 0, :], A["L0_gnn_U1"][0:P, :])
            load(u1[:, 1, :], A["L0_gnn_U1"][P:2 * P, :])
            load(u2[:, :], A["L0_gnn_U2"])
            load(wsk[:, :], A["L1_gnn_skip_W"])
            load(wext[1][:, 0:P], A["L1_gnn_W"])
            load(wext[2][:, 0:P], A["L2_gnn_W_val"])
            load(wside[:, 0, :], A["L2_gnn_W_src"])
            load(wside[:, 1, :], A["L2_gnn_W_dst"])
            load(wext[3][:, 0:P], A["L3_gnn_W"])
            for name, k in COL.items():
                load(cols[:, k:k + 1], A[name].rearrange("(p o) -> p o", o=1))
            for name, k in RW.items():
                load(rowv[0:1, k, :], A[name].rearrange("(o n) -> o n", o=1))
            load(xn[:, :, :], A["x"].rearrange("(t p) f -> p t f", p=P))
            assert n_in[0] == N_LOADS, n_in

            sp.wait_ge(step, STEP_TABLES)
            sp.dma_start(breaks.rearrange("(c k) n -> c (k n)", k=K),
                         msg[0:CH, 1, :, :].rearrange("p k n -> p (k n)")).then_inc(tables_in, 16)
            sp.dma_start(joins[0:1, :], share[0:1, 2 * TILES:3 * TILES]).then_inc(tables_in, 16)
            sp.dma_start(joins[1:2, :], share[0:1, 3 * TILES:4 * TILES]).then_inc(tables_in, 16)
            sp.wait_ge(tables_in, 48)

            def store_tables(l, k):
                sp.wait_ge(tab_ready, blocks(MORE, l, k) + 1)
                d = bass.ds(k * BLK, BLK)
                wr = width[l + 1]
                wt = wins[l + 1].shape[1]
                sp.dma_start(rows[l + 1][d, :].rearrange("(q p) c -> p q c", p=P),
                             tab[:, :, 0:wr]).then_inc(stored, 16)
                sp.dma_start(wins[l + 1][d, :].rearrange("(q p) c -> p q c", p=P),
                             tab[:, :, wr:wr + wt]).then_inc(stored, 16)

            for l in range(LAYERS):
                with sp.Fori(0, NBLK) as k:
                    store_tables(l - 1, k)
                sp.wait_ge(stored, 32 * NBLK * (l + 1))
                if l in (1, 3):
                    sp.wait_ge(wtab_clear, 1 if l == 1 else 2)
                H = HEADS[l]
                with sp.Fori(0, PAIRS) as i:
                    for b in range(2):
                        t0 = (2 * i + b) * K
                        sp.wait_ge(gathered[l][b], 16 * K * i)
                        sp.dma_start(idx[:, b, :], A["src"][bass.ds(2 * i + b, 1), :, :]
                                     .rearrange("o p k -> p (o k)")).then_inc(idx_loaded[b], 16)
                        if l == 0:
                            sp.wait_ge(summed[b], uses(l, i))
                            sp.dma_start(lhs[0:ED, b, :], A["edge_attr_64"][:, bass.ds(t0 * P, K * P)]).then_inc(
                                ef_loaded[b], 16)
                        else:
                            sp.wait_ge(dst_ready[b], guses(l, i))
                            sp.wait_ge(messages[b], guses(l, i))
                            for h in range(H):
                                sp.dma_start(brk[h * K:(h + 1) * K, b, :],
                                             breaks[bass.ds(t0, K), :]).then_inc(brk_loaded[b], 16)
                            sp.dma_start(join[0:H, b, :, :], joins[:, bass.ds(t0, K)].unsqueeze(0)
                                         .to_broadcast([H, 2, K])).then_inc(brk_loaded[b], 16)
                        _, first = nc.values_load_multi_w_load_instructions(
                            base_i[0:1, bass.ds(t0, K)], engines=(sp.engine,), min_val=0, max_val=N,
                            skip_runtime_bounds_check_because="targets are node numbers")
                        for t in range(K):
                            g, q = t // 4, t % 4
                            if l == 0:
                                dst = wtab[ED:ED + WIN, b, t * P:(t + 1) * P]
                            else:
                                dst = wtab[WIN * q:WIN * (q + 1), b, g * BLK + q * H:g * BLK + (q + 1) * H]
                            sp.dma_start(dst, wins[l][bass.ds(first[t], WIN), :]).then_inc(win_loaded[l][b], 16)

            with sp.Fori(0, NBLK - 1) as k:
                sp.wait_ge(new_ready, blocks(MID, 3, k) + 1)
                sp.dma_start(out[bass.ds(k * BLK, BLK), :].rearrange("(q p) c -> p q c", p=P),
                             rowsof(new)).then_inc(final, 16)
            sp.wait_ge(new_ready, blocks(MID, 3, NBLK))
            left = N - (NBLK - 1) * BLK
            assert left <= P
            sp.dma_start(out[(NBLK - 1) * BLK:N, :], new[0:left, 0:P]).then_inc(final, 16)
            sp.wait_ge(final, 16 * NBLK)

        @block.gpsimd
        def _(pool):
            nc.gpsimd.memset(ones[:, :], 1.0).then_inc(built, 1)
            nc.gpsimd.iota(win_iota[:, :], [[1, WIN]], base=0, channel_multiplier=0,
                           allow_small_or_imprecise_dtypes=True).then_inc(built, 1)
            pool.wait_ge(built, 2)
            nc.gpsimd.affine_select(out=ident[:, :], in_=ones[:, :], compare_op=ALU.is_equal, fill=0.0, base=0,
                                    pattern=[[-1, P]], channel_multiplier=1).then_inc(built, 1)
            n = 3
            for size, tens, count in ((P // 4, head_of[4], 4), (P // 8, head_of[8], 8),
                                      (K, row_head[8], 8)):
                nc.gpsimd.affine_select(out=tens[:, :], in_=ones[:, 0:count], compare_op=ALU.is_ge, fill=0.0,
                                        base=0, pattern=[[-size, count]], channel_multiplier=1).then_inc(built, 1)
                n += 1
                pool.wait_ge(built, n)
                nc.gpsimd.affine_select(out=tens[:, :], in_=tens[:, :], compare_op=ALU.is_ge, fill=0.0,
                                        base=size - 1, pattern=[[size, count]],
                                        channel_multiplier=-1).then_inc(built, 1)
                n += 1
            nc.gpsimd.memset(minus_half[:, :], -0.5)
            for unused in (sflat, segm, lastm, brk):
                nc.gpsimd.memset(unused[:], 0.0)
            nc.gpsimd.memset(runmax[:, :], -BIG).then_inc(built, 1)
            assert n + 1 == N_BUILT, n

            def node_norms(l, k):
                for j in range(NORMS[l]):
                    pool.wait_ge(var_ready, norms_before(l, k) + j + 1)
                    nc.gpsimd.tensor_tensor(rstd[:, :], varn[:, :], minus_half[:, :], ALU.pow).then_inc(rstd_ready, 1)

            for l in range(LAYERS):
                if l:
                    with pool.Fori(0, NBLK) as k:
                        node_norms(l - 1, k)
                pool.wait_ge(stored, 32 * NBLK * (l + 1))
                with pool.Fori(0, PAIRS) as i:
                    for b in range(2):
                        pool.wait_ge(idx_loaded[b], 16 * (uses(l, i) + 1))
                        if l == 0:
                            pool.wait_ge(summed[b], uses(l, i))
                        else:
                            pool.wait_ge(messages[b], guses(l, i))
                            if l == 1:
                                pool.wait_ge(summed[b], PAIRS)
                        pool.wait_ge(gather_paced, chunks(l, i, b))
                        nc.gpsimd.tensor_tensor(paced[0:1, 1:2], minus_half[0:1, 0:1], minus_half[0:1, 0:1],
                                                ALU.add).then_inc(gather_paced, 1)
                        for t in range(K):
                            nc.gpsimd.indirect_dma_start(
                                G[:, b, t, 0:width[l]], None, rows[l],
                                bass.IndirectOffsetOnAxis(idx[:, b, t:t + 1], 0)).then_inc(gathered[l][b], 16)
            pool.wait_ge(bn_var, 1)
            nc.gpsimd.tensor_tensor(bnsc[:, 0:1], bnsc[:, 0:1], minus_half[:, 0:1], ALU.pow).then_inc(bn_rstd, 1)
            with pool.Fori(0, NBLK) as k:
                node_norms(3, k)

        @block.tensor
        def _(pe):
            pe.wait_ge(loaded, 16 * N_LOADS)
            pe.wait_ge(built, N_BUILT)
            for k, w in enumerate((wext[1][:, 0:P], wside[:, 0, :], wside[:, 1, :], wext[3][:, 0:P])):
                nc.tensor.transpose(ps_t[:, k * P:(k + 1) * P], w, ident[:, :])
            for k in range(4):
                nc.tensor.matmul(ps_mT[:, k * P:(k + 1) * P], ones[0:1, :], rowv[0:1, k, :], start=True, stop=True)
            pe.wait_ge(step, STEP_FIRST)
            for k in range(PIECES):
                last = nc.tensor.matmul(ps[:, k, 0:PIECE], ones[0:1, :],
                                        acc[0:1, k * PIECE:(k + 1) * PIECE], start=True, stop=True)
            last.then_inc(setup_pe, 1)
            pe.wait_ge(step, STEP_ATT)
            for k, (w, h) in enumerate(((0, 4), (0, 4), (1, 4), (2, 4), (3, 8), (3, 8))):
                nc.tensor.matmul(ps_e[:, k * HM:k * HM + h], wT[:, w, :], att[:, k, 0:h], start=True, stop=True)
            nc.tensor.matmul(ps_e[0:1, 64:68], col("L2_gnn_b_src"), att[:, 2, 0:4], start=True, stop=True)
            nc.tensor.matmul(ps_e[0:1, 68:72], col("L2_gnn_b_dst"), att[:, 3, 0:4],
                             start=True, stop=True)
            for k, h in enumerate((4, 8)):
                last = nc.tensor.transpose(ps[0:h, 6 + k, 0:P], head_of[h][:, :], ident[:, :])
            last.then_inc(setup_pe, 1)
            pe.wait_ge(setup_copied, 1)

            def turn(dst, src, signal):
                for q in range(Q):
                    last = nc.tensor.transpose(dst[:, q * P:(q + 1) * P], src[:, q * P:(q + 1) * P], ident[:, :])
                last.then_inc(signal, 1)

            def node_block(l, k):
                pe.wait_ge(x_in, blocks(ALL, l, k) + 1)
                if l in SOME:
                    turn(pn_t, old, old_turned)
                n = blocks((l,), l, k)
                if l in (0, 1, 2):
                    H = HEADS[l]
                    sp_ = ones[0:1, :] if l == 0 else spread[0:H, 0, :]
                    last = nc.tensor.matmul(pn_n, sp_, hst[0:H, 0, :], start=True, stop=True)
                    if l == 1:
                        last = nc.tensor.matmul(pn_max, sp_, hst[0:H, 1, :], start=True, stop=True)
                    last.then_inc(wide_out, 1)
                if l == 0:
                    pe.wait_ge(agg_in, n + 1)
                    nc.tensor.matmul(pn_a, w2[:, :], f1, start=True, stop=False)
                    nc.tensor.matmul(pn_a, rowv[0:1, RW["L0_gnn_b2"], :], f2[0:1, :], start=False,
                                     stop=True).then_inc(agg_out, 1)
                    pe.wait_ge(old_copied, blocks(SOME, l, k) + 1)
                    pe.wait_ge(agg_copied, n + 1)
                    nc.tensor.matmul(pn_b, u1[:, 0, :], xt, start=True, stop=False)
                    nc.tensor.matmul(pn_b, u1[:, 1, :], f3, start=False, stop=True).then_inc(hid_out, 1)
                    pe.wait_ge(hid_ready, n + 1)
                    nc.tensor.matmul(pn_c, u2[:, :], f4, start=True, stop=True).then_inc(upd_out, 1)
                if l == 1:
                    pe.wait_ge(old_copied, blocks(SOME, l, k) + 1)
                    nc.tensor.matmul(pn_a, wsk[:, :], xt, start=True, stop=True)
                    nc.tensor.matmul(pn_b, wext[1][:, 0:P], xt, start=True, stop=True)
                    nc.tensor.matmul(pn_c, wexp[:, 0, :], xt, start=True, stop=True)
                    nc.tensor.matmul(pn_d, wexp[:, 1, :], xt, start=True, stop=True).then_inc(self_out, 1)
                if l >= 0:
                    pe.wait_ge(feat_ready, blocks(MID, l, k) + 1)
                    turn(pn_n, feat, feat_turned)
                if l < 3:
                    if l >= 0:
                        pe.wait_ge(new_ready, blocks(MID, l, k) + 1)
                    turn(pn_t, new, new_turned)
                    pe.wait_ge(new_copied, blocks(MORE, l, k) + 1)
                    w = w1 if l == -1 else wext[l + 1]
                    cw = w.shape[1]
                    bias = {-1: 0, 1: 1}.get(l)
                    for q in range(Q):
                        last = nc.tensor.matmul(pn_tab[:, q, 0:cw], xt[:, q * P:(q + 1) * P], w[:, :],
                                                start=True, stop=bias is None)
                        if bias is not None:
                            last = nc.tensor.matmul(pn_tab[:, q, 0:cw], ones[0:1, :], brow[0:1, bias, 0:cw],
                                                    start=False, stop=True)
                    last.then_inc(tab_out, 1)
                    pe.wait_ge(tab_ready, blocks(MORE, l, k) + 1)

            def turn_membership(l, i, b):
                pe.wait_ge(memb_ready, chunks(l, i, b) + 1)
                pe.wait_ge(memb_copied, chunks(l, i, b))
                for g in range(GR):
                    n = tiles_of(g) * WIN
                    last = nc.tensor.transpose(ps_mT[0:n, g * P:(g + 1) * P],
                                               memb[:, b, g * P:g * P + n], ident[:, :])
                last.then_inc(memb_turned, 1)

            def front_mlp(l, i, b):
                c = chunks(l, i, b)
                turn_membership(l, i, b)
                pe.wait_ge(ef_loaded[b], 16 * (i + 1))
                pe.wait_ge(win_loaded[l][b], 16 * K * (i + 1))
                pe.wait_ge(memb_copied, c + 1)
                for g in range(GR):
                    pe.wait_ge(pre_added[g % 2], (GR // 2) * c + g // 2)
                    for q in range(tiles_of(g)):
                        t = slice((4 * g + q) * P, (4 * g + q + 1) * P)
                        last = nc.tensor.matmul(ps_pre[g % 2][:, q * P:(q + 1) * P], lhs[:, b, t],
                                                wtab[0:ED + WIN, b, t], start=True, stop=True)
                    last.then_inc(pre_ready[g % 2], 1)

            def sums_mlp(l, i, b):
                c = chunks(l, i, b)
                pe.wait_ge(added[b], K * uses(l, i))
                pe.wait_ge(weighed[b], K * uses(l, i))
                for t in range(K):
                    if t % 4 == 0:
                        pe.wait_ge(hidden, GR * c + t // 4 + 1)
                    m = memb[:, b, t * WIN:(t + 1) * WIN]
                    o = slice(t * WIN, (t + 1) * WIN)
                    nc.tensor.matmul(ps_msg[b][:, o], msg[:, b, t, :], m, start=True, stop=True)
                    last = nc.tensor.matmul(ps_wgt[b][0:1, o], ones[:, 0:1], m, start=True, stop=True)
                last.then_inc(summed[b], 1)

            def front_attention(l, i, b):
                g_ = gchunks(l, i, b)
                H = HEADS[l]
                JH = K * H
                pe.wait_ge(sc_copied, g_ + 1)
                pe.wait_ge(run_ready, g_)
                nc.tensor.transpose(ps_t[:, 0:P], sflat[:, :], ident[:, :]).then_inc(sc_turned, 1)
                turn_membership(l, i, b)
                pe.wait_ge(last_masked, g_ + 1)
                nc.tensor.matmul(ps_last[0:H, :], lastm[:, 0:H], row_tile[H][:, :],
                                 start=True, stop=True).then_inc(last_ready, 1)
                pe.wait_ge(seg_all, g_ + 1)
                pe.wait_ge(fac_masked, g_)
                nc.tensor.transpose(ps_e[:, O_SEG:O_SEG + P], segm[:, :], ident[:, :]).then_inc(seg_turned, 1)
                if l == 1:
                    nc.tensor.transpose(ps_max[:, 0:P], brk[:, b, :], ident[:, :]).then_inc(brkT_ready, 1)
                pe.wait_ge(memb_copied, chunks(l, i, b) + 1)
                pe.wait_ge(win_loaded[l][b], 16 * K * (i + 1))
                for g in range(GR):
                    n = tiles_of(g)
                    last = nc.tensor.matmul(ps_e[:, O_DST + 4 * g * H:O_DST + (4 * g + n) * H],
                                            membT[0:n * WIN, g * P:(g + 1) * P],
                                            wtab[0:n * WIN, b, g * BLK:g * BLK + n * H], start=True, stop=True)
                last.then_inc(dst_ready[b], 1)
                pe.wait_ge(cdiag_ready, g_ + 1)
                nc.tensor.matmul(ps_e[:, O_CAR:O_CAR + JH], ones[0:H, :], cdiag[0:H, 0:JH],
                                 start=True, stop=True).then_inc(carry_spread, 1)

            def spread_factors(l, i, b):
                g_ = gchunks(l, i, b)
                JH = K * HEADS[l]
                pe.wait_ge(factor_ready, g_ + 1)
                nc.tensor.matmul(ps_e[:, O_FAC:O_FAC + JH], ones[0:1, :], prow[0:1, 0:JH],
                                 start=True, stop=True).then_inc(fac_spread, 1)

            def sums_attention(l, i, b):
                H = HEADS[l]
                pe.wait_ge(added[b], K * uses(l, i))
                pe.wait_ge(weighed[b], K * uses(l, i))
                pe.wait_ge(messages[b], guses(l, i) + 1)
                if l == 1:
                    pe.wait_ge(maxf_ready, 2 * i + b + (1 if is_last(i, b) else 2))
                    if is_last(i, b):
                        pe.wait_ge(maxed, K * (CH - 1))
                for t in range(K):
                    m = memb[:, b, t * WIN:(t + 1) * WIN]
                    o = slice(t * WIN, (t + 1) * WIN)
                    heads = slice(t, t + (H - 1) * K + 1, K)
                    nc.tensor.matmul(ps_msg[b][:, o], msg[:, b, t, :], m, start=True, stop=True)
                    last = nc.tensor.matmul(ps_wgt[b][0:H, o], prob[:, b, heads], m, start=True, stop=True)
                    if l == 1:
                        last = nc.tensor.matmul(ps_max[0:H, o], maxf[:, b, heads], m, start=True, stop=True)
                last.then_inc(summed[b], 1)

            def front(l, i, b):
                (front_attention if l else front_mlp)(l, i, b)

            def sums(l, i, b):
                (sums_attention if l else sums_mlp)(l, i, b)

            def factors(l, i, b):
                if l:
                    spread_factors(l, i, b)

            for l in range(LAYERS):
                with pe.Fori(0, NBLK) as k:
                    node_block(l - 1, k)
                front(l, 0, 0)
                with pe.Fori(0, PAIRS - 1) as i:
                    factors(l, i, 0)
                    front(l, i, 1)
                    sums(l, i, 0)
                    factors(l, i, 1)
                    front(l, i + 1, 0)
                    sums(l, i, 1)
                factors(l, PAIRS - 1, 0)
                front(l, PAIRS - 1, 1)
                sums(l, PAIRS - 1, 0)
                factors(l, PAIRS - 1, 1)
                sums(l, PAIRS - 1, 1)
                pe.wait_ge(added[1], K * uses(l + 1, 0))
                pe.wait_ge(weighed[1], K * uses(l + 1, 0))
                if l == 1:
                    pe.wait_ge(maxed, K * CH)
            with pe.Fori(0, NBLK) as k:
                pe.wait_ge(bn_in, k + 1)
                pe.wait_ge(bn_done, k)
                nc.tensor.matmul(pn_n, spread[0:HM, 1, :], hst[:, 0, :], start=True, stop=True).then_inc(bn_wide, 1)
            pe.wait_ge(bn_ready, 1)
            with pe.Fori(0, NBLK) as k:
                node_block(3, k)

        @block.scalar
        def _(act):
            act.wait_ge(loaded, 16 * N_LOADS)
            act.wait_ge(setup_copied, 1)

            def copy(dst, src):
                return nc.scalar.activation(dst, src, ACT.Copy)

            def node_block(l, k):
                n = blocks((l,), l, k)
                xk = xn[:, bass.ds(k * Q, Q), :]
                if l == -1:
                    act.wait_ge(new_turned, k)
                    copy(rowsof(new), xk).then_inc(x_in, 1)
                else:
                    act.wait_ge(new_ready, blocks(MID, l, k))
                    if l < 3:
                        for c in range(2 if l == 1 else 1):
                            copy(hst[0:HEADS[l], c, :],
                                 hacc[c * WIN:c * WIN + HEADS[l], bass.ds(k * BLK, BLK)])
                    copy(rowsof(old), xk).then_inc(x_in, 1)
                if l in SOME:
                    act.wait_ge(old_turned, blocks(SOME, l, k) + 1)
                    copy(xt, pn_t).then_inc(old_copied, 1)
                if l == 0:
                    act.wait_ge(agg_out, n + 1)
                    copy(f3, pn_a).then_inc(agg_copied, 1)
                    act.wait_ge(hid_out, n + 1)
                    nc.scalar.activation(f4, pn_b, ACT.Relu, bias=col("L0_gnn_c1")).then_inc(hid_ready, 1)
                if l == 1:
                    act.wait_ge(self_diff, n + 1)
                    nc.scalar.activation(share[:, 4 * BLK:6 * BLK], share[:, 4 * BLK:6 * BLK],
                                         ACT.Exp).then_inc(self_exp, 1)
                if l == 3:
                    act.wait_ge(bn_ready, 1)
                    act.wait_ge(feat_turned, blocks(MID, l, k))
                    nc.scalar.activation(feat, acc[:, bass.ds(k * BLK, BLK)], ACT.Relu,
                                         bias=bnsc[:, 1:2], scale=bnsc[:, 0:1]).then_inc(feat_ready, 1)
                if l < 3:
                    act.wait_ge(new_turned, blocks(MORE, l, k) + 1)
                    copy(xt, pn_t).then_inc(new_copied, 1)
                    if l >= 0:
                        copy(xk, rowsof(new)).then_inc(new_kept, 1)
                    act.wait_ge(tab_out, blocks(MORE, l, k) + 1)
                    act.wait_ge(stored, 32 * blocks(MORE, l, k))
                    cw = (w1 if l == -1 else wext[l + 1]).shape[1]
                    copy(tab[:, :, 0:cw], pn_tab[:, :, 0:cw]).then_inc(tab_ready, 1)

            def copy_membership(l, i, b):
                act.wait_ge(memb_turned, chunks(l, i, b) + 1)
                if l == 0:
                    act.wait_ge(pre_ready[1], (GR // 2) * chunks(l, i, b))
                    for t in range(K):
                        q = t % 4
                        last = copy(lhs[ED:ED + WIN, b, t * P:(t + 1) * P],
                                    ps_mT[q * WIN:(q + 1) * WIN, (t // 4) * P:(t // 4 + 1) * P])
                    last.then_inc(memb_copied, 1)
                    return
                act.wait_ge(dst_ready[1 - b], guses(l, i) + b)
                full = (K // 4) * P
                copy(membT[:, 0:full], ps_mT[:, 0:full])
                n = tiles_of(GR - 1) * WIN
                copy(membT[0:n, full:full + P], ps_mT[0:n, full:full + P]).then_inc(memb_copied, 1)

            def edge_mlp(l, i, b):
                c = chunks(l, i, b)
                copy_membership(l, i, b)
                for g in range(GR):
                    act.wait_ge(pre_added[g % 2], (GR // 2) * c + g // 2 + 1)
                    m = msg[:, b, 4 * g:4 * g + tiles_of(g), :]
                    nc.scalar.activation(m, m, ACT.Relu).then_inc(hidden, 1)

            def edge_attention(l, i, b):
                g_ = gchunks(l, i, b)
                H = HEADS[l]
                JH = K * H
                act.wait_ge(gathered[l][b], 16 * K * (i + 1))
                act.wait_ge(diff_ready, g_)
                copy(sflat[:, 0:JH].rearrange("p (h k) -> p h k", h=H),
                     G[:, b, :, P:P + H].rearrange("p k h -> p h k")).then_inc(sc_copied, 1)
                copy_membership(l, i, b)
                act.wait_ge(diff_ready, g_ + 1)
                act.wait_ge(fac_spread, g_)
                nc.scalar.activation(prow[0:1, 0:JH], diff[0:1, 1, 0:JH], ACT.Exp).then_inc(factor_ready, 1)
                act.wait_ge(summed[b], uses(l, i))
                nc.scalar.activation(prob[:, b, 0:JH], diff[:, 0, 0:JH], ACT.Exp).then_inc(prob_ready, 1)

            for l in range(LAYERS):
                act.wait_ge(added[1], K * uses(l, 0))
                act.wait_ge(weighed[1], K * uses(l, 0))
                if l == 2:
                    act.wait_ge(maxed, K * CH)
                with act.Fori(0, NBLK) as k:
                    node_block(l - 1, k)
                with act.Fori(0, PAIRS) as i:
                    for b in range(2):
                        (edge_mlp if l == 0 else edge_attention)(l, i, b)
            act.wait_ge(added[1], K * uses(LAYERS, 0))
            act.wait_ge(weighed[1], K * uses(LAYERS, 0))
            with act.Fori(0, NBLK) as k:
                act.wait_ge(bn_wide, k)
                copy(hst[:, 0, :], hacc[0:HM, bass.ds(k * BLK, BLK)]).then_inc(bn_in, 1)
            with act.Fori(0, NBLK) as k:
                node_block(3, k)

        @block.vector
        def _(dve):
            done = [0]

            def link(ins):
                done[0] += 1
                ins.then_inc(step, 1)
                dve.wait_ge(step, done[0])

            dve.wait_ge(loaded, 16 * N_LOADS)
            dve.wait_ge(built, N_BUILT)
            first = acc[0:1, 0:TILES]
            link(nc.vector.tensor_copy(first, base_i[0:1, :]))
            assert done[0] == STEP_FIRST
            nc.vector.tensor_copy(rel[:, :], base_i[:, :])
            for k, (h, name) in enumerate(((4, "L1_gnn_att_src"), (4, "L1_gnn_att_dst"), (4, "L2_gnn_attn_l"),
                                           (4, "L2_gnn_attn_r"), (8, "L3_gnn_att_src"), (8, "L3_gnn_att_dst"))):
                nc.vector.tensor_scalar(att[:, k, 0:h], head_of[h][:, :], col(name), None, ALU.mult)
            nc.vector.tensor_copy(row_head[4][:, :], row_head[8][:, 0:4])
            for h in (4, 8):
                nc.vector.tensor_reduce(row_tile[h][:, :],
                                        ident[:, 0:K * h].rearrange("p (h k) -> p k h", h=h), AX.X, ALU.add)
            nc.vector.tensor_tensor(skipb[:, :], col("L1_gnn_gat_bias"), col("L1_gnn_skip_b"), ALU.add)
            nc.vector.memset(brow[:, :, :], 0.0)
            nc.vector.tensor_copy(wtab[0:ED, :, :].rearrange("p b (k n) -> p (b k) n", k=K),
                                  w1e[:, :].unsqueeze(1).to_broadcast([ED, 2 * K, P]))
            for h in (4, 8):
                nc.vector.tensor_copy(masks[h][:, 0, :], head_of[h][:, :])
                nc.vector.tensor_copy(masks[h][:, 1, :], ident[:, 0:h])
            link(nc.vector.memset(hacc[:, :], 0.0))
            dve.wait_ge(setup_pe, 1)
            nc.vector.tensor_copy(wT[:, :, :].rearrange("p a n -> p (a n)"), ps_t)
            nc.vector.tensor_copy(bc[:, :, :].rearrange("p a n -> p (a n)"), ps_mT)
            link(nc.vector.tensor_tensor(rel[:, :].rearrange("p (a n) -> p a n", a=PIECES),
                                         rel[:, :].rearrange("p (a n) -> p a n", a=PIECES),
                                         ps[:, 0:PIECES, 0:PIECE], ALU.subtract))
            assert done[0] == STEP_ATT
            t_int = msg[0:CH, 0, :, :].rearrange("p k n -> p (k n)").bitcast(i32)
            t_flt = G[0:CH, :, :, :].rearrange("p b k n -> p (b k n)")[:, 0:K * P]
            brk_all = msg[0:CH, 1, :, :].rearrange("p k n -> p (k n)")
            link(nc.vector.tensor_copy(t_flt, t_int))
            link(nc.vector.tensor_tensor(brk_all[:, 1:K * P], t_flt[:, 1:K * P], t_flt[:, 0:K * P - 1], ALU.not_equal))
            link(nc.vector.tensor_scalar(brk_all[:, 1:K * P], brk_all[:, 1:K * P], -BIG, None, ALU.mult))
            link(nc.vector.memset(msg[0:CH, 1, :, 0:1], -BIG))
            last_i = share[0:1, 0:TILES].bitcast(i32)
            last = share[0:1, TILES:2 * TILES]
            single = share[0:1, 2 * TILES:3 * TILES]
            cont = share[0:1, 3 * TILES:4 * TILES]
            link(nc.vector.tensor_copy(last, last_i))
            nc.vector.memset(cont[:, 0:1], 0.0)
            nc.vector.tensor_tensor(single, first, last, ALU.is_equal)
            link(nc.vector.tensor_tensor(cont[:, 1:TILES], first[:, 1:TILES], last[:, 0:TILES - 1], ALU.is_equal))
            link(nc.vector.tensor_tensor(single, single, cont, ALU.mult))
            link(nc.vector.tensor_scalar(single, single, 1.0, BIG, ALU.subtract, ALU.mult))
            link(nc.vector.tensor_scalar(cont, cont, 1.0, BIG, ALU.subtract, ALU.mult))
            link(nc.vector.memset(notfirst[:, :], 0.0))
            assert done[0] == STEP_TABLES, done
            link(nc.vector.memset(acc[:, :], 0.0))
            dve.wait_ge(setup_pe, 2)
            for l, k in ((1, 0), (2, 2), (3, 4)):
                H = HEADS[l]
                nc.vector.tensor_copy(wext[l][:, P:P + 2 * H].rearrange("p (a h) -> p a h", a=2),
                                      ps_e[:, k * HM:(k + 2) * HM].rearrange("p (a h) -> p a h", a=2)[:, :, 0:H])
            nc.vector.tensor_copy(wexp[:, :, :].rearrange("p a (h c) -> p a h c", h=4),
                                  ps_e[:, 0:2 * HM].rearrange("p (a h) -> p a h", a=2)[:, :, 0:4]
                                  .unsqueeze(3).to_broadcast([P, 2, 4, P // 4]))
            for k, h in enumerate((4, 8)):
                nc.vector.tensor_copy(spread[0:h, k, :], ps[0:h, 6 + k, 0:P])
            nc.vector.tensor_copy(brow[0:1, 0, P:2 * P], rowv[0:1, RW["L0_gnn_b1"], :])
            nc.vector.tensor_copy(brow[0:1, 1, 0:P], rowv[0:1, RW["L2_gnn_b_val"], :])
            dve.wait_ge(tables_in, 48)
            nc.vector.tensor_copy(brow[0:1, 1, P:P + 8], ps_e[0:1, 64:72]).then_inc(setup_copied, 1)

            count = [0]

            def node_loop(l, steps, body):
                start = count[0]
                with dve.Fori(0, NBLK) as k:
                    count[0] = start + steps * k
                    made = [0]

                    def then(ins):
                        made[0] += 1
                        ins.then_inc(nvec, 1)
                        dve.wait_ge(nvec, start + steps * k + made[0])

                    body(l, k, then)
                    assert made[0] == steps, (l, made)
                count[0] = start + steps * NBLK

            norms = [0]

            def stretch(a):
                return a.unsqueeze(2).to_broadcast([P, Q, P])

            def layer_norm(then, src, dst):
                for q in range(Q):
                    o = nc.vector.bn_stats(stats[:, q, :], src[:, q, :])
                then(o)
                dve.wait_ge(norm_paced, norms[0])
                nc.vector.tensor_copy(paced[0:1, 0:1], minus_half[0:1, 0:1]).then_inc(norm_paced, 1)
                for q in range(Q):
                    o = nc.vector.bn_aggr(mv[:, q, :], stats[:, q, :])
                then(o)
                nc.vector.tensor_scalar(varn[:, :], mv[:, :, 1], EPS_LN, None, ALU.add).then_inc(var_ready, 1)
                norms[0] = norms[0] + 1
                then(nc.vector.tensor_tensor(dst, src, stretch(mv[:, :, 0]), ALU.subtract))
                dve.wait_ge(rstd_ready, norms[0])
                return nc.vector.tensor_tensor(dst, dst, stretch(rstd[:, :]), ALU.mult)

            def node_block(l, k, then):
                tt, ts, stt = nc.vector.tensor_tensor, nc.vector.tensor_scalar, nc.vector.scalar_tensor_tensor
                norms[0] = norms_before(l, k)
                d = bass.ds(k * BLK, BLK)
                a_sum, a_wgt, a_max = acc[:, d], pn_n, pn_max
                n = blocks((l,), l, k)
                m = blocks(MID, l, k)
                if l < 3:
                    dve.wait_ge(wide_out, blocks((0, 1, 2), l, k) + 1)
                if l == 0:
                    then(ts(f5, a_wgt, 1.0, None, ALU.max))
                    then(nc.vector.reciprocal(f5, f5))
                    dve.wait_ge(agg_out, n)
                    then(tt(f1, a_sum, f5, ALU.mult))
                    ts(f2[0:1, :], a_wgt[0:1, :], 1.0, None, ALU.min).then_inc(agg_in, 1)
                    dve.wait_ge(upd_out, n + 1)
                    dve.wait_ge(feat_turned, m)
                    stt(feat, pn_c, col("L0_gnn_c2"), xt, ALU.add, ALU.add).then_inc(feat_ready, 1)
                if l == 1:
                    then(ts(f1, a_wgt, 0.0, -BIG, ALU.is_equal, ALU.mult))
                    then(tt(f1, f1, a_max, ALU.add))
                    dve.wait_ge(self_out, n + 1)
                    tt(f2, f1, pn_c, ALU.max)
                    then(nc.vector.tensor_copy(f3, pn_c))
                    tt(f1, f1, pn_d, ALU.add)
                    tt(f2, f2, pn_d, ALU.add)
                    then(tt(f3, f3, pn_d, ALU.add))
                    f123 = share[:, BLK:4 * BLK]
                    then(stt(f123, f123, SLOPE, f123, ALU.mult, ALU.max))
                    tt(f4, f1, f2, ALU.subtract)
                    tt(f5, f3, f2, ALU.subtract).then_inc(self_diff, 1)
                    dve.wait_ge(self_exp, n + 1)
                    tt(f1, a_sum, f4, ALU.mult)
                    tt(f2, pn_b, f5, ALU.mult)
                    then(tt(f3, a_wgt, f4, ALU.mult))
                    tt(f1, f1, f2, ALU.add)
                    then(stt(f3, f3, 1e-16, f5, ALU.add, ALU.add))
                    then(nc.vector.reciprocal(f3, f3))
                    then(tt(f1, f1, f3, ALU.mult))
                    dve.wait_ge(feat_turned, m)
                    stt(feat, pn_a, skipb[:, 0:1], f1, ALU.add, ALU.add).then_inc(feat_ready, 1)
                if l == 2:
                    then(ts(f1, a_wgt, 1e-30, None, ALU.max))
                    then(nc.vector.reciprocal(f1, f1))
                    dve.wait_ge(feat_turned, m)
                    tt(feat, a_sum, f1, ALU.mult).then_inc(feat_ready, 1)
                dve.wait_ge(feat_turned, m + 1)
                if l < 3:
                    ts(acc[:, d], acc[:, d], 0.0, None, ALU.mult)
                    ts(hacc[0:HM, d], hacc[0:HM, d], 0.0, None, ALU.mult)
                src, t3 = rowsof(pn_n), rowsof(tmp)
                dve.wait_ge(x_in, blocks(ALL, l, k) + 1)
                if l in SOME:
                    then(layer_norm(then, src, t3))
                    g, b_ = (bc[:, 2 * l + j, :].unsqueeze(1).to_broadcast([P, Q, P]) for j in range(2))
                    then(tt(t3, t3, g, ALU.mult))
                    then(tt(t3, t3, b_, ALU.add))
                    then(tt(t3, t3, rowsof(old), ALU.add))
                else:
                    then(tt(t3, src, rowsof(old), ALU.add))
                    if l == 3:
                        then(tt(t3, t3, rowsof(old), ALU.add))
                if l < 3:
                    dve.wait_ge(new_turned, blocks(MORE, l, k))
                    dve.wait_ge(new_kept, m)
                else:
                    dve.wait_ge(final, 16 * k)
                layer_norm(then, t3, rowsof(new)).then_inc(new_ready, 1)

            def batch_sums(l, k, then):
                d = bass.ds(k * BLK, BLK)
                dve.wait_ge(bn_wide, k + 1)
                then(nc.vector.tensor_scalar(f1, pn_n, 1e-16, 1e-30, ALU.add, ALU.max))
                then(nc.vector.reciprocal(f1, f1))
                then(nc.vector.tensor_tensor(f1, acc[:, d], f1, ALU.mult))
                then(nc.vector.tensor_scalar(acc[:, d], f1, col("L3_gnn_bias"), None, ALU.add))
                nc.vector.bn_stats(bnst[:, bass.ds(k, 1), :].rearrange("p o s -> p (o s)"),
                                   acc[:, d]).then_inc(bn_done, 1)

            def make_membership(l, i, b):
                dve.wait_ge(summed[b], uses(l, i))
                r = rel[:, bass.ds((2 * i + b) * K, K)].unsqueeze(2).to_broadcast([P, K, WIN])
                w = win_iota[:, :].unsqueeze(1).to_broadcast([P, K, WIN])
                nc.vector.tensor_tensor(memb[:, b, :].rearrange("p (k w) -> p k w", k=K), r, w,
                                        ALU.is_equal).then_inc(memb_ready, 1)

            def edge_mlp(l, i, b):
                c = chunks(l, i, b)
                make_membership(l, i, b)
                dve.wait_ge(gathered[l][b], 16 * K * (i + 1))
                for g in range(GR):
                    n = tiles_of(g)
                    dve.wait_ge(pre_ready[g % 2], (GR // 2) * c + g // 2 + 1)
                    nc.vector.tensor_tensor(msg[:, b, 4 * g:4 * g + n, :], G[:, b, 4 * g:4 * g + n, 0:P],
                                            ps_pre[g % 2][:, 0:n * P].rearrange("p (k f) -> p k f", k=n),
                                            ALU.add).then_inc(pre_added[g % 2], 1)

            def edge_attention(l, i, b):
                g_ = gchunks(l, i, b)
                H = HEADS[l]
                JH = K * H
                tt, ts, stt = nc.vector.tensor_tensor, nc.vector.tensor_scalar, nc.vector.scalar_tensor_tensor
                v0 = VEC * g_
                tiles = bass.ds((2 * i + b) * K, K)
                make_membership(l, i, b)
                ts(notfirst[:, :], rel[:, tiles], 0.0, -BIG, ALU.not_equal, ALU.mult).then_inc(vec, 1)
                dve.wait_ge(brk_loaded[b], 16 * sum((HEADS[m] + 1) * PAIRS for m in range(1, l))
                            + 16 * (H + 1) * (i + 1))
                dve.wait_ge(sc_turned, g_ + 1)
                dve.wait_ge(seg_turned, g_)
                nc.vector.tensor_tensor_scan(segm[0:JH, :], brk[0:JH, b, :], ps_t[0:JH, 0:P], -BIG,
                                             ALU.add, ALU.max).then_inc(seg_fwd, 1)
                dve.wait_ge(seg_fwd, g_ + 1)
                dve.wait_ge(last_ready, g_)
                ts(lastm[0:JH, 0:H], row_head[H][0:JH, :], segm[0:JH, P - 1:P], None,
                   ALU.mult).then_inc(last_masked, 1)
                body = segm[0:JH, 0:P - 1][:, ::-1]
                nc.vector.tensor_tensor_scan(body, brk[0:JH, b, 1:P][:, ::-1], body, segm[0:JH, P - 1:P],
                                             ALU.add, ALU.max).then_inc(seg_all, 1)

            def edge_scores(l, i, b):
                g_ = gchunks(l, i, b)
                H = HEADS[l]
                JH = K * H
                tt, ts, stt = nc.vector.tensor_tensor, nc.vector.tensor_scalar, nc.vector.scalar_tensor_tensor
                v0 = VEC * g_
                dve.wait_ge(last_ready, g_ + 1)
                dve.wait_ge(run_kept, g_ + l - 1)
                nc.vector.tensor_tensor_scan(runmax[0:H, 1:K + 1], join[0:H, b, 0, :], ps_last[0:H, :],
                                             runmax[0:H, 0:1], ALU.add, ALU.max).then_inc(run_ready, 1)
                dve.wait_ge(run_ready, g_ + 1)
                tt(carry[0:H, :], runmax[0:H, 0:K], join[0:H, b, 1, :], ALU.add).then_inc(carry_ready, 1)
                dve.wait_ge(carry_ready, g_ + 1)
                nc.vector.tensor_copy(runmax[0:H, 0:1], runmax[0:H, K:K + 1]).then_inc(run_kept, 1)
                dve.wait_ge(carry_spread, g_)
                tt(cdiag[0:H, 0:JH].rearrange("p (h k) -> p h k", h=H),
                   carry[0:H, :].unsqueeze(1).to_broadcast([H, H, K]),
                   ident[0:H, 0:H].unsqueeze(2).to_broadcast([H, H, K]), ALU.mult).then_inc(cdiag_ready, 1)

                def hk(a):
                    return a.rearrange("p (h k) -> p h k", h=H)

                s = [scores[:, c, 0:JH] for c in range(3)]
                dst = ps_e[:, O_DST:O_DST + JH].rearrange("p (k h) -> p h k", h=H)
                dve.wait_ge(carry_spread, g_ + 1)
                tt(hk(s[0]), hk(sflat[:, 0:JH]), dst, ALU.add).then_inc(vec, 1)
                dve.wait_ge(vec, v0 + 2)
                tt(hk(s[1]), hk(ps_e[:, O_CAR:O_CAR + JH]), notfirst[:, :].unsqueeze(1).to_broadcast([P, H, K]),
                   ALU.add).then_inc(vec, 1)
                dve.wait_ge(vec, v0 + 3)
                tt(s[2], s[1], ps_e[:, O_SEG:O_SEG + JH], ALU.max).then_inc(vec, 1)
                dve.wait_ge(vec, v0 + 4)
                if l == 1:
                    dve.wait_ge(brkT_ready, 2 * i + b + 1)
                    stt(maxf[:, b, 0:JH], ps_max[:, 0:JH], -1.0 / BIG, s[2], ALU.mult, ALU.mult).then_inc(maxf_ready, 1)
                    dve.wait_ge(maxf_ready, 2 * i + b + 1)
                s12 = scores[:, 1:3, 0:JH].rearrange("p a (h k) -> p a h k", h=H)
                tt(s12, s12, dst.unsqueeze(1).to_broadcast([P, 2, H, K]), ALU.add).then_inc(vec, 1)
                dve.wait_ge(vec, v0 + 5)
                sall = scores[:, :, 0:JH]
                stt(sall, sall, SLOPE, sall, ALU.mult, ALU.max).then_inc(vec, 1)
                dve.wait_ge(vec, v0 + 6)
                dve.wait_ge(prob_ready, g_)
                tt(diff[:, :, 0:JH], scores[:, 0:2, 0:JH],
                   scores[:, 2:3, 0:JH].to_broadcast([P, 2, JH]), ALU.subtract).then_inc(diff_ready, 1)

            def edge_messages(l, i, b):
                g_ = gchunks(l, i, b)
                H = HEADS[l]
                JH = K * H
                dve.wait_ge(prob_ready, g_ + 1)
                nc.vector.tensor_tensor(msg[:, b, :, :].rearrange("p k (h c) -> p k h c", h=H),
                                        G[:, b, :, 0:P].rearrange("p k (h c) -> p k h c", h=H),
                                        prob[:, b, 0:JH].rearrange("p (h k) -> p k h", h=H).unsqueeze(3)
                                        .to_broadcast([P, K, H, P // H]),
                                        ALU.mult).then_inc(messages[b], 1)

            def edge_factors(l, i, b):
                g_ = gchunks(l, i, b)
                H = HEADS[l]
                JH = K * H
                dve.wait_ge(fac_spread, g_ + 1)
                dve.wait_ge(fac_ready, g_)
                nc.vector.tensor_tensor(facm[:, :, 0:JH].rearrange("p a (h k) -> p a h k", h=H),
                                        ps_e[:, O_FAC:O_FAC + JH].rearrange("p (h k) -> p h k", h=H)
                                        .unsqueeze(1).to_broadcast([P, 2, H, K]),
                                        masks[H][:, :, :].unsqueeze(3).to_broadcast([P, 2, H, K]),
                                        ALU.mult).then_inc(fac_masked, 1)
                dve.wait_ge(fac_masked, g_ + 1)
                nc.vector.tensor_reduce(fac[:, b, :, :], facm[:, :, 0:JH].rearrange("p a (h k) -> p a k h", h=H),
                                        AX.X, ALU.add).then_inc(fac_ready, 1)

            def add_sums(l, i, b):
                dve.wait_ge(summed[b], uses(l, i) + 1)
                if l:
                    dve.wait_ge(fac_ready, gchunks(l, i, b) + 1)
                _, first = nc.values_load_multi_w_load_instructions(
                    base_i[0:1, bass.ds((2 * i + b) * K, K)], engines=(dve.engine,), min_val=0, max_val=N,
                    skip_runtime_bounds_check_because="targets are node numbers")
                H = HEADS[l]
                for t in range(K):
                    def after(done):
                        if t:
                            dve.wait_ge(done[b], K * uses(l, i) + t)
                        else:
                            dve.wait_ge(done[1 - b], K * (uses(l, i) + b))

                    w = slice(t * WIN, (t + 1) * WIN)
                    d = bass.ds(first[t], WIN)
                    node, wgt = acc[:, d], hacc[0:H, d]
                    after(added)
                    if l == 0:
                        nc.vector.tensor_tensor(node, node, ps_msg[b][:, w], ALU.add).then_inc(added[b], 1)
                    else:
                        nc.vector.scalar_tensor_tensor(node, node, fac[:, b, 0, t:t + 1], ps_msg[b][:, w],
                                                       ALU.mult, ALU.add).then_inc(added[b], 1)
                    after(weighed)
                    if l == 0:
                        nc.vector.tensor_tensor(wgt, wgt, ps_wgt[b][0:H, w], ALU.add).then_inc(weighed[b], 1)
                    else:
                        nc.vector.scalar_tensor_tensor(wgt, wgt, fac[0:H, b, 1, t:t + 1], ps_wgt[b][0:H, w],
                                                       ALU.mult, ALU.add).then_inc(weighed[b], 1)
                    if l == 1:
                        dve.wait_ge(maxed, K * (2 * i + b) + t)
                        nc.vector.tensor_copy(hacc[WIN:WIN + H, d], ps_max[0:H, w]).then_inc(maxed, 1)

            def front(l, i, b):
                if l == 0:
                    edge_mlp(l, i, b)
                else:
                    edge_attention(l, i, b)
                    edge_scores(l, i, b)
                    edge_messages(l, i, b)

            def factors(l, i, b):
                if l:
                    edge_factors(l, i, b)

            STEPS = {0: 13, 1: 19, 2: 6, 3: 5}
            for l in range(LAYERS):
                if l in (1, 3):
                    nc.vector.memset(wtab[:, :, :], 0.0).then_inc(wtab_clear, 1)
                if l:
                    node_loop(l - 1, STEPS[l - 1], node_block)
                    nc.vector.memset(runmax[:, :], -BIG).then_inc(run_kept, 1)
                front(l, 0, 0)
                with dve.Fori(0, PAIRS - 1) as i:
                    factors(l, i, 0)
                    front(l, i, 1)
                    add_sums(l, i, 0)
                    factors(l, i, 1)
                    front(l, i + 1, 0)
                    add_sums(l, i, 1)
                factors(l, PAIRS - 1, 0)
                front(l, PAIRS - 1, 1)
                add_sums(l, PAIRS - 1, 0)
                factors(l, PAIRS - 1, 1)
                add_sums(l, PAIRS - 1, 1)
            node_loop(3, 4, batch_sums)
            dve.wait_ge(bn_done, NBLK)
            start = count[0]
            left = N - (NBLK - 1) * BLK
            nth = [start]

            def then(ins):
                nth[0] += 1
                ins.then_inc(nvec, 1)
                dve.wait_ge(nvec, nth[0])

            then(nc.vector.bn_stats(bnst[:, NBLK - 1, :], acc[:, (NBLK - 1) * BLK:N]))
            then(nc.vector.bn_aggr(bnmv[:, :], bnst[:, :, :].rearrange("p k s -> p (k s)")))
            nc.vector.tensor_scalar(bnsc[:, 0:1], bnmv[:, 1:2], EPS_LN, None, ALU.add).then_inc(bn_var, 1)
            dve.wait_ge(bn_rstd, 1)
            then(nc.vector.tensor_tensor(bnsc[:, 0:1], bnsc[:, 0:1], col("L3_gnn_gamma"), ALU.mult))
            then(nc.vector.tensor_tensor(bnsc[:, 2:3], bnmv[:, 0:1], bnsc[:, 0:1], ALU.mult))
            nc.vector.tensor_tensor(bnsc[:, 1:2], col("L3_gnn_beta"), bnsc[:, 2:3], ALU.subtract).then_inc(bn_ready, 1)
            count[0] = nth[0]
            node_loop(3, STEPS[3], node_block)


def _lay(a, pad, value):
    import numpy as np
    return np.pad(a, [(0, pad)] + [(0, 0)] * (a.ndim - 1), constant_values=value)


def kernel(**inputs):
    import numpy as np
    import concourse.bacc as bacc
    from concourse.bass_utils import run_bass_kernel_spmd

    P, K = 128, 13
    a = {k: np.ascontiguousarray(v) for k, v in inputs.items()}
    n = a["x"].shape[0]
    edges = a["src"].shape[0]
    chunks = -(-edges // (P * K))
    pad = chunks * P * K - edges
    arrays = {}
    for name, v in a.items():
        if name.startswith("L1_gnn_att_") or name.startswith("L2_gnn_attn") or name.startswith("L3_gnn_att_"):
            v = v.reshape(-1)
        arrays[name] = v
    arrays["x"] = _lay(a["x"], -n % 512, 0)
    arrays["src"] = np.ascontiguousarray(_lay(a["src"], pad, 0).reshape(chunks, K, P).transpose(0, 2, 1))
    dst = _lay(a["dst"], pad, n)
    del arrays["dst"]
    arrays["dst_cols"] = np.ascontiguousarray(dst.reshape(chunks * K, P).T)
    arrays["dst_rows"] = np.ascontiguousarray(dst.reshape(chunks, K * P))
    arrays["edge_attr_64"] = np.ascontiguousarray(_lay(a["edge_attr_64"], pad, 0).T)

    nc = bacc.Bacc("TRN2", target_bir_lowering=False, num_devices=1, dynamic_dma_scratch_size=8192)
    aps, fed = {}, {}
    for name, v in arrays.items():
        aps[name] = nc.dram_tensor(f"in_{name}", v.shape, mybir.dt.from_np(v.dtype), kind="ExternalInput").ap()
        fed[f"in_{name}"] = v
    out = nc.dram_tensor("out", (n, P), mybir.dt.float32, kind="ExternalOutput").ap()
    gnn_program(nc, aps, out)
    r = run_bass_kernel_spmd(nc, [fed], core_ids=[0])
    return r.results[0]["out"]
```

```python
import concourse.bass as bass
from concourse import mybir
from contextlib import ExitStack


def gnn_program(nc, A, out):
    fp32 = mybir.dt.float32
    i32 = mybir.dt.int32
    ALU = mybir.AluOpType
    ACT = mybir.ActivationFunctionType
    AX = mybir.AxisListType

    P = 128
    N = out.shape[0]
    E = A["edge_attr_64"].shape[1]
    ED = A["edge_attr_64"].shape[0]
    K = A["src"].shape[2]
    CH = A["src"].shape[0]
    TILES = K * CH
    PAIRS = CH // 2
    PIECES = 4
    PIECE = TILES // PIECES
    WIN = 32
    BLK = 512
    NP = A["x"].shape[0]
    NBLK = NP // BLK
    Q = BLK // P
    GR = -(-K // 4)
    LAYERS = 4
    HEADS = [1, 4, 4, 8]
    HM = max(HEADS)
    BIG = float(2 ** 100)
    SLOPE = 0.2
    EPS_LN = 1e-5
    ROW = P + HM

    def tiles_of(g):
        return min(4, K - 4 * g)

    ctx = ExitStack()
    with ctx:
        def sb(name, shape, dt=fp32):
            return ctx.enter_context(nc.sbuf_tensor(name, shape, dt))

        def sem(name):
            return ctx.enter_context(nc.semaphore(name))

        def pair(name):
            return [sem(f"{name}{b}") for b in range(2)]

        def dram(name, shape, dt=fp32):
            return nc.dram_tensor(name, shape, dt, kind="Internal").ap()

        width = [P] + [P + h for h in HEADS[1:]]
        rows = [dram(f"rows{l}", (NP, width[l])) for l in range(LAYERS)]
        wins = [dram(f"wins{l}", (NP, P if l == 0 else HEADS[l])) for l in range(LAYERS)]
        breaks = dram("breaks", (TILES, P))
        joins = dram("joins", (2, TILES))

        acc = sb("acc", [P, NP])
        hacc = sb("hacc", [HM, NP])
        xn = sb("xn", [P, NP // P, P])
        base_i = sb("base_i", [P, TILES], i32)
        rel = sb("rel", [P, TILES])
        ident = sb("ident", [P, P])
        spread = sb("spread", [HM, 3, P])
        masks = {4: sb("masks4", [P, 2, 4]), 8: sb("masks8", [P, 2, 8])}
        ones = sb("ones", [P, P])
        win_iota = sb("win_iota", [P, WIN])
        head_of = {4: sb("head4", [P, 4]), 8: sb("head8", [P, 8])}
        late4 = sb("late4", [P, 8])
        row_head = {h: sb(f"row_head{h}", [P, h]) for h in (4, 8)}
        row_tile = {h: sb(f"row_tile{h}", [P, K]) for h in (4, 8)}

        G = sb("G", [P, 2, K, ROW])
        idx = sb("idx", [P, 2, K], i32)
        msg = sb("msg", [P, 2, K, P])
        prob = sb("prob", [P, 2, K * HM])
        memb = sb("memb", [P, 2, K * WIN])
        membT = sb("membT", [P, GR * P])
        brk = sb("brk", [P, 2, P])
        join = sb("join", [HM, 2, 2, K])
        wtab = sb("wtab", [P, 2, K * P])
        sflat = sb("sflat", [P, P])
        segm = sb("segm", [P, P])
        lastm = sb("lastm", [P, HM])
        runmax = sb("runmax", [HM, K + 1])
        carry = sb("carry", [HM, K])
        cdiag = sb("cdiag", [HM, HM * K])
        notfirst = sb("notfirst", [P, K])
        scores = sb("scores", [P, 3, K * HM])
        diff = sb("diff", [P, 2, K * HM])
        prow = sb("prow", [1, K * HM])
        facm = sb("facm", [P, 2, K * HM])
        fac = sb("fac", [P, 2, 2, K])

        share = sb("share", [P, max(12 * BLK, 4 * TILES)])
        lhs = share[0:ED + WIN, 0:2 * K * P].rearrange("p (b n) -> p b n", b=2)
        xt, f1, f2, f3, f4, f5, feat, old, tmp, new = (share[:, k * BLK:(k + 1) * BLK] for k in range(10))
        tab = share[:, 10 * BLK:12 * BLK].rearrange("p (q n) -> p q n", q=Q)

        def rowsof(a):
            return a.rearrange("p (q f) -> p q f", q=Q)

        hst = sb("hst", [HM, BLK])
        minus_half = sb("minus_half", [P, Q])
        paced = sb("paced", [1, 2])
        varn = sb("varn", [P, Q])
        stats = sb("stats", [P, Q, 6])
        mv = sb("mv", [P, Q, 2])
        rstd = sb("rstd", [P, Q])
        bnst = sb("bnst", [P, NBLK, 6])
        bnmv = sb("bnmv", [P, 2])
        bnsc = sb("bnsc", [P, 3])

        w1 = sb("w1", [P, 2 * P])
        w1e = sb("w1e", [ED, P])
        w2 = sb("w2", [P, P])
        u1 = sb("u1", [P, 2, P])
        u2 = sb("u2", [P, P])
        wsk = sb("wsk", [P, P])
        wext = [None] + [sb(f"wext{l}", [P, P + 2 * HEADS[l]]) for l in (1, 2, 3)]
        wside = sb("wside", [P, 2, P])
        wexp = sb("wexp", [P, 2, P])
        wT = sb("wT", [P, 4, P])
        att = sb("att", [P, 6, HM])
        rowv = sb("rowv", [1, 7, P])
        brow = sb("brow", [1, 2, 2 * P])
        bc = sb("bc", [P, 4, P])
        COL = {n: k for k, n in enumerate(
            ["L0_gnn_c1", "L0_gnn_c2", "L1_gnn_gat_bias", "L1_gnn_skip_b", "L3_gnn_bias", "L3_gnn_gamma",
             "L3_gnn_beta", "L1_gnn_att_src", "L1_gnn_att_dst", "L2_gnn_attn_l", "L2_gnn_attn_r",
             "L3_gnn_att_src", "L3_gnn_att_dst", "L2_gnn_b_src", "L2_gnn_b_dst"])}
        RW = {n: k for k, n in enumerate(
            ["L0_gnn_gamma", "L0_gnn_beta", "L1_gnn_ln_g", "L1_gnn_ln_b", "L0_gnn_b1", "L0_gnn_b2", "L2_gnn_b_val"])}
        cols = sb("cols", [P, len(COL)])
        skipb = sb("skipb", [P, 1])

        def col(name):
            return cols[:, COL[name]:COL[name] + 1]

        ps = ctx.enter_context(nc.psum_tensor("ps", [P, 8, BLK], fp32))
        ps_msg, ps_wgt = [ps[:, 0, :], ps[:, 2, :]], [ps[:, 1, :], ps[:, 3, :]]
        ps_mT, ps_e, ps_t, ps_brk = (ps[:, k, :] for k in (4, 5, 6, 7))
        ps_pre = [ps[:, 5 + g % 3, :] for g in range(GR)]
        O_DST, O_CAR, O_FAC, O_SEG = (k * K * HM for k in range(4))
        ps_last = ps[:, 6, 2 * P:2 * P + K]
        pn_tab = ps[:, 0:2, :].rearrange("p a n -> p (a n)").rearrange("p (q n) -> p q n", q=Q)
        pn_max = ps[:, 0, :]
        pn_a, pn_b, pn_c, pn_d, pn_n, pn_t = (ps[:, k, :] for k in range(2, 8))

        loaded = sem("inputs_loaded")
        built = sem("constants_built")
        norm_paced, gather_paced = sem("norm_paced"), sem("gather_paced")
        step = sem("vector_setup_step")
        setup_pe = sem("setup_products_ready")
        setup_copied = sem("setup_products_copied")
        tables_in = sem("edge_tables_stored")
        gathered = [pair(f"gathered_l{l}_") for l in range(LAYERS)]
        win_loaded = [pair(f"windows_loaded_l{l}_") for l in range(LAYERS)]
        idx_loaded = pair("indices_loaded")
        ef_loaded = pair("edge_features_loaded")
        brk_loaded = pair("breaks_loaded")
        messages = pair("messages_ready")
        memb_ready, memb_turned, memb_copied = (sem(f"membership_{w}") for w in ("ready", "turned", "copied"))
        summed = pair("window_sums_ready")
        added = pair("window_sums_added")
        weighed = pair("window_weights_added")
        wtab_clear = sem("window_blocks_cleared")
        pre_ready = [pair(f"preactivation{g}_ready") for g in range(GR)]
        pre_added = [sem(f"preactivation{g}_added") for g in range(GR)]
        hidden = pair("hidden_ready")
        sc_copied, sc_turned = sem("scores_copied"), sem("scores_turned")
        seg_fwd, seg_all, seg_turned = (sem(f"segment_maxima_{w}") for w in ("scanned_forward", "ready", "turned"))
        last_masked, last_ready = sem("last_maxima_masked"), sem("last_maxima_ready")
        run_ready, carry_ready, run_kept = sem("running_maxima_ready"), sem("carry_ready"), sem("running_maximum_kept")
        cdiag_ready, carry_spread = sem("carry_diagonal_ready"), sem("carry_spread")
        dst_ready = pair("target_scores_ready")
        vec = sem("vector_score_step")
        diff_ready = sem("score_differences_ready")
        factor_ready, prob_ready = sem("carry_factors_ready"), sem("weights_ready")
        fac_spread, fac_masked, fac_ready = (sem(f"carry_factors_{w}") for w in ("spread", "masked", "by_feature"))
        brkT_ready, maxf_ready = sem("first_flags_turned"), sem("first_maxima_ready")
        nvec = sem("node_vector_step")
        x_in = sem("node_rows_copied")
        old_turned, old_copied = sem("old_features_turned"), sem("old_features_copied")
        agg_in, agg_out, agg_copied = (sem(f"aggregate_{w}") for w in ("ready", "multiplied", "copied"))
        hid_out, hid_ready, upd_out = sem("update_hidden_multiplied"), sem("update_hidden_ready"), sem("update_multiplied")
        self_out, self_diff, self_exp = (sem(f"self_loop_{w}") for w in ("products_ready", "differences_ready", "weights_ready"))
        var_ready, rstd_ready = sem("variances_ready"), sem("inverse_deviations_ready")
        wide_out = sem("head_sums_spread")
        bn_in, bn_wide, bn_done = sem("batch_head_sums_copied"), sem("batch_head_sums_spread"), sem("batch_block_ready")
        bn_var, bn_rstd = sem("batch_variance_ready"), sem("batch_inverse_deviation_ready")
        bn_ready = sem("batch_statistics_ready")
        feat_ready, feat_turned = sem("layer_output_ready"), sem("layer_output_turned")
        new_ready, new_kept = sem("new_features_ready"), sem("new_features_kept")
        new_turned, new_copied = sem("new_features_turned"), sem("new_features_copied")
        tab_out, tab_ready, stored = sem("table_rows_multiplied"), sem("table_rows_ready"), sem("table_rows_stored")
        final = sem("output_stored")

        block = ctx.enter_context(nc.Block())

        N_LOADS = 17 + len(COL) + len(RW)
        N_BUILT = 10
        STEP_FIRST, STEP_ATT, STEP_TABLES, STEP_END = 1, 3, 13, 22
        VEC = 6

        ROWS = [1, 8, 4, 8]

        def chunks(l, i, b):
            return l * CH + 2 * i + b

        def gchunks(l, i, b):
            return (l - 1) * CH + 2 * i + b

        def is_last(i, b):
            return isinstance(i, int) and i == PAIRS - 1 and b == 1

        def uses(l, i):
            return l * PAIRS + i

        def guses(l, i):
            return (l - 1) * PAIRS + i

        def blocks(layers, l, k):
            return NBLK * sum(m < l for m in layers) + k

        NORMS = {0: 2, 1: 2, 2: 1, 3: 1}

        def norms_before(l, k):
            return NBLK * sum(NORMS[m] for m in range(l)) + NORMS[l] * k

        ALL, SOME, MID, MORE = (-1, 0, 1, 2, 3), (0, 1), (0, 1, 2, 3), (-1, 0, 1, 2)

        @block.sync
        def _(sp):
            n_in = [0]

            def load(dst, src):
                sp.dma_start(dst, src).then_inc(loaded, 16)
                n_in[0] += 1

            load(base_i[:, :], A["dst_cols"])
            load(share[0:1, 0:TILES].bitcast(i32), A["dst_cols"][P - 1:P, :])
            load(msg[0:CH, 0, :, :].rearrange("p k n -> p (k n)").bitcast(i32), A["dst_rows"])
            load(w1[:, 0:P], A["L0_gnn_W1"][0:P, :])
            load(w1[:, P:2 * P], A["L0_gnn_W1"][P:2 * P, :])
            load(w1e[:, :], A["L0_gnn_W1"][2 * P:2 * P + ED, :])
            load(w2[:, :], A["L0_gnn_W2"])
            load(u1[:, 0, :], A["L0_gnn_U1"][0:P, :])
            load(u1[:, 1, :], A["L0_gnn_U1"][P:2 * P, :])
            load(u2[:, :], A["L0_gnn_U2"])
            load(wsk[:, :], A["L1_gnn_skip_W"])
            load(wext[1][:, 0:P], A["L1_gnn_W"])
            load(wext[2][:, 0:P], A["L2_gnn_W_val"])
            load(wside[:, 0, :], A["L2_gnn_W_src"])
            load(wside[:, 1, :], A["L2_gnn_W_dst"])
            load(wext[3][:, 0:P], A["L3_gnn_W"])
            for name, k in COL.items():
                load(cols[:, k:k + 1], A[name].rearrange("(p o) -> p o", o=1))
            for name, k in RW.items():
                load(rowv[0:1, k, :], A[name].rearrange("(o n) -> o n", o=1))
            load(xn[:, :, :], A["x"].rearrange("(t p) f -> p t f", p=P))
            assert n_in[0] == N_LOADS, n_in

            sp.wait_ge(step, STEP_TABLES)
            sp.dma_start(breaks.rearrange("(c k) n -> c (k n)", k=K),
                         msg[0:CH, 1, :, :].rearrange("p k n -> p (k n)")).then_inc(tables_in, 16)
            sp.dma_start(joins[0:1, :], share[0:1, 2 * TILES:3 * TILES]).then_inc(tables_in, 16)
            sp.dma_start(joins[1:2, :], share[0:1, 3 * TILES:4 * TILES]).then_inc(tables_in, 16)
            sp.wait_ge(tables_in, 48)

            def store_tables(l, k):
                sp.wait_ge(tab_ready, blocks(MORE, l, k) + 1)
                d = bass.ds(k * BLK, BLK)
                wr = width[l + 1]
                wt = wins[l + 1].shape[1]
                sp.dma_start(rows[l + 1][d, :].rearrange("(q p) c -> p q c", p=P),
                             tab[:, :, 0:wr]).then_inc(stored, 16)
                sp.dma_start(wins[l + 1][d, :].rearrange("(q p) c -> p q c", p=P),
                             tab[:, :, wr:wr + wt]).then_inc(stored, 16)

            for l in range(LAYERS):
                with sp.Fori(0, NBLK) as k:
                    store_tables(l - 1, k)
                sp.wait_ge(stored, 32 * NBLK * (l + 1))
                if l in (1, 3):
                    sp.wait_ge(wtab_clear, 1 if l == 1 else 2)
                H = HEADS[l]
                with sp.Fori(0, PAIRS) as i:
                    for b in range(2):
                        t0 = (2 * i + b) * K
                        sp.wait_ge(gathered[l][b], 16 * K * i)
                        sp.dma_start(idx[:, b, :], A["src"][bass.ds(2 * i + b, 1), :, :]
                                     .rearrange("o p k -> p (o k)")).then_inc(idx_loaded[b], 16)
                        if l == 0:
                            sp.wait_ge(pre_ready[GR - 1][b], i)
                            sp.dma_start(lhs[0:ED, b, :], A["edge_attr_64"][:, bass.ds(t0 * P, K * P)]).then_inc(
                                ef_loaded[b], 16)
                        else:
                            sp.wait_ge(dst_ready[b], guses(l, i))
                            sp.wait_ge(messages[b], guses(l, i))
                            for h in range(H):
                                sp.dma_start(brk[h * K:(h + 1) * K, b, :],
                                             breaks[bass.ds(t0, K), :]).then_inc(brk_loaded[b], 16)
                            sp.dma_start(join[0:H, b, :, :], joins[:, bass.ds(t0, K)].unsqueeze(0)
                                         .to_broadcast([H, 2, K])).then_inc(brk_loaded[b], 16)
                        _, first = nc.values_load_multi_w_load_instructions(
                            base_i[0:1, bass.ds(t0, K)], engines=(sp.engine,), min_val=0, max_val=N,
                            skip_runtime_bounds_check_because="targets are node numbers")
                        for t in range(K):
                            g, q = t // 4, t % 4
                            if l == 0:
                                dst = wtab[ED:ED + WIN, b, t * P:(t + 1) * P]
                            else:
                                dst = wtab[WIN * q:WIN * (q + 1), b, g * BLK + q * H:g * BLK + (q + 1) * H]
                            sp.dma_start(dst, wins[l][bass.ds(first[t], WIN), :]).then_inc(win_loaded[l][b], 16)

            with sp.Fori(0, NBLK - 1) as k:
                sp.wait_ge(new_ready, blocks(MID, 3, k) + 1)
                sp.dma_start(out[bass.ds(k * BLK, BLK), :].rearrange("(q p) c -> p q c", p=P),
                             rowsof(new)).then_inc(final, 16)
            sp.wait_ge(new_ready, blocks(MID, 3, NBLK))
            left = N - (NBLK - 1) * BLK
            assert left <= P
            sp.dma_start(out[(NBLK - 1) * BLK:N, :], new[0:left, 0:P]).then_inc(final, 16)
            sp.wait_ge(final, 16 * NBLK)

        @block.gpsimd
        def _(pool):
            nc.gpsimd.memset(ones[:, :], 1.0).then_inc(built, 1)
            nc.gpsimd.iota(win_iota[:, :], [[1, WIN]], base=0, channel_multiplier=0,
                           allow_small_or_imprecise_dtypes=True).then_inc(built, 1)
            pool.wait_ge(built, 2)
            nc.gpsimd.affine_select(out=ident[:, :], in_=ones[:, :], compare_op=ALU.is_equal, fill=0.0, base=0,
                                    pattern=[[-1, P]], channel_multiplier=1).then_inc(built, 1)
            n = 3
            for size, tens, count in ((P // 4, head_of[4], 4), (P // 8, head_of[8], 8),
                                      (K, row_head[8], 8)):
                nc.gpsimd.affine_select(out=tens[:, :], in_=ones[:, 0:count], compare_op=ALU.is_ge, fill=0.0,
                                        base=0, pattern=[[-size, count]], channel_multiplier=1).then_inc(built, 1)
                n += 1
                pool.wait_ge(built, n)
                nc.gpsimd.affine_select(out=tens[:, :], in_=tens[:, :], compare_op=ALU.is_ge, fill=0.0,
                                        base=size - 1, pattern=[[size, count]],
                                        channel_multiplier=-1).then_inc(built, 1)
                n += 1
            nc.gpsimd.memset(minus_half[:, :], -0.5)
            for unused in (sflat, segm, lastm, brk):
                nc.gpsimd.memset(unused[:], 0.0)
            nc.gpsimd.memset(runmax[:, :], -BIG).then_inc(built, 1)
            assert n + 1 == N_BUILT, n

            def node_norms(l, k):
                for j in range(NORMS[l]):
                    pool.wait_ge(var_ready, norms_before(l, k) + j + 1)
                    nc.gpsimd.tensor_tensor(rstd[:, :], varn[:, :], minus_half[:, :], ALU.pow).then_inc(rstd_ready, 1)

            for l in range(LAYERS):
                if l:
                    with pool.Fori(0, NBLK) as k:
                        node_norms(l - 1, k)
                pool.wait_ge(stored, 32 * NBLK * (l + 1))
                with pool.Fori(0, PAIRS) as i:
                    for b in range(2):
                        pool.wait_ge(idx_loaded[b], 16 * (uses(l, i) + 1))
                        if l == 0:
                            pool.wait_ge(hidden[b], GR * i)
                        else:
                            pool.wait_ge(messages[b], guses(l, i))
                            if l == 1:
                                pool.wait_ge(summed[b], PAIRS)
                        pool.wait_ge(gather_paced, chunks(l, i, b))
                        nc.gpsimd.tensor_tensor(paced[0:1, 1:2], minus_half[0:1, 0:1], minus_half[0:1, 0:1],
                                                ALU.add).then_inc(gather_paced, 1)
                        for t in range(K):
                            nc.gpsimd.indirect_dma_start(
                                G[:, b, t, 0:width[l]], None, rows[l],
                                bass.IndirectOffsetOnAxis(idx[:, b, t:t + 1], 0)).then_inc(gathered[l][b], 16)
            pool.wait_ge(bn_var, 1)
            nc.gpsimd.tensor_tensor(bnsc[:, 0:1], bnsc[:, 0:1], minus_half[:, 0:1], ALU.pow).then_inc(bn_rstd, 1)
            with pool.Fori(0, NBLK) as k:
                node_norms(3, k)

        @block.tensor
        def _(pe):
            pe.wait_ge(loaded, 16 * N_LOADS)
            pe.wait_ge(built, N_BUILT)
            for k, w in enumerate((wext[1][:, 0:P], wside[:, 0, :], wside[:, 1, :], wext[3][:, 0:P])):
                nc.tensor.transpose(ps_t[:, k * P:(k + 1) * P], w, ident[:, :])
            for k in range(4):
                nc.tensor.matmul(ps_mT[:, k * P:(k + 1) * P], ones[0:1, :], rowv[0:1, k, :], start=True, stop=True)
            pe.wait_ge(step, STEP_FIRST)
            for k in range(PIECES):
                last = nc.tensor.matmul(ps[:, k, 0:PIECE], ones[0:1, :],
                                        acc[0:1, k * PIECE:(k + 1) * PIECE], start=True, stop=True)
            last.then_inc(setup_pe, 1)
            pe.wait_ge(step, STEP_ATT)
            for k, (w, h) in enumerate(((0, 4), (0, 4), (1, 4), (2, 4), (3, 8), (3, 8))):
                nc.tensor.matmul(ps_e[:, k * HM:k * HM + h], wT[:, w, :], att[:, k, 0:h], start=True, stop=True)
            nc.tensor.matmul(ps_e[0:1, 64:68], col("L2_gnn_b_src"), att[:, 2, 0:4], start=True, stop=True)
            nc.tensor.matmul(ps_e[0:1, 68:72], col("L2_gnn_b_dst"), att[:, 3, 0:4],
                             start=True, stop=True)
            for k, heads in enumerate((head_of[4], head_of[8], late4)):
                h = heads.shape[1]
                last = nc.tensor.transpose(ps[0:h, 6, k * P:(k + 1) * P], heads[:, :], ident[:, :])
            last.then_inc(setup_pe, 1)
            pe.wait_ge(setup_copied, 1)

            def turn(dst, src, signal):
                for q in range(Q):
                    last = nc.tensor.transpose(dst[:, q * P:(q + 1) * P], src[:, q * P:(q + 1) * P], ident[:, :])
                last.then_inc(signal, 1)

            def node_block(l, k):
                pe.wait_ge(x_in, blocks(ALL, l, k) + 1)
                if l in SOME:
                    turn(pn_t, old, old_turned)
                n = blocks((l,), l, k)
                if l in (0, 1, 2):
                    H = HEADS[l]
                    sp_ = ones[0:1, :] if l == 0 else spread[0:H, 0, :]
                    last = nc.tensor.matmul(pn_n, sp_, hst[0:H, :], start=True, stop=True)
                    if l == 1:
                        last = nc.tensor.matmul(pn_max, spread[:, 2, :], hst[:, :], start=True, stop=True)
                    last.then_inc(wide_out, 1)
                if l == 0:
                    pe.wait_ge(agg_in, n + 1)
                    nc.tensor.matmul(pn_a, w2[:, :], f1, start=True, stop=False)
                    nc.tensor.matmul(pn_a, rowv[0:1, RW["L0_gnn_b2"], :], f2[0:1, :], start=False,
                                     stop=True).then_inc(agg_out, 1)
                    pe.wait_ge(old_copied, blocks(SOME, l, k) + 1)
                    pe.wait_ge(agg_copied, n + 1)
                    nc.tensor.matmul(pn_b, u1[:, 0, :], xt, start=True, stop=False)
                    nc.tensor.matmul(pn_b, u1[:, 1, :], f3, start=False, stop=True).then_inc(hid_out, 1)
                    pe.wait_ge(hid_ready, n + 1)
                    nc.tensor.matmul(pn_c, u2[:, :], f4, start=True, stop=True).then_inc(upd_out, 1)
                if l == 1:
                    pe.wait_ge(old_copied, blocks(SOME, l, k) + 1)
                    nc.tensor.matmul(pn_a, wsk[:, :], xt, start=True, stop=True)
                    nc.tensor.matmul(pn_b, wext[1][:, 0:P], xt, start=True, stop=True)
                    nc.tensor.matmul(pn_c, wexp[:, 0, :], xt, start=True, stop=True)
                    nc.tensor.matmul(pn_d, wexp[:, 1, :], xt, start=True, stop=True).then_inc(self_out, 1)
                if l >= 0:
                    pe.wait_ge(feat_ready, blocks(MID, l, k) + 1)
                    turn(pn_n, feat, feat_turned)
                if l < 3:
                    if l >= 0:
                        pe.wait_ge(new_ready, blocks(MID, l, k) + 1)
                    turn(pn_t, new, new_turned)
                    pe.wait_ge(new_copied, blocks(MORE, l, k) + 1)
                    w = w1 if l == -1 else wext[l + 1]
                    cw = w.shape[1]
                    bias = {-1: 0, 1: 1}.get(l)
                    for q in range(Q):
                        last = nc.tensor.matmul(pn_tab[:, q, 0:cw], xt[:, q * P:(q + 1) * P], w[:, :],
                                                start=True, stop=bias is None)
                        if bias is not None:
                            last = nc.tensor.matmul(pn_tab[:, q, 0:cw], ones[0:1, :], brow[0:1, bias, 0:cw],
                                                    start=False, stop=True)
                    last.then_inc(tab_out, 1)
                    pe.wait_ge(tab_ready, blocks(MORE, l, k) + 1)

            def turn_membership(l, i, b):
                pe.wait_ge(memb_ready, chunks(l, i, b) + 1)
                pe.wait_ge(memb_copied, chunks(l, i, b))
                for g in range(GR):
                    n = tiles_of(g) * WIN
                    last = nc.tensor.transpose(ps_mT[0:n, g * P:(g + 1) * P],
                                               memb[:, b, g * P:g * P + n], ident[:, :])
                last.then_inc(memb_turned, 1)

            def front_mlp(l, i, b, prev):
                c = chunks(l, i, b)
                turn_membership(l, i, b)
                if prev:
                    sums(l, *prev, 0, 8)
                pe.wait_ge(ef_loaded[b], 16 * (i + 1))
                pe.wait_ge(win_loaded[l][b], 16 * K * (i + 1))
                pe.wait_ge(memb_copied, c + 1)
                for g in range(GR):
                    if g == 0:
                        pe.wait_ge(pre_added[GR - 1], c)
                    elif g < GR - 1:
                        pe.wait_ge(pre_added[g], c)
                    else:
                        if prev:
                            sums(l, *prev, 8, K)
                        pe.wait_ge(pre_added[0], c + 1)
                    for q in range(tiles_of(g)):
                        t = slice((4 * g + q) * P, (4 * g + q + 1) * P)
                        last = nc.tensor.matmul(ps_pre[g][:, q * P:(q + 1) * P], lhs[:, b, t],
                                                wtab[0:ED + WIN, b, t], start=True, stop=True)
                    last.then_inc(pre_ready[g][b], 1)

            def front_attention(l, i, b, prev):
                g_ = gchunks(l, i, b)
                H = HEADS[l]
                JH = K * H
                turn_membership(l, i, b)
                if prev:
                    sums(l, *prev, 0, 5)
                pe.wait_ge(fac_masked, g_)
                pe.wait_ge(memb_copied, chunks(l, i, b) + 1)
                pe.wait_ge(win_loaded[l][b], 16 * K * (i + 1))
                for g in range(GR):
                    n = tiles_of(g)
                    last = nc.tensor.matmul(ps_e[:, O_DST + 4 * g * H:O_DST + (4 * g + n) * H],
                                            membT[0:n * WIN, g * P:(g + 1) * P],
                                            wtab[0:n * WIN, b, g * BLK:g * BLK + n * H], start=True, stop=True)
                last.then_inc(dst_ready[b], 1)
                pe.wait_ge(sc_copied, g_ + 1)
                pe.wait_ge(run_ready, g_)
                nc.tensor.transpose(ps_t[:, 0:P], sflat[:, :], ident[:, :]).then_inc(sc_turned, 1)
                if prev:
                    sums(l, *prev, 5, 6)
                pe.wait_ge(last_masked, g_ + 1)
                nc.tensor.matmul(ps_last[0:H, :], lastm[:, 0:H], row_tile[H][:, :],
                                 start=True, stop=True).then_inc(last_ready, 1)
                pe.wait_ge(seg_all, g_ + 1)
                nc.tensor.transpose(ps_e[:, O_SEG:O_SEG + P], segm[:, :], ident[:, :]).then_inc(seg_turned, 1)
                if l == 1:
                    nc.tensor.transpose(ps_brk[:, 0:P], brk[:, b, :], ident[:, :]).then_inc(brkT_ready, 1)
                pe.wait_ge(cdiag_ready, g_ + 1)
                nc.tensor.matmul(ps_e[:, O_CAR:O_CAR + JH], ones[0:H, :], cdiag[0:H, 0:JH],
                                 start=True, stop=True).then_inc(carry_spread, 1)
                if prev:
                    sums(l, *prev, 6, K)

            def spread_factors(l, i, b):
                g_ = gchunks(l, i, b)
                JH = K * HEADS[l]
                pe.wait_ge(factor_ready, g_ + 1)
                nc.tensor.matmul(ps_e[:, O_FAC:O_FAC + JH], ones[0:1, :], prow[0:1, 0:JH],
                                 start=True, stop=True).then_inc(fac_spread, 1)

            def sums(l, i, b, t0, t1):
                H = HEADS[l]
                if t0 == 0:
                    pe.wait_ge(added[b], K * uses(l, i))
                    pe.wait_ge(weighed[b], K * uses(l, i))
                    if l:
                        pe.wait_ge(messages[b], guses(l, i) + 1)
                for t in range(t0, t1):
                    if l == 0 and (t % 4 == 0 or t == t0):
                        pe.wait_ge(hidden[b], GR * i + t // 4 + 1)
                    m = memb[:, b, t * WIN:(t + 1) * WIN]
                    o = slice(t * WIN, (t + 1) * WIN)
                    nc.tensor.matmul(ps_msg[b][:, o], msg[:, b, t, :], m, start=True, stop=True)
                    if l == 0:
                        wgt = ones[:, 0:1]
                    else:
                        wgt = prob[:, b, t:t + (ROWS[l] - 1) * K + 1:K]
                    last = nc.tensor.matmul(ps_wgt[b][0:ROWS[l], o], wgt, m, start=True, stop=True)
                if t1 == K:
                    last.then_inc(summed[b], 1)

            def front(l, i, b, prev):
                (front_attention if l else front_mlp)(l, i, b, prev)

            def factors(l, i, b):
                if l:
                    spread_factors(l, i, b)

            for l in range(LAYERS):
                with pe.Fori(0, NBLK) as k:
                    node_block(l - 1, k)
                front(l, 0, 0, None)
                factors(l, 0, 0)
                front(l, 0, 1, (0, 0))
                with pe.Fori(0, PAIRS - 1) as i:
                    factors(l, i, 1)
                    front(l, i + 1, 0, (i, 1))
                    factors(l, i + 1, 0)
                    front(l, i + 1, 1, (i + 1, 0))
                factors(l, PAIRS - 1, 1)
                sums(l, PAIRS - 1, 1, 0, K)
                pe.wait_ge(added[1], K * uses(l + 1, 0))
                pe.wait_ge(weighed[1], K * uses(l + 1, 0))
            with pe.Fori(0, NBLK) as k:
                pe.wait_ge(bn_in, k + 1)
                pe.wait_ge(bn_done, k)
                nc.tensor.matmul(pn_n, spread[:, 1, :], hst[:, :], start=True, stop=True).then_inc(bn_wide, 1)
            pe.wait_ge(bn_ready, 1)
            with pe.Fori(0, NBLK) as k:
                node_block(3, k)

        @block.scalar
        def _(act):
            act.wait_ge(loaded, 16 * N_LOADS)
            act.wait_ge(setup_copied, 1)

            def copy(dst, src):
                return nc.scalar.activation(dst, src, ACT.Copy)

            def node_block(l, k):
                n = blocks((l,), l, k)
                xk = xn[:, bass.ds(k * Q, Q), :]
                if l == -1:
                    act.wait_ge(new_turned, k)
                    copy(rowsof(new), xk).then_inc(x_in, 1)
                else:
                    act.wait_ge(new_ready, blocks(MID, l, k))
                    if l < 3:
                        copy(hst[:, :], hacc[:, bass.ds(k * BLK, BLK)])
                    copy(rowsof(old), xk).then_inc(x_in, 1)
                if l in SOME:
                    act.wait_ge(old_turned, blocks(SOME, l, k) + 1)
                    copy(xt, pn_t).then_inc(old_copied, 1)
                if l == 0:
                    act.wait_ge(agg_out, n + 1)
                    copy(f3, pn_a).then_inc(agg_copied, 1)
                    act.wait_ge(hid_out, n + 1)
                    nc.scalar.activation(f4, pn_b, ACT.Relu, bias=col("L0_gnn_c1")).then_inc(hid_ready, 1)
                if l == 1:
                    act.wait_ge(self_diff, n + 1)
                    nc.scalar.activation(share[:, 4 * BLK:6 * BLK], share[:, 4 * BLK:6 * BLK],
                                         ACT.Exp).then_inc(self_exp, 1)
                if l == 3:
                    act.wait_ge(bn_ready, 1)
                    act.wait_ge(feat_turned, blocks(MID, l, k))
                    nc.scalar.activation(feat, acc[:, bass.ds(k * BLK, BLK)], ACT.Relu,
                                         bias=bnsc[:, 1:2], scale=bnsc[:, 0:1]).then_inc(feat_ready, 1)
                if l < 3:
                    act.wait_ge(new_turned, blocks(MORE, l, k) + 1)
                    copy(xt, pn_t).then_inc(new_copied, 1)
                    if l >= 0:
                        copy(xk, rowsof(new)).then_inc(new_kept, 1)
                    act.wait_ge(tab_out, blocks(MORE, l, k) + 1)
                    act.wait_ge(stored, 32 * blocks(MORE, l, k))
                    cw = (w1 if l == -1 else wext[l + 1]).shape[1]
                    copy(tab[:, :, 0:cw], pn_tab[:, :, 0:cw]).then_inc(tab_ready, 1)

            def copy_membership(l, i, b):
                act.wait_ge(memb_turned, chunks(l, i, b) + 1)
                if l == 0:
                    act.wait_ge(pre_ready[GR - 1][b], i)
                    for t in range(K):
                        q = t % 4
                        last = copy(lhs[ED:ED + WIN, b, t * P:(t + 1) * P],
                                    ps_mT[q * WIN:(q + 1) * WIN, (t // 4) * P:(t // 4 + 1) * P])
                    last.then_inc(memb_copied, 1)
                    return
                act.wait_ge(dst_ready[1 - b], guses(l, i) + b)
                full = (K // 4) * P
                copy(membT[:, 0:full], ps_mT[:, 0:full])
                n = tiles_of(GR - 1) * WIN
                copy(membT[0:n, full:full + P], ps_mT[0:n, full:full + P]).then_inc(memb_copied, 1)

            def edge_mlp(l, i, b):
                c = chunks(l, i, b)
                copy_membership(l, i, b)
                for g in range(GR):
                    act.wait_ge(pre_added[g], c + 1)
                    m = msg[:, b, 4 * g:4 * g + tiles_of(g), :]
                    nc.scalar.activation(m, m, ACT.Relu).then_inc(hidden[b], 1)

            def edge_attention(l, i, b):
                g_ = gchunks(l, i, b)
                H = HEADS[l]
                JH = K * H
                act.wait_ge(gathered[l][b], 16 * K * (i + 1))
                act.wait_ge(diff_ready, g_)
                copy(sflat[:, 0:JH].rearrange("p (h k) -> p h k", h=H),
                     G[:, b, :, P:P + H].rearrange("p k h -> p h k")).then_inc(sc_copied, 1)
                copy_membership(l, i, b)
                act.wait_ge(diff_ready, g_ + 1)
                act.wait_ge(fac_spread, g_)
                nc.scalar.activation(prow[0:1, 0:JH], diff[0:1, 1, 0:JH], ACT.Exp).then_inc(factor_ready, 1)
                act.wait_ge(summed[b], uses(l, i))
                nc.scalar.activation(prob[:, b, 0:JH], diff[:, 0, 0:JH], ACT.Exp).then_inc(prob_ready, 1)

            for l in range(LAYERS):
                act.wait_ge(added[1], K * uses(l, 0))
                act.wait_ge(weighed[1], K * uses(l, 0))
                with act.Fori(0, NBLK) as k:
                    node_block(l - 1, k)
                with act.Fori(0, PAIRS) as i:
                    for b in range(2):
                        (edge_mlp if l == 0 else edge_attention)(l, i, b)
            act.wait_ge(added[1], K * uses(LAYERS, 0))
            act.wait_ge(weighed[1], K * uses(LAYERS, 0))
            with act.Fori(0, NBLK) as k:
                act.wait_ge(bn_wide, k)
                copy(hst[:, :], hacc[:, bass.ds(k * BLK, BLK)]).then_inc(bn_in, 1)
            with act.Fori(0, NBLK) as k:
                node_block(3, k)

        @block.vector
        def _(dve):
            done = [0]

            def link(ins):
                done[0] += 1
                ins.then_inc(step, 1)
                dve.wait_ge(step, done[0])

            dve.wait_ge(loaded, 16 * N_LOADS)
            dve.wait_ge(built, N_BUILT)
            first = acc[0:1, 0:TILES]
            link(nc.vector.tensor_copy(first, base_i[0:1, :]))
            assert done[0] == STEP_FIRST
            nc.vector.tensor_copy(rel[:, :], base_i[:, :])
            for k, (h, name) in enumerate(((4, "L1_gnn_att_src"), (4, "L1_gnn_att_dst"), (4, "L2_gnn_attn_l"),
                                           (4, "L2_gnn_attn_r"), (8, "L3_gnn_att_src"), (8, "L3_gnn_att_dst"))):
                nc.vector.tensor_scalar(att[:, k, 0:h], head_of[h][:, :], col(name), None, ALU.mult)
            nc.vector.tensor_copy(row_head[4][:, :], row_head[8][:, 0:4])
            for h in (4, 8):
                nc.vector.tensor_reduce(row_tile[h][:, :],
                                        ident[:, 0:K * h].rearrange("p (h k) -> p k h", h=h), AX.X, ALU.add)
            nc.vector.tensor_tensor(skipb[:, :], col("L1_gnn_gat_bias"), col("L1_gnn_skip_b"), ALU.add)
            nc.vector.memset(brow[:, :, :], 0.0)
            nc.vector.tensor_copy(wtab[0:ED, :, :].rearrange("p b (k n) -> p (b k) n", k=K),
                                  w1e[:, :].unsqueeze(1).to_broadcast([ED, 2 * K, P]))
            nc.vector.memset(late4[:, 0:4], 0.0)
            nc.vector.tensor_copy(late4[:, 4:8], head_of[4][:, :])
            for h in (4, 8):
                nc.vector.tensor_copy(masks[h][:, 0, :], head_of[h][:, :])
                nc.vector.tensor_copy(masks[h][:, 1, :], ident[:, 0:h])
            link(nc.vector.memset(hacc[:, :], 0.0))
            dve.wait_ge(setup_pe, 1)
            nc.vector.tensor_copy(wT[:, :, :].rearrange("p a n -> p (a n)"), ps_t)
            nc.vector.tensor_copy(bc[:, :, :].rearrange("p a n -> p (a n)"), ps_mT)
            link(nc.vector.tensor_tensor(rel[:, :].rearrange("p (a n) -> p a n", a=PIECES),
                                         rel[:, :].rearrange("p (a n) -> p a n", a=PIECES),
                                         ps[:, 0:PIECES, 0:PIECE], ALU.subtract))
            assert done[0] == STEP_ATT
            t_int = msg[0:CH, 0, :, :].rearrange("p k n -> p (k n)").bitcast(i32)
            t_flt = G[0:CH, :, :, :].rearrange("p b k n -> p (b k n)")[:, 0:K * P]
            brk_all = msg[0:CH, 1, :, :].rearrange("p k n -> p (k n)")
            link(nc.vector.tensor_copy(t_flt, t_int))
            link(nc.vector.tensor_tensor(brk_all[:, 1:K * P], t_flt[:, 1:K * P], t_flt[:, 0:K * P - 1], ALU.not_equal))
            link(nc.vector.tensor_scalar(brk_all[:, 1:K * P], brk_all[:, 1:K * P], -BIG, None, ALU.mult))
            link(nc.vector.memset(msg[0:CH, 1, :, 0:1], -BIG))
            last_i = share[0:1, 0:TILES].bitcast(i32)
            last = share[0:1, TILES:2 * TILES]
            single = share[0:1, 2 * TILES:3 * TILES]
            cont = share[0:1, 3 * TILES:4 * TILES]
            link(nc.vector.tensor_copy(last, last_i))
            nc.vector.memset(cont[:, 0:1], 0.0)
            nc.vector.tensor_tensor(single, first, last, ALU.is_equal)
            link(nc.vector.tensor_tensor(cont[:, 1:TILES], first[:, 1:TILES], last[:, 0:TILES - 1], ALU.is_equal))
            link(nc.vector.tensor_tensor(single, single, cont, ALU.mult))
            link(nc.vector.tensor_scalar(single, single, 1.0, BIG, ALU.subtract, ALU.mult))
            link(nc.vector.tensor_scalar(cont, cont, 1.0, BIG, ALU.subtract, ALU.mult))
            link(nc.vector.memset(notfirst[:, :], 0.0))
            assert done[0] == STEP_TABLES, done
            link(nc.vector.memset(acc[:, :], 0.0))
            dve.wait_ge(setup_pe, 2)
            for l, k in ((1, 0), (2, 2), (3, 4)):
                H = HEADS[l]
                nc.vector.tensor_copy(wext[l][:, P:P + 2 * H].rearrange("p (a h) -> p a h", a=2),
                                      ps_e[:, k * HM:(k + 2) * HM].rearrange("p (a h) -> p a h", a=2)[:, :, 0:H])
            nc.vector.tensor_copy(wexp[:, :, :].rearrange("p a (h c) -> p a h c", h=4),
                                  ps_e[:, 0:2 * HM].rearrange("p (a h) -> p a h", a=2)[:, :, 0:4]
                                  .unsqueeze(3).to_broadcast([P, 2, 4, P // 4]))
            for k, h in enumerate((4, 8, 8)):
                nc.vector.tensor_copy(spread[0:h, k, :], ps[0:h, 6, k * P:(k + 1) * P])
            nc.vector.tensor_copy(brow[0:1, 0, P:2 * P], rowv[0:1, RW["L0_gnn_b1"], :])
            nc.vector.tensor_copy(brow[0:1, 1, 0:P], rowv[0:1, RW["L2_gnn_b_val"], :])
            dve.wait_ge(tables_in, 48)
            nc.vector.tensor_copy(brow[0:1, 1, P:P + 8], ps_e[0:1, 64:72]).then_inc(setup_copied, 1)

            count = [0]

            def node_loop(l, steps, body):
                start = count[0]
                with dve.Fori(0, NBLK) as k:
                    count[0] = start + steps * k
                    made = [0]

                    def then(ins):
                        made[0] += 1
                        ins.then_inc(nvec, 1)
                        dve.wait_ge(nvec, start + steps * k + made[0])

                    body(l, k, then)
                    assert made[0] == steps, (l, made)
                count[0] = start + steps * NBLK

            norms = [0]

            def stretch(a):
                return a.unsqueeze(2).to_broadcast([P, Q, P])

            def layer_norm(then, src, dst):
                for q in range(Q):
                    o = nc.vector.bn_stats(stats[:, q, :], src[:, q, :])
                then(o)
                dve.wait_ge(norm_paced, norms[0])
                nc.vector.tensor_copy(paced[0:1, 0:1], minus_half[0:1, 0:1]).then_inc(norm_paced, 1)
                for q in range(Q):
                    o = nc.vector.bn_aggr(mv[:, q, :], stats[:, q, :])
                then(o)
                nc.vector.tensor_scalar(varn[:, :], mv[:, :, 1], EPS_LN, None, ALU.add).then_inc(var_ready, 1)
                norms[0] = norms[0] + 1
                then(nc.vector.tensor_tensor(dst, src, stretch(mv[:, :, 0]), ALU.subtract))
                dve.wait_ge(rstd_ready, norms[0])
                return nc.vector.tensor_tensor(dst, dst, stretch(rstd[:, :]), ALU.mult)

            def node_block(l, k, then):
                tt, ts, stt = nc.vector.tensor_tensor, nc.vector.tensor_scalar, nc.vector.scalar_tensor_tensor
                norms[0] = norms_before(l, k)
                d = bass.ds(k * BLK, BLK)
                a_sum, a_wgt, a_max = acc[:, d], pn_n, pn_max
                n = blocks((l,), l, k)
                m = blocks(MID, l, k)
                if l < 3:
                    dve.wait_ge(wide_out, blocks((0, 1, 2), l, k) + 1)
                if l == 0:
                    then(ts(f5, a_wgt, 1.0, None, ALU.max))
                    then(nc.vector.reciprocal(f5, f5))
                    dve.wait_ge(agg_out, n)
                    then(tt(f1, a_sum, f5, ALU.mult))
                    ts(f2[0:1, :], a_wgt[0:1, :], 1.0, None, ALU.min).then_inc(agg_in, 1)
                    dve.wait_ge(upd_out, n + 1)
                    dve.wait_ge(feat_turned, m)
                    stt(feat, pn_c, col("L0_gnn_c2"), xt, ALU.add, ALU.add).then_inc(feat_ready, 1)
                if l == 1:
                    then(ts(f1, a_wgt, 0.0, -BIG, ALU.is_equal, ALU.mult))
                    then(tt(f1, f1, a_max, ALU.add))
                    dve.wait_ge(self_out, n + 1)
                    tt(f2, f1, pn_c, ALU.max)
                    then(nc.vector.tensor_copy(f3, pn_c))
                    tt(f1, f1, pn_d, ALU.add)
                    tt(f2, f2, pn_d, ALU.add)
                    then(tt(f3, f3, pn_d, ALU.add))
                    f123 = share[:, BLK:4 * BLK]
                    then(stt(f123, f123, SLOPE, f123, ALU.mult, ALU.max))
                    tt(f4, f1, f2, ALU.subtract)
                    tt(f5, f3, f2, ALU.subtract).then_inc(self_diff, 1)
                    dve.wait_ge(self_exp, n + 1)
                    tt(f1, a_sum, f4, ALU.mult)
                    tt(f2, pn_b, f5, ALU.mult)
                    then(tt(f3, a_wgt, f4, ALU.mult))
                    tt(f1, f1, f2, ALU.add)
                    then(stt(f3, f3, 1e-16, f5, ALU.add, ALU.add))
                    then(nc.vector.reciprocal(f3, f3))
                    then(tt(f1, f1, f3, ALU.mult))
                    dve.wait_ge(feat_turned, m)
                    stt(feat, pn_a, skipb[:, 0:1], f1, ALU.add, ALU.add).then_inc(feat_ready, 1)
                if l == 2:
                    then(ts(f1, a_wgt, 1e-30, None, ALU.max))
                    then(nc.vector.reciprocal(f1, f1))
                    dve.wait_ge(feat_turned, m)
                    tt(feat, a_sum, f1, ALU.mult).then_inc(feat_ready, 1)
                dve.wait_ge(feat_turned, m + 1)
                if l < 3:
                    ts(acc[:, d], acc[:, d], 0.0, None, ALU.mult)
                    ts(hacc[:, d], hacc[:, d], 0.0, None, ALU.mult)
                src, t3 = rowsof(pn_n), rowsof(tmp)
                dve.wait_ge(x_in, blocks(ALL, l, k) + 1)
                if l in SOME:
                    then(layer_norm(then, src, t3))
                    g, b_ = (bc[:, 2 * l + j, :].unsqueeze(1).to_broadcast([P, Q, P]) for j in range(2))
                    then(tt(t3, t3, g, ALU.mult))
                    then(tt(t3, t3, b_, ALU.add))
                    then(tt(t3, t3, rowsof(old), ALU.add))
                else:
                    then(tt(t3, src, rowsof(old), ALU.add))
                    if l == 3:
                        then(tt(t3, t3, rowsof(old), ALU.add))
                if l < 3:
                    dve.wait_ge(new_turned, blocks(MORE, l, k))
                    dve.wait_ge(new_kept, m)
                else:
                    dve.wait_ge(final, 16 * k)
                layer_norm(then, t3, rowsof(new)).then_inc(new_ready, 1)

            def batch_sums(l, k, then):
                d = bass.ds(k * BLK, BLK)
                dve.wait_ge(bn_wide, k + 1)
                then(nc.vector.tensor_scalar(f1, pn_n, 1e-16, 1e-30, ALU.add, ALU.max))
                then(nc.vector.reciprocal(f1, f1))
                then(nc.vector.tensor_tensor(f1, acc[:, d], f1, ALU.mult))
                then(nc.vector.tensor_scalar(acc[:, d], f1, col("L3_gnn_bias"), None, ALU.add))
                nc.vector.bn_stats(bnst[:, bass.ds(k, 1), :].rearrange("p o s -> p (o s)"),
                                   acc[:, d]).then_inc(bn_done, 1)

            def make_membership(l, i, b):
                dve.wait_ge(summed[b], uses(l, i))
                r = rel[:, bass.ds((2 * i + b) * K, K)].unsqueeze(2).to_broadcast([P, K, WIN])
                w = win_iota[:, :].unsqueeze(1).to_broadcast([P, K, WIN])
                nc.vector.tensor_tensor(memb[:, b, :].rearrange("p (k w) -> p k w", k=K), r, w,
                                        ALU.is_equal).then_inc(memb_ready, 1)

            def edge_mlp(l, i, b, prev):
                c = chunks(l, i, b)
                make_membership(l, i, b)
                if prev:
                    add_sums(l, *prev, first_nodes(*prev), 0, K)
                dve.wait_ge(gathered[l][b], 16 * K * (i + 1))
                for g in range(GR):
                    n = tiles_of(g)
                    dve.wait_ge(pre_ready[g][b], i + 1)
                    nc.vector.tensor_tensor(msg[:, b, 4 * g:4 * g + n, :], G[:, b, 4 * g:4 * g + n, 0:P],
                                            ps_pre[g][:, 0:n * P].rearrange("p (k f) -> p k f", k=n),
                                            ALU.add).then_inc(pre_added[g], 1)

            def edge_attention(l, i, b, prev):
                g_ = gchunks(l, i, b)
                H = HEADS[l]
                JH = K * H
                tt, ts, stt = nc.vector.tensor_tensor, nc.vector.tensor_scalar, nc.vector.scalar_tensor_tensor
                v0 = VEC * g_
                tiles = bass.ds((2 * i + b) * K, K)
                make_membership(l, i, b)
                ts(notfirst[:, :], rel[:, tiles], 0.0, -BIG, ALU.not_equal, ALU.mult).then_inc(vec, 1)
                if prev:
                    first = first_nodes(*prev)
                    add_sums(l, *prev, first, 0, 6)
                dve.wait_ge(brk_loaded[b], 16 * sum((HEADS[m] + 1) * PAIRS for m in range(1, l))
                            + 16 * (H + 1) * (i + 1))
                dve.wait_ge(sc_turned, g_ + 1)
                dve.wait_ge(seg_turned, g_)
                nc.vector.tensor_tensor_scan(segm[0:JH, :], brk[0:JH, b, :], ps_t[0:JH, 0:P], -BIG,
                                             ALU.add, ALU.max).then_inc(seg_fwd, 1)
                dve.wait_ge(seg_fwd, g_ + 1)
                dve.wait_ge(last_ready, g_)
                ts(lastm[0:JH, 0:H], row_head[H][0:JH, :], segm[0:JH, P - 1:P], None,
                   ALU.mult).then_inc(last_masked, 1)
                body = segm[0:JH, 0:P - 1][:, ::-1]
                nc.vector.tensor_tensor_scan(body, brk[0:JH, b, 1:P][:, ::-1], body, segm[0:JH, P - 1:P],
                                             ALU.add, ALU.max).then_inc(seg_all, 1)
                if prev:
                    add_sums(l, *prev, first, 6, 7)
                dve.wait_ge(last_ready, g_ + 1)
                dve.wait_ge(run_kept, g_ + l - 1)
                nc.vector.tensor_tensor_scan(runmax[0:H, 1:K + 1], join[0:H, b, 0, :], ps_last[0:H, :],
                                             runmax[0:H, 0:1], ALU.add, ALU.max).then_inc(run_ready, 1)
                dve.wait_ge(run_ready, g_ + 1)
                tt(carry[0:H, :], runmax[0:H, 0:K], join[0:H, b, 1, :], ALU.add).then_inc(carry_ready, 1)
                dve.wait_ge(carry_ready, g_ + 1)
                nc.vector.tensor_copy(runmax[0:H, 0:1], runmax[0:H, K:K + 1]).then_inc(run_kept, 1)
                dve.wait_ge(carry_spread, g_)
                tt(cdiag[0:H, 0:JH].rearrange("p (h k) -> p h k", h=H),
                   carry[0:H, :].unsqueeze(1).to_broadcast([H, H, K]),
                   ident[0:H, 0:H].unsqueeze(2).to_broadcast([H, H, K]), ALU.mult).then_inc(cdiag_ready, 1)

                def hk(a):
                    return a.rearrange("p (h k) -> p h k", h=H)

                if prev:
                    add_sums(l, *prev, first, 7, 9)
                s = [scores[:, c, 0:JH] for c in range(3)]
                dst = ps_e[:, O_DST:O_DST + JH].rearrange("p (k h) -> p h k", h=H)
                dve.wait_ge(carry_spread, g_ + 1)
                tt(hk(s[0]), hk(sflat[:, 0:JH]), dst, ALU.add).then_inc(vec, 1)
                dve.wait_ge(vec, v0 + 2)
                tt(hk(s[1]), hk(ps_e[:, O_CAR:O_CAR + JH]), notfirst[:, :].unsqueeze(1).to_broadcast([P, H, K]),
                   ALU.add).then_inc(vec, 1)
                dve.wait_ge(vec, v0 + 3)
                tt(s[2], s[1], ps_e[:, O_SEG:O_SEG + JH], ALU.max).then_inc(vec, 1)
                dve.wait_ge(vec, v0 + 4)
                if l == 1:
                    dve.wait_ge(brkT_ready, 2 * i + b + 1)
                    stt(prob[:, b, JH:2 * JH], ps_brk[:, 0:JH], -1.0 / BIG, s[2], ALU.mult, ALU.mult).then_inc(maxf_ready, 1)
                    dve.wait_ge(maxf_ready, 2 * i + b + 1)
                s12 = scores[:, 1:3, 0:JH].rearrange("p a (h k) -> p a h k", h=H)
                tt(s12, s12, dst.unsqueeze(1).to_broadcast([P, 2, H, K]), ALU.add).then_inc(vec, 1)
                dve.wait_ge(vec, v0 + 5)
                sall = scores[:, :, 0:JH]
                stt(sall, sall, SLOPE, sall, ALU.mult, ALU.max).then_inc(vec, 1)
                dve.wait_ge(vec, v0 + 6)
                dve.wait_ge(prob_ready, g_)
                tt(diff[:, :, 0:JH], scores[:, 0:2, 0:JH],
                   scores[:, 2:3, 0:JH].to_broadcast([P, 2, JH]), ALU.subtract).then_inc(diff_ready, 1)

                if prev:
                    add_sums(l, *prev, first, 9, K)
                dve.wait_ge(prob_ready, g_ + 1)
                nc.vector.tensor_tensor(msg[:, b, :, :].rearrange("p k (h c) -> p k h c", h=H),
                                        G[:, b, :, 0:P].rearrange("p k (h c) -> p k h c", h=H),
                                        prob[:, b, 0:JH].rearrange("p (h k) -> p k h", h=H).unsqueeze(3)
                                        .to_broadcast([P, K, H, P // H]),
                                        ALU.mult).then_inc(messages[b], 1)

            def edge_factors(l, i, b):
                g_ = gchunks(l, i, b)
                H = HEADS[l]
                JH = K * H
                dve.wait_ge(fac_spread, g_ + 1)
                dve.wait_ge(fac_ready, g_)
                nc.vector.tensor_tensor(facm[:, :, 0:JH].rearrange("p a (h k) -> p a h k", h=H),
                                        ps_e[:, O_FAC:O_FAC + JH].rearrange("p (h k) -> p h k", h=H)
                                        .unsqueeze(1).to_broadcast([P, 2, H, K]),
                                        masks[H][:, :, :].unsqueeze(3).to_broadcast([P, 2, H, K]),
                                        ALU.mult).then_inc(fac_masked, 1)
                dve.wait_ge(fac_masked, g_ + 1)
                nc.vector.tensor_reduce(fac[:, b, :, :], facm[:, :, 0:JH].rearrange("p a (h k) -> p a k h", h=H),
                                        AX.X, ALU.add).then_inc(fac_ready, 1)

            def first_nodes(i, b):
                return nc.values_load_multi_w_load_instructions(
                    base_i[0:1, bass.ds((2 * i + b) * K, K)], engines=(dve.engine,), min_val=0, max_val=N,
                    skip_runtime_bounds_check_because="targets are node numbers")[1]

            def add_sums(l, i, b, first, t0, t1):
                if t0 == 0:
                    dve.wait_ge(summed[b], uses(l, i) + 1)
                    if l:
                        dve.wait_ge(fac_ready, gchunks(l, i, b) + 1)
                R = ROWS[l]
                for t in range(t0, t1):
                    def after(done):
                        if t:
                            dve.wait_ge(done[b], K * uses(l, i) + t)
                        else:
                            dve.wait_ge(done[1 - b], K * (uses(l, i) + b))

                    w = slice(t * WIN, (t + 1) * WIN)
                    d = bass.ds(first[t], WIN)
                    node, wgt = acc[:, d], hacc[0:R, d]
                    after(added)
                    if l == 0:
                        nc.vector.tensor_tensor(node, node, ps_msg[b][:, w], ALU.add).then_inc(added[b], 1)
                    else:
                        nc.vector.scalar_tensor_tensor(node, node, fac[:, b, 0, t:t + 1], ps_msg[b][:, w],
                                                       ALU.mult, ALU.add).then_inc(added[b], 1)
                    after(weighed)
                    if l == 0:
                        nc.vector.tensor_tensor(wgt, wgt, ps_wgt[b][0:R, w], ALU.add).then_inc(weighed[b], 1)
                    else:
                        nc.vector.scalar_tensor_tensor(wgt, wgt, fac[0:R, b, 1, t:t + 1], ps_wgt[b][0:R, w],
                                                       ALU.mult, ALU.add).then_inc(weighed[b], 1)

            def front(l, i, b, prev):
                (edge_attention if l else edge_mlp)(l, i, b, prev)

            def factors(l, i, b):
                if l:
                    edge_factors(l, i, b)

            STEPS = {0: 13, 1: 19, 2: 6, 3: 5}
            for l in range(LAYERS):
                if l in (1, 3):
                    nc.vector.memset(wtab[:, :, :], 0.0).then_inc(wtab_clear, 1)
                if l:
                    node_loop(l - 1, STEPS[l - 1], node_block)
                    nc.vector.memset(runmax[:, :], -BIG).then_inc(run_kept, 1)
                front(l, 0, 0, None)
                factors(l, 0, 0)
                front(l, 0, 1, None)
                with dve.Fori(0, PAIRS - 1) as i:
                    factors(l, i, 1)
                    front(l, i + 1, 0, (i, 0))
                    factors(l, i + 1, 0)
                    front(l, i + 1, 1, (i, 1))
                factors(l, PAIRS - 1, 1)
                for b in range(2):
                    add_sums(l, PAIRS - 1, b, first_nodes(PAIRS - 1, b), 0, K)
            node_loop(3, 4, batch_sums)
            dve.wait_ge(bn_done, NBLK)
            start = count[0]
            left = N - (NBLK - 1) * BLK
            nth = [start]

            def then(ins):
                nth[0] += 1
                ins.then_inc(nvec, 1)
                dve.wait_ge(nvec, nth[0])

            then(nc.vector.bn_stats(bnst[:, NBLK - 1, :], acc[:, (NBLK - 1) * BLK:N]))
            then(nc.vector.bn_aggr(bnmv[:, :], bnst[:, :, :].rearrange("p k s -> p (k s)")))
            nc.vector.tensor_scalar(bnsc[:, 0:1], bnmv[:, 1:2], EPS_LN, None, ALU.add).then_inc(bn_var, 1)
            dve.wait_ge(bn_rstd, 1)
            then(nc.vector.tensor_tensor(bnsc[:, 0:1], bnsc[:, 0:1], col("L3_gnn_gamma"), ALU.mult))
            then(nc.vector.tensor_tensor(bnsc[:, 2:3], bnmv[:, 0:1], bnsc[:, 0:1], ALU.mult))
            nc.vector.tensor_tensor(bnsc[:, 1:2], col("L3_gnn_beta"), bnsc[:, 2:3], ALU.subtract).then_inc(bn_ready, 1)
            count[0] = nth[0]
            node_loop(3, STEPS[3], node_block)


def _lay(a, pad, value):
    import numpy as np
    return np.pad(a, [(0, pad)] + [(0, 0)] * (a.ndim - 1), constant_values=value)


def kernel(**inputs):
    import numpy as np
    import concourse.bacc as bacc
    from concourse.bass_utils import run_bass_kernel_spmd

    P, K = 128, 13
    a = {k: np.ascontiguousarray(v) for k, v in inputs.items()}
    n = a["x"].shape[0]
    edges = a["src"].shape[0]
    chunks = -(-edges // (P * K))
    pad = chunks * P * K - edges
    arrays = {}
    for name, v in a.items():
        if name.startswith("L1_gnn_att_") or name.startswith("L2_gnn_attn") or name.startswith("L3_gnn_att_"):
            v = v.reshape(-1)
        arrays[name] = v
    arrays["x"] = _lay(a["x"], -n % 512, 0)
    arrays["src"] = np.ascontiguousarray(_lay(a["src"], pad, 0).reshape(chunks, K, P).transpose(0, 2, 1))
    dst = _lay(a["dst"], pad, n)
    del arrays["dst"]
    arrays["dst_cols"] = np.ascontiguousarray(dst.reshape(chunks * K, P).T)
    arrays["dst_rows"] = np.ascontiguousarray(dst.reshape(chunks, K * P))
    arrays["edge_attr_64"] = np.ascontiguousarray(_lay(a["edge_attr_64"], pad, 0).T)

    nc = bacc.Bacc("TRN2", target_bir_lowering=False, num_devices=1, dynamic_dma_scratch_size=8192)
    aps, fed = {}, {}
    for name, v in arrays.items():
        aps[name] = nc.dram_tensor(f"in_{name}", v.shape, mybir.dt.from_np(v.dtype), kind="ExternalInput").ap()
        fed[f"in_{name}"] = v
    out = nc.dram_tensor("out", (n, P), mybir.dt.float32, kind="ExternalOutput").ap()
    gnn_program(nc, aps, out)
    r = run_bass_kernel_spmd(nc, [fed], core_ids=[0])
    return r.results[0]["out"]
```

```python
import concourse.bass as bass
from concourse import mybir
from contextlib import ExitStack


def gnn_program(nc, A, out):
    fp32 = mybir.dt.float32
    i32 = mybir.dt.int32
    ALU = mybir.AluOpType
    ACT = mybir.ActivationFunctionType
    AX = mybir.AxisListType

    P = 128
    N = out.shape[0]
    E = A["edge_attr_64"].shape[1]
    ED = A["edge_attr_64"].shape[0]
    K = A["src"].shape[2]
    CH = A["src"].shape[0]
    TILES = K * CH
    PAIRS = CH // 2
    PIECES = 4
    PIECE = TILES // PIECES
    WIN = 32
    BLK = 512
    NP = A["x"].shape[0]
    NBLK = NP // BLK
    Q = BLK // P
    GR = -(-K // 4)
    LAYERS = 4
    HEADS = [1, 4, 4, 8]
    HM = max(HEADS)
    BIG = float(2 ** 100)
    SLOPE = 0.2
    EPS_LN = 1e-5
    ROW = P + HM

    def tiles_of(g):
        return min(4, K - 4 * g)

    ctx = ExitStack()
    with ctx:
        def sb(name, shape, dt=fp32):
            return ctx.enter_context(nc.sbuf_tensor(name, shape, dt))

        counters = []

        def sem(name, counter=True):
            s = ctx.enter_context(nc.semaphore(name))
            if counter:
                counters.append(s)
            return s

        def pair(name):
            return [sem(f"{name}{b}") for b in range(2)]

        def dram(name, shape, dt=fp32):
            return nc.dram_tensor(name, shape, dt, kind="Internal").ap()

        width = [P] + [P + h for h in HEADS[1:]]
        rows = [dram(f"rows{l}", (NP, width[l])) for l in range(LAYERS)]
        wins = [dram(f"wins{l}", (NP, P if l == 0 else HEADS[l])) for l in range(LAYERS)]
        breaks = dram("breaks", (TILES, P))
        joins = dram("joins", (2, TILES))

        acc = sb("acc", [P, NP])
        hacc = sb("hacc", [HM, NP])
        xn = sb("xn", [P, NP // P, P])
        base_i = sb("base_i", [P, TILES], i32)
        rel = sb("rel", [P, TILES])
        ident = sb("ident", [P, P])
        spread = sb("spread", [HM, 3, P])
        masks = {4: sb("masks4", [P, 2, 4]), 8: sb("masks8", [P, 2, 8])}
        ones = sb("ones", [P, P])
        win_iota = sb("win_iota", [P, WIN])
        head_of = {4: sb("head4", [P, 4]), 8: sb("head8", [P, 8])}
        late4 = sb("late4", [P, 8])
        row_head = {h: sb(f"row_head{h}", [P, h]) for h in (4, 8)}
        row_tile = {h: sb(f"row_tile{h}", [P, K]) for h in (4, 8)}

        G = sb("G", [P, 2, K, ROW])
        idx = sb("idx", [P, 2, K], i32)
        msg = sb("msg", [P, 2, K, P])
        prob = sb("prob", [P, 2, K * HM])
        memb = sb("memb", [P, 2, K * WIN])
        membT = sb("membT", [P, GR * P])
        brk = sb("brk", [P, 2, P])
        join = sb("join", [HM, 2, 2, K])
        wtab = sb("wtab", [P, 2, K * P])
        sflat = sb("sflat", [P, P])
        segm = sb("segm", [P, P])
        lastm = sb("lastm", [P, HM])
        runmax = sb("runmax", [HM, K + 1])
        carry = sb("carry", [HM, K])
        cdiag = sb("cdiag", [HM, HM * K])
        notfirst = sb("notfirst", [P, K])
        scores = sb("scores", [P, 3, K * HM])
        diff = sb("diff", [P, 2, K * HM])
        prow = sb("prow", [1, K * HM])
        facm = sb("facm", [P, 2, K * HM])
        fac = sb("fac", [P, 2, 2, K])

        share = sb("share", [P, max(12 * BLK, 4 * TILES)])
        lhs = share[0:ED + WIN, 0:2 * K * P].rearrange("p (b n) -> p b n", b=2)
        xt, f1, f2, f3, f4, f5, feat, old, tmp, new = (share[:, k * BLK:(k + 1) * BLK] for k in range(10))
        tab = share[:, 10 * BLK:12 * BLK].rearrange("p (q n) -> p q n", q=Q)

        def rowsof(a):
            return a.rearrange("p (q f) -> p q f", q=Q)

        hst = sb("hst", [HM, BLK])
        minus_half = sb("minus_half", [P, Q])
        varn = sb("varn", [P, Q])
        stats = sb("stats", [P, Q, 6])
        mv = sb("mv", [P, Q, 2])
        rstd = sb("rstd", [P, Q])
        bnst = sb("bnst", [P, NBLK, 6])
        bnmv = sb("bnmv", [P, 2])
        bnsc = sb("bnsc", [P, 3])

        w1 = sb("w1", [P, 2 * P])
        w1e = sb("w1e", [ED, P])
        w2 = sb("w2", [P, P])
        u1 = sb("u1", [P, 2, P])
        u2 = sb("u2", [P, P])
        wsk = sb("wsk", [P, P])
        wext = [None] + [sb(f"wext{l}", [P, P + 2 * HEADS[l]]) for l in (1, 2, 3)]
        wside = sb("wside", [P, 2, P])
        wexp = sb("wexp", [P, 2, P])
        wT = sb("wT", [P, 4, P])
        att = sb("att", [P, 6, HM])
        rowv = sb("rowv", [1, 7, P])
        brow = sb("brow", [1, 2, 2 * P])
        bc = sb("bc", [P, 4, P])
        COL = {n: k for k, n in enumerate(
            ["L0_gnn_c1", "L0_gnn_c2", "L1_gnn_gat_bias", "L1_gnn_skip_b", "L3_gnn_bias", "L3_gnn_gamma",
             "L3_gnn_beta", "L1_gnn_att_src", "L1_gnn_att_dst", "L2_gnn_attn_l", "L2_gnn_attn_r",
             "L3_gnn_att_src", "L3_gnn_att_dst", "L2_gnn_b_src", "L2_gnn_b_dst"])}
        RW = {n: k for k, n in enumerate(
            ["L0_gnn_gamma", "L0_gnn_beta", "L1_gnn_ln_g", "L1_gnn_ln_b", "L0_gnn_b1", "L0_gnn_b2", "L2_gnn_b_val"])}
        cols = sb("cols", [P, len(COL)])
        skipb = sb("skipb", [P, 1])

        def col(name):
            return cols[:, COL[name]:COL[name] + 1]

        ps = ctx.enter_context(nc.psum_tensor("ps", [P, 8, BLK], fp32))
        ps_msg, ps_wgt = [ps[:, 0, :], ps[:, 2, :]], [ps[:, 1, :], ps[:, 3, :]]
        ps_mT, ps_e, ps_t, ps_brk = (ps[:, k, :] for k in (4, 5, 6, 7))
        ps_pre = [ps[:, 5 + g % 3, :] for g in range(GR)]
        O_DST, O_CAR, O_FAC, O_SEG = (k * K * HM for k in range(4))
        ps_last = ps[:, 6, 2 * P:2 * P + K]
        pn_tab = ps[:, 0:2, :].rearrange("p a n -> p (a n)").rearrange("p (q n) -> p q n", q=Q)
        pn_max = ps[:, 0, :]
        pn_a, pn_b, pn_c, pn_d, pn_n, pn_t = (ps[:, k, :] for k in range(2, 8))

        loaded = sem("inputs_loaded", counter=False)
        built = sem("constants_built", counter=False)
        norm_paced, gather_paced = (sem(f"{w}_paced", counter=False) for w in ("norm", "gather"))
        step = sem("vector_setup_step", counter=False)
        setup_pe = sem("setup_products_ready", counter=False)
        setup_copied = sem("setup_products_copied", counter=False)
        tables_in = sem("edge_tables_stored", counter=False)
        gathered = [[sem(f"gathered_l{l}_{b}", counter=False) for b in range(2)] for l in range(LAYERS)]
        win_loaded = [pair(f"windows_loaded_l{l}_") for l in range(LAYERS)]
        idx_loaded = pair("indices_loaded")
        ef_loaded = pair("edge_features_loaded")
        brk_loaded = pair("breaks_loaded")
        messages = pair("messages_ready")
        memb_ready, memb_turned, memb_copied = (sem(f"membership_{w}") for w in ("ready", "turned", "copied"))
        summed = pair("window_sums_ready")
        added = pair("window_sums_added")
        weighed = pair("window_weights_added")
        wtab_clear = sem("window_blocks_cleared")
        pre_ready = [pair(f"preactivation{g}_ready") for g in range(GR)]
        pre_added = [sem(f"preactivation{g}_added") for g in range(GR)]
        hidden = pair("hidden_ready")
        sc_copied, sc_turned = sem("scores_copied"), sem("scores_turned")
        seg_fwd, seg_all, seg_turned = (sem(f"segment_maxima_{w}") for w in ("scanned_forward", "ready", "turned"))
        last_masked, last_ready = sem("last_maxima_masked"), sem("last_maxima_ready")
        run_ready, carry_ready, run_kept = sem("running_maxima_ready"), sem("carry_ready"), sem("running_maximum_kept")
        cdiag_ready, carry_spread = sem("carry_diagonal_ready"), sem("carry_spread")
        dst_ready = pair("target_scores_ready")
        vec = sem("vector_score_step")
        diff_ready = sem("score_differences_ready")
        factor_ready, prob_ready = sem("carry_factors_ready"), sem("weights_ready")
        fac_spread, fac_masked, fac_ready = (sem(f"carry_factors_{w}") for w in ("spread", "masked", "by_feature"))
        brkT_ready, maxf_ready = sem("first_flags_turned"), sem("first_maxima_ready")
        nvec = sem("node_vector_step", counter=False)
        x_in = sem("node_rows_copied")
        old_turned, old_copied = sem("old_features_turned"), sem("old_features_copied")
        agg_in, agg_out, agg_copied = (sem(f"aggregate_{w}") for w in ("ready", "multiplied", "copied"))
        hid_out, hid_ready, upd_out = sem("update_hidden_multiplied"), sem("update_hidden_ready"), sem("update_multiplied")
        self_out, self_diff, self_exp = (sem(f"self_loop_{w}") for w in ("products_ready", "differences_ready", "weights_ready"))
        var_ready, rstd_ready = sem("variances_ready"), sem("inverse_deviations_ready")
        wide_out = sem("head_sums_spread")
        bn_in, bn_wide, bn_done = sem("batch_head_sums_copied"), sem("batch_head_sums_spread"), sem("batch_block_ready")
        bn_var, bn_rstd = sem("batch_variance_ready"), sem("batch_inverse_deviation_ready")
        bn_ready = sem("batch_statistics_ready")
        feat_ready, feat_turned = sem("layer_output_ready"), sem("layer_output_turned")
        new_ready, new_kept = sem("new_features_ready"), sem("new_features_kept")
        new_turned, new_copied = sem("new_features_turned"), sem("new_features_copied")
        tab_out, tab_ready, stored = sem("table_rows_multiplied"), sem("table_rows_ready"), sem("table_rows_stored")
        final = sem("output_stored")

        block = ctx.enter_context(nc.Block())

        N_LOADS = 17 + len(COL) + len(RW)
        N_BUILT = 10
        STEP_FIRST, STEP_ATT, STEP_TABLES = 1, 3, 13
        VEC = 6

        ROWS = [1, 8, 4, 8]

        def chunks(l, i, b):
            return l * CH + 2 * i + b

        def gchunks(l, i, b):
            return (l - 1) * CH + 2 * i + b

        def is_last(i, b):
            return isinstance(i, int) and i == PAIRS - 1 and b == 1

        def uses(l, i):
            return l * PAIRS + i

        def guses(l, i):
            return (l - 1) * PAIRS + i

        def blocks(layers, l, k):
            return NBLK * sum(m < l for m in layers) + k

        NORMS = {0: 2, 1: 2, 2: 1, 3: 1}

        def norms_before(l, k):
            return NBLK * sum(NORMS[m] for m in range(l)) + NORMS[l] * k

        ALL, SOME, MID, MORE = (-1, 0, 1, 2, 3), (0, 1), (0, 1, 2, 3), (-1, 0, 1, 2)

        @block.sync
        def _(sp):
            n_in = [0]

            def load(dst, src):
                sp.dma_start(dst, src).then_inc(loaded, 16)
                n_in[0] += 1

            load(base_i[:, :], A["dst_cols"])
            load(share[0:1, 0:TILES].bitcast(i32), A["dst_cols"][P - 1:P, :])
            load(msg[0:CH, 0, :, :].rearrange("p k n -> p (k n)").bitcast(i32), A["dst_rows"])
            load(w1[:, 0:P], A["L0_gnn_W1"][0:P, :])
            load(w1[:, P:2 * P], A["L0_gnn_W1"][P:2 * P, :])
            load(w1e[:, :], A["L0_gnn_W1"][2 * P:2 * P + ED, :])
            load(w2[:, :], A["L0_gnn_W2"])
            load(u1[:, 0, :], A["L0_gnn_U1"][0:P, :])
            load(u1[:, 1, :], A["L0_gnn_U1"][P:2 * P, :])
            load(u2[:, :], A["L0_gnn_U2"])
            load(wsk[:, :], A["L1_gnn_skip_W"])
            load(wext[1][:, 0:P], A["L1_gnn_W"])
            load(wext[2][:, 0:P], A["L2_gnn_W_val"])
            load(wside[:, 0, :], A["L2_gnn_W_src"])
            load(wside[:, 1, :], A["L2_gnn_W_dst"])
            load(wext[3][:, 0:P], A["L3_gnn_W"])
            for name, k in COL.items():
                load(cols[:, k:k + 1], A[name].rearrange("(p o) -> p o", o=1))
            for name, k in RW.items():
                load(rowv[0:1, k, :], A[name].rearrange("(o n) -> o n", o=1))
            load(xn[:, :, :], A["x"].rearrange("(t p) f -> p t f", p=P))
            assert n_in[0] == N_LOADS, n_in

            for counter in counters:
                sp.sem_inc(counter, 1)

            sp.wait_ge(step, STEP_TABLES)
            sp.dma_start(breaks.rearrange("(c k) n -> c (k n)", k=K),
                         msg[0:CH, 1, :, :].rearrange("p k n -> p (k n)")).then_inc(tables_in, 16)
            sp.dma_start(joins[0:1, :], share[0:1, 2 * TILES:3 * TILES]).then_inc(tables_in, 16)
            sp.dma_start(joins[1:2, :], share[0:1, 3 * TILES:4 * TILES]).then_inc(tables_in, 16)
            sp.wait_ge(tables_in, 48)

            def store_tables(l, k):
                sp.wait_ge(tab_ready, 1 + blocks(MORE, l, k) + 1)
                d = bass.ds(k * BLK, BLK)
                wr = width[l + 1]
                wt = wins[l + 1].shape[1]
                sp.dma_start(rows[l + 1][d, :].rearrange("(q p) c -> p q c", p=P),
                             tab[:, :, 0:wr]).then_inc(stored, 16)
                sp.dma_start(wins[l + 1][d, :].rearrange("(q p) c -> p q c", p=P),
                             tab[:, :, wr:wr + wt]).then_inc(stored, 16)

            def load_indices(l, i, b):
                sp.dma_start(idx[:, b, :], A["src"][bass.ds(2 * i + b, 1), :, :]
                             .rearrange("o p k -> p (o k)")).then_inc(idx_loaded[b], 16)

            def load_chunk(l, i, b):
                H = HEADS[l]
                t0 = (2 * i + b) * K
                if l == 0:
                    sp.wait_ge(pre_ready[GR - 1][b], 1 + i)
                    sp.dma_start(lhs[0:ED, b, :], A["edge_attr_64"][:, bass.ds(t0 * P, K * P)]).then_inc(
                        ef_loaded[b], 16)
                else:
                    sp.wait_ge(dst_ready[b], 1 + guses(l, i))
                    sp.wait_ge(messages[b], 1 + guses(l, i))
                    for h in range(H):
                        sp.dma_start(brk[h * K:(h + 1) * K, b, :],
                                     breaks[bass.ds(t0, K), :]).then_inc(brk_loaded[b], 16)
                    sp.dma_start(join[0:H, b, :, :], joins[:, bass.ds(t0, K)].unsqueeze(0)
                                 .to_broadcast([H, 2, K])).then_inc(brk_loaded[b], 16)
                _, first = nc.values_load_multi_w_load_instructions(
                    base_i[0:1, bass.ds(t0, K)], engines=(sp.engine,), min_val=0, max_val=N,
                    skip_runtime_bounds_check_because="targets are node numbers")
                for t in range(K):
                    g, q = t // 4, t % 4
                    if l == 0:
                        dst = wtab[ED:ED + WIN, b, t * P:(t + 1) * P]
                    else:
                        dst = wtab[WIN * q:WIN * (q + 1), b, g * BLK + q * H:g * BLK + (q + 1) * H]
                    sp.dma_start(dst, wins[l][bass.ds(first[t], WIN), :]).then_inc(win_loaded[l][b], 16)

            for l in range(LAYERS):
                with sp.Fori(0, NBLK) as k:
                    store_tables(l - 1, k)
                sp.wait_ge(stored, 1 + 32 * NBLK * (l + 1))
                if l in (1, 3):
                    sp.wait_ge(wtab_clear, 1 + (1 if l == 1 else 2))
                for b in range(2):
                    if l:
                        sp.wait_ge(gathered[l - 1][b], 16 * K * PAIRS)
                    load_indices(l, 0, b)
                with sp.Fori(0, PAIRS - 1) as i:
                    for b in range(2):
                        load_chunk(l, i, b)
                    for b in range(2):
                        sp.wait_ge(gathered[l][b], 16 * K * (i + 1))
                        load_indices(l, i + 1, b)
                for b in range(2):
                    load_chunk(l, PAIRS - 1, b)

            with sp.Fori(0, NBLK - 1) as k:
                sp.wait_ge(new_ready, 1 + blocks(MID, 3, k) + 1)
                sp.dma_start(out[bass.ds(k * BLK, BLK), :].rearrange("(q p) c -> p q c", p=P),
                             rowsof(new)).then_inc(final, 16)
            sp.wait_ge(new_ready, 1 + blocks(MID, 3, NBLK))
            left = N - (NBLK - 1) * BLK
            assert left <= P
            sp.dma_start(out[(NBLK - 1) * BLK:N, :], new[0:left, 0:P]).then_inc(final, 16)
            sp.wait_ge(final, 1 + 16 * NBLK)

        @block.gpsimd
        def _(pool):
            nc.gpsimd.memset(ones[:, :], 1.0).then_inc(built, 1)
            nc.gpsimd.iota(win_iota[:, :], [[1, WIN]], base=0, channel_multiplier=0,
                           allow_small_or_imprecise_dtypes=True).then_inc(built, 1)
            pool.wait_ge(built, 2)
            nc.gpsimd.affine_select(out=ident[:, :], in_=ones[:, :], compare_op=ALU.is_equal, fill=0.0, base=0,
                                    pattern=[[-1, P]], channel_multiplier=1).then_inc(built, 1)
            n = 3
            for size, tens, count in ((P // 4, head_of[4], 4), (P // 8, head_of[8], 8),
                                      (K, row_head[8], 8)):
                nc.gpsimd.affine_select(out=tens[:, :], in_=ones[:, 0:count], compare_op=ALU.is_ge, fill=0.0,
                                        base=0, pattern=[[-size, count]], channel_multiplier=1).then_inc(built, 1)
                n += 1
                pool.wait_ge(built, n)
                nc.gpsimd.affine_select(out=tens[:, :], in_=tens[:, :], compare_op=ALU.is_ge, fill=0.0,
                                        base=size - 1, pattern=[[size, count]],
                                        channel_multiplier=-1).then_inc(built, 1)
                n += 1
            nc.gpsimd.memset(minus_half[:, :], -0.5)
            for unused in (sflat, segm, lastm, brk):
                nc.gpsimd.memset(unused[:], 0.0)
            nc.gpsimd.memset(runmax[:, :], -BIG).then_inc(built, 1)
            assert n + 1 == N_BUILT, n

            def node_norms(l, k):
                for j in range(NORMS[l]):
                    pool.wait_ge(var_ready, 1 + norms_before(l, k) + j + 1)
                    nc.gpsimd.tensor_tensor(rstd[:, :], varn[:, :], minus_half[:, :], ALU.pow).then_inc(rstd_ready, 1)

            for l in range(LAYERS):
                if l:
                    with pool.Fori(0, NBLK) as k:
                        node_norms(l - 1, k)
                pool.wait_ge(stored, 1 + 32 * NBLK * (l + 1))
                with pool.Fori(0, PAIRS) as i:
                    for b in range(2):
                        pool.wait_ge(idx_loaded[b], 1 + 16 * (uses(l, i) + 1))
                        if l == 0:
                            pool.wait_ge(hidden[b], 1 + GR * i)
                        else:
                            pool.wait_ge(messages[b], 1 + guses(l, i))
                            if l == 1:
                                pool.wait_ge(summed[b], 1 + PAIRS)
                        pool.sem_inc(gather_paced, 1)
                        for t in range(K):
                            nc.gpsimd.indirect_dma_start(
                                G[:, b, t, 0:width[l]], None, rows[l],
                                bass.IndirectOffsetOnAxis(idx[:, b, t:t + 1], 0)).then_inc(gathered[l][b], 16)
            pool.wait_ge(bn_var, 1 + 1)
            nc.gpsimd.tensor_tensor(bnsc[:, 0:1], bnsc[:, 0:1], minus_half[:, 0:1], ALU.pow).then_inc(bn_rstd, 1)
            with pool.Fori(0, NBLK) as k:
                node_norms(3, k)

        @block.tensor
        def _(pe):
            pe.wait_ge(loaded, 16 * N_LOADS)
            pe.wait_ge(built, N_BUILT)
            for k, w in enumerate((wext[1][:, 0:P], wside[:, 0, :], wside[:, 1, :], wext[3][:, 0:P])):
                nc.tensor.transpose(ps_t[:, k * P:(k + 1) * P], w, ident[:, :])
            for k in range(4):
                nc.tensor.matmul(ps_mT[:, k * P:(k + 1) * P], ones[0:1, :], rowv[0:1, k, :], start=True, stop=True)
            pe.wait_ge(step, STEP_FIRST)
            for k in range(PIECES):
                last = nc.tensor.matmul(ps[:, k, 0:PIECE], ones[0:1, :],
                                        acc[0:1, k * PIECE:(k + 1) * PIECE], start=True, stop=True)
            last.then_inc(setup_pe, 1)
            pe.wait_ge(step, STEP_ATT)
            for k, (w, h) in enumerate(((0, 4), (0, 4), (1, 4), (2, 4), (3, 8), (3, 8))):
                nc.tensor.matmul(ps_e[:, k * HM:k * HM + h], wT[:, w, :], att[:, k, 0:h], start=True, stop=True)
            nc.tensor.matmul(ps_e[0:1, 64:68], col("L2_gnn_b_src"), att[:, 2, 0:4], start=True, stop=True)
            nc.tensor.matmul(ps_e[0:1, 68:72], col("L2_gnn_b_dst"), att[:, 3, 0:4],
                             start=True, stop=True)
            for k, heads in enumerate((head_of[4], head_of[8], late4)):
                h = heads.shape[1]
                last = nc.tensor.transpose(ps[0:h, 6, k * P:(k + 1) * P], heads[:, :], ident[:, :])
            last.then_inc(setup_pe, 1)
            pe.wait_ge(setup_copied, 1)

            def turn(dst, src, signal):
                for q in range(Q):
                    last = nc.tensor.transpose(dst[:, q * P:(q + 1) * P], src[:, q * P:(q + 1) * P], ident[:, :])
                last.then_inc(signal, 1)

            def node_block(l, k):
                pe.wait_ge(x_in, 1 + blocks(ALL, l, k) + 1)
                if l in SOME:
                    turn(pn_t, old, old_turned)
                n = blocks((l,), l, k)
                if l in (0, 1, 2):
                    H = HEADS[l]
                    sp_ = ones[0:1, :] if l == 0 else spread[0:H, 0, :]
                    last = nc.tensor.matmul(pn_n, sp_, hst[0:H, :], start=True, stop=True)
                    if l == 1:
                        last = nc.tensor.matmul(pn_max, spread[:, 2, :], hst[:, :], start=True, stop=True)
                    last.then_inc(wide_out, 1)
                if l == 0:
                    pe.wait_ge(agg_in, 1 + n + 1)
                    nc.tensor.matmul(pn_a, w2[:, :], f1, start=True, stop=False)
                    nc.tensor.matmul(pn_a, rowv[0:1, RW["L0_gnn_b2"], :], f2[0:1, :], start=False,
                                     stop=True).then_inc(agg_out, 1)
                    pe.wait_ge(old_copied, 1 + blocks(SOME, l, k) + 1)
                    pe.wait_ge(agg_copied, 1 + n + 1)
                    nc.tensor.matmul(pn_b, u1[:, 0, :], xt, start=True, stop=False)
                    nc.tensor.matmul(pn_b, u1[:, 1, :], f3, start=False, stop=True).then_inc(hid_out, 1)
                    pe.wait_ge(hid_ready, 1 + n + 1)
                    nc.tensor.matmul(pn_c, u2[:, :], f4, start=True, stop=True).then_inc(upd_out, 1)
                if l == 1:
                    pe.wait_ge(old_copied, 1 + blocks(SOME, l, k) + 1)
                    nc.tensor.matmul(pn_a, wsk[:, :], xt, start=True, stop=True)
                    nc.tensor.matmul(pn_b, wext[1][:, 0:P], xt, start=True, stop=True)
                    nc.tensor.matmul(pn_c, wexp[:, 0, :], xt, start=True, stop=True)
                    nc.tensor.matmul(pn_d, wexp[:, 1, :], xt, start=True, stop=True).then_inc(self_out, 1)
                if l >= 0:
                    pe.wait_ge(feat_ready, 1 + blocks(MID, l, k) + 1)
                    turn(pn_n, feat, feat_turned)
                if l < 3:
                    if l >= 0:
                        pe.wait_ge(new_ready, 1 + blocks(MID, l, k) + 1)
                    turn(pn_t, new, new_turned)
                    pe.wait_ge(new_copied, 1 + blocks(MORE, l, k) + 1)
                    w = w1 if l == -1 else wext[l + 1]
                    cw = w.shape[1]
                    bias = {-1: 0, 1: 1}.get(l)
                    for q in range(Q):
                        last = nc.tensor.matmul(pn_tab[:, q, 0:cw], xt[:, q * P:(q + 1) * P], w[:, :],
                                                start=True, stop=bias is None)
                        if bias is not None:
                            last = nc.tensor.matmul(pn_tab[:, q, 0:cw], ones[0:1, :], brow[0:1, bias, 0:cw],
                                                    start=False, stop=True)
                    last.then_inc(tab_out, 1)
                    pe.wait_ge(tab_ready, 1 + blocks(MORE, l, k) + 1)

            def turn_membership(l, i, b):
                pe.wait_ge(memb_ready, 1 + chunks(l, i, b) + 1)
                pe.wait_ge(memb_copied, 1 + chunks(l, i, b))
                for g in range(GR):
                    n = tiles_of(g) * WIN
                    last = nc.tensor.transpose(ps_mT[0:n, g * P:(g + 1) * P],
                                               memb[:, b, g * P:g * P + n], ident[:, :])
                last.then_inc(memb_turned, 1)

            def front_mlp(l, i, b, prev):
                c = chunks(l, i, b)
                turn_membership(l, i, b)
                if prev:
                    sums(l, *prev, 0, 8)
                pe.wait_ge(ef_loaded[b], 1 + 16 * (i + 1))
                pe.wait_ge(win_loaded[l][b], 1 + 16 * K * (i + 1))
                pe.wait_ge(memb_copied, 1 + c + 1)
                for g in range(GR):
                    if g == 0:
                        pe.wait_ge(pre_added[GR - 1], 1 + c)
                    elif g < GR - 1:
                        pe.wait_ge(pre_added[g], 1 + c)
                    else:
                        if prev:
                            sums(l, *prev, 8, K)
                        pe.wait_ge(pre_added[0], 1 + c + 1)
                    for q in range(tiles_of(g)):
                        t = slice((4 * g + q) * P, (4 * g + q + 1) * P)
                        last = nc.tensor.matmul(ps_pre[g][:, q * P:(q + 1) * P], lhs[:, b, t],
                                                wtab[0:ED + WIN, b, t], start=True, stop=True)
                    last.then_inc(pre_ready[g][b], 1)

            def front_attention(l, i, b, prev):
                g_ = gchunks(l, i, b)
                H = HEADS[l]
                JH = K * H
                turn_membership(l, i, b)
                pe.wait_ge(sc_copied, 1 + g_ + 1)
                pe.wait_ge(run_ready, 1 + g_)
                nc.tensor.transpose(ps_t[:, 0:P], sflat[:, :], ident[:, :]).then_inc(sc_turned, 1)
                if prev:
                    sums(l, *prev, 0, 1)
                pe.wait_ge(last_masked, 1 + g_ + 1)
                nc.tensor.matmul(ps_last[0:H, :], lastm[:, 0:H], row_tile[H][:, :],
                                 start=True, stop=True).then_inc(last_ready, 1)
                pe.wait_ge(fac_masked, 1 + g_)
                pe.wait_ge(seg_all, 1 + g_ + 1)
                nc.tensor.transpose(ps_e[:, O_SEG:O_SEG + P], segm[:, :], ident[:, :]).then_inc(seg_turned, 1)
                if l == 1:
                    nc.tensor.transpose(ps_brk[:, 0:P], brk[:, b, :], ident[:, :]).then_inc(brkT_ready, 1)
                pe.wait_ge(memb_copied, 1 + chunks(l, i, b) + 1)
                pe.wait_ge(win_loaded[l][b], 1 + 16 * K * (i + 1))
                for g in range(GR):
                    n = tiles_of(g)
                    last = nc.tensor.matmul(ps_e[:, O_DST + 4 * g * H:O_DST + (4 * g + n) * H],
                                            membT[0:n * WIN, g * P:(g + 1) * P],
                                            wtab[0:n * WIN, b, g * BLK:g * BLK + n * H], start=True, stop=True)
                last.then_inc(dst_ready[b], 1)
                pe.wait_ge(cdiag_ready, 1 + g_ + 1)
                nc.tensor.matmul(ps_e[:, O_CAR:O_CAR + JH], ones[0:H, :], cdiag[0:H, 0:JH],
                                 start=True, stop=True).then_inc(carry_spread, 1)
                if prev:
                    sums(l, *prev, 1, K)

            def spread_factors(l, i, b):
                g_ = gchunks(l, i, b)
                JH = K * HEADS[l]
                pe.wait_ge(factor_ready, 1 + g_ + 1)
                nc.tensor.matmul(ps_e[:, O_FAC:O_FAC + JH], ones[0:1, :], prow[0:1, 0:JH],
                                 start=True, stop=True).then_inc(fac_spread, 1)

            def sums(l, i, b, t0, t1):
                H = HEADS[l]
                if t0 == 0:
                    pe.wait_ge(added[b], 1 + K * uses(l, i))
                    pe.wait_ge(weighed[b], 1 + K * uses(l, i))
                    if l:
                        pe.wait_ge(messages[b], 1 + guses(l, i) + 1)
                for t in range(t0, t1):
                    if l == 0 and (t % 4 == 0 or t == t0):
                        pe.wait_ge(hidden[b], 1 + GR * i + t // 4 + 1)
                    m = memb[:, b, t * WIN:(t + 1) * WIN]
                    o = slice(t * WIN, (t + 1) * WIN)
                    nc.tensor.matmul(ps_msg[b][:, o], msg[:, b, t, :], m, start=True, stop=True)
                    if l == 0:
                        wgt = ones[:, 0:1]
                    else:
                        wgt = prob[:, b, t:t + (ROWS[l] - 1) * K + 1:K]
                    last = nc.tensor.matmul(ps_wgt[b][0:ROWS[l], o], wgt, m, start=True, stop=True)
                if t1 == K:
                    last.then_inc(summed[b], 1)

            def front(l, i, b, prev):
                (front_attention if l else front_mlp)(l, i, b, prev)

            def factors(l, i, b):
                if l:
                    spread_factors(l, i, b)

            for l in range(LAYERS):
                with pe.Fori(0, NBLK) as k:
                    node_block(l - 1, k)
                front(l, 0, 0, None)
                factors(l, 0, 0)
                front(l, 0, 1, (0, 0))
                with pe.Fori(0, PAIRS - 1) as i:
                    factors(l, i, 1)
                    front(l, i + 1, 0, (i, 1))
                    factors(l, i + 1, 0)
                    front(l, i + 1, 1, (i + 1, 0))
                factors(l, PAIRS - 1, 1)
                sums(l, PAIRS - 1, 1, 0, K)
                pe.wait_ge(added[1], 1 + K * uses(l + 1, 0))
                pe.wait_ge(weighed[1], 1 + K * uses(l + 1, 0))
            with pe.Fori(0, NBLK) as k:
                pe.wait_ge(bn_in, 1 + k + 1)
                pe.wait_ge(bn_done, 1 + k)
                nc.tensor.matmul(pn_n, spread[:, 1, :], hst[:, :], start=True, stop=True).then_inc(bn_wide, 1)
            pe.wait_ge(bn_ready, 1 + 1)
            with pe.Fori(0, NBLK) as k:
                node_block(3, k)

        @block.scalar
        def _(act):
            act.wait_ge(loaded, 16 * N_LOADS)
            act.wait_ge(setup_copied, 1)

            def copy(dst, src):
                return nc.scalar.activation(dst, src, ACT.Copy)

            def node_block(l, k):
                n = blocks((l,), l, k)
                xk = xn[:, bass.ds(k * Q, Q), :]
                if l == -1:
                    act.wait_ge(new_turned, 1 + k)
                    copy(rowsof(new), xk).then_inc(x_in, 1)
                else:
                    act.wait_ge(new_ready, 1 + blocks(MID, l, k))
                    if l < 3:
                        copy(hst[:, :], hacc[:, bass.ds(k * BLK, BLK)])
                    copy(rowsof(old), xk).then_inc(x_in, 1)
                if l in SOME:
                    act.wait_ge(old_turned, 1 + blocks(SOME, l, k) + 1)
                    copy(xt, pn_t).then_inc(old_copied, 1)
                if l == 0:
                    act.wait_ge(agg_out, 1 + n + 1)
                    copy(f3, pn_a).then_inc(agg_copied, 1)
                    act.wait_ge(hid_out, 1 + n + 1)
                    nc.scalar.activation(f4, pn_b, ACT.Relu, bias=col("L0_gnn_c1")).then_inc(hid_ready, 1)
                if l == 1:
                    act.wait_ge(self_diff, 1 + n + 1)
                    nc.scalar.activation(share[:, 4 * BLK:6 * BLK], share[:, 4 * BLK:6 * BLK],
                                         ACT.Exp).then_inc(self_exp, 1)
                if l == 3:
                    act.wait_ge(bn_ready, 1 + 1)
                    act.wait_ge(feat_turned, 1 + blocks(MID, l, k))
                    nc.scalar.activation(feat, acc[:, bass.ds(k * BLK, BLK)], ACT.Relu,
                                         bias=bnsc[:, 1:2], scale=bnsc[:, 0:1]).then_inc(feat_ready, 1)
                if l < 3:
                    act.wait_ge(new_turned, 1 + blocks(MORE, l, k) + 1)
                    copy(xt, pn_t).then_inc(new_copied, 1)
                    if l >= 0:
                        copy(xk, rowsof(new)).then_inc(new_kept, 1)
                    act.wait_ge(tab_out, 1 + blocks(MORE, l, k) + 1)
                    act.wait_ge(stored, 1 + 32 * blocks(MORE, l, k))
                    cw = (w1 if l == -1 else wext[l + 1]).shape[1]
                    copy(tab[:, :, 0:cw], pn_tab[:, :, 0:cw]).then_inc(tab_ready, 1)

            def copy_membership(l, i, b):
                act.wait_ge(memb_turned, 1 + chunks(l, i, b) + 1)
                if l == 0:
                    act.wait_ge(pre_ready[GR - 1][b], 1 + i)
                    for t in range(K):
                        q = t % 4
                        last = copy(lhs[ED:ED + WIN, b, t * P:(t + 1) * P],
                                    ps_mT[q * WIN:(q + 1) * WIN, (t // 4) * P:(t // 4 + 1) * P])
                    last.then_inc(memb_copied, 1)
                    return
                act.wait_ge(dst_ready[1 - b], 1 + guses(l, i) + b)
                full = (K // 4) * P
                copy(membT[:, 0:full], ps_mT[:, 0:full])
                n = tiles_of(GR - 1) * WIN
                copy(membT[0:n, full:full + P], ps_mT[0:n, full:full + P]).then_inc(memb_copied, 1)

            def edge_mlp(l, i, b):
                c = chunks(l, i, b)
                copy_membership(l, i, b)
                for g in range(GR):
                    act.wait_ge(pre_added[g], 1 + c + 1)
                    m = msg[:, b, 4 * g:4 * g + tiles_of(g), :]
                    nc.scalar.activation(m, m, ACT.Relu).then_inc(hidden[b], 1)

            def edge_attention(l, i, b):
                g_ = gchunks(l, i, b)
                H = HEADS[l]
                JH = K * H
                act.wait_ge(gathered[l][b], 16 * K * (i + 1))
                act.wait_ge(diff_ready, 1 + g_)
                copy(sflat[:, 0:JH].rearrange("p (h k) -> p h k", h=H),
                     G[:, b, :, P:P + H].rearrange("p k h -> p h k")).then_inc(sc_copied, 1)
                copy_membership(l, i, b)
                act.wait_ge(diff_ready, 1 + g_ + 1)
                act.wait_ge(fac_spread, 1 + g_)
                nc.scalar.activation(prow[0:1, 0:JH], diff[0:1, 1, 0:JH], ACT.Exp).then_inc(factor_ready, 1)
                act.wait_ge(summed[b], 1 + uses(l, i))
                nc.scalar.activation(prob[:, b, 0:JH], diff[:, 0, 0:JH], ACT.Exp).then_inc(prob_ready, 1)

            for l in range(LAYERS):
                act.wait_ge(added[1], 1 + K * uses(l, 0))
                act.wait_ge(weighed[1], 1 + K * uses(l, 0))
                with act.Fori(0, NBLK) as k:
                    node_block(l - 1, k)
                with act.Fori(0, PAIRS) as i:
                    for b in range(2):
                        (edge_mlp if l == 0 else edge_attention)(l, i, b)
            act.wait_ge(added[1], 1 + K * uses(LAYERS, 0))
            act.wait_ge(weighed[1], 1 + K * uses(LAYERS, 0))
            with act.Fori(0, NBLK) as k:
                act.wait_ge(bn_wide, 1 + k)
                copy(hst[:, :], hacc[:, bass.ds(k * BLK, BLK)]).then_inc(bn_in, 1)
            with act.Fori(0, NBLK) as k:
                node_block(3, k)

        @block.vector
        def _(dve):
            done = [0]

            def link(ins):
                done[0] += 1
                ins.then_inc(step, 1)
                dve.wait_ge(step, done[0])

            dve.wait_ge(loaded, 16 * N_LOADS)
            dve.wait_ge(built, N_BUILT)
            first = acc[0:1, 0:TILES]
            link(nc.vector.tensor_copy(first, base_i[0:1, :]))
            assert done[0] == STEP_FIRST
            nc.vector.tensor_copy(rel[:, :], base_i[:, :])
            for k, (h, name) in enumerate(((4, "L1_gnn_att_src"), (4, "L1_gnn_att_dst"), (4, "L2_gnn_attn_l"),
                                           (4, "L2_gnn_attn_r"), (8, "L3_gnn_att_src"), (8, "L3_gnn_att_dst"))):
                nc.vector.tensor_scalar(att[:, k, 0:h], head_of[h][:, :], col(name), None, ALU.mult)
            nc.vector.tensor_copy(row_head[4][:, :], row_head[8][:, 0:4])
            for h in (4, 8):
                nc.vector.tensor_reduce(row_tile[h][:, :],
                                        ident[:, 0:K * h].rearrange("p (h k) -> p k h", h=h), AX.X, ALU.add)
            nc.vector.tensor_tensor(skipb[:, :], col("L1_gnn_gat_bias"), col("L1_gnn_skip_b"), ALU.add)
            nc.vector.memset(brow[:, :, :], 0.0)
            nc.vector.tensor_copy(wtab[0:ED, :, :].rearrange("p b (k n) -> p (b k) n", k=K),
                                  w1e[:, :].unsqueeze(1).to_broadcast([ED, 2 * K, P]))
            nc.vector.memset(late4[:, 0:4], 0.0)
            nc.vector.tensor_copy(late4[:, 4:8], head_of[4][:, :])
            for h in (4, 8):
                nc.vector.tensor_copy(masks[h][:, 0, :], head_of[h][:, :])
                nc.vector.tensor_copy(masks[h][:, 1, :], ident[:, 0:h])
            link(nc.vector.memset(hacc[:, :], 0.0))
            dve.wait_ge(setup_pe, 1)
            nc.vector.tensor_copy(wT[:, :, :].rearrange("p a n -> p (a n)"), ps_t)
            nc.vector.tensor_copy(bc[:, :, :].rearrange("p a n -> p (a n)"), ps_mT)
            link(nc.vector.tensor_tensor(rel[:, :].rearrange("p (a n) -> p a n", a=PIECES),
                                         rel[:, :].rearrange("p (a n) -> p a n", a=PIECES),
                                         ps[:, 0:PIECES, 0:PIECE], ALU.subtract))
            assert done[0] == STEP_ATT
            t_int = msg[0:CH, 0, :, :].rearrange("p k n -> p (k n)").bitcast(i32)
            t_flt = G[0:CH, :, :, :].rearrange("p b k n -> p (b k n)")[:, 0:K * P]
            brk_all = msg[0:CH, 1, :, :].rearrange("p k n -> p (k n)")
            link(nc.vector.tensor_copy(t_flt, t_int))
            link(nc.vector.tensor_tensor(brk_all[:, 1:K * P], t_flt[:, 1:K * P], t_flt[:, 0:K * P - 1], ALU.not_equal))
            link(nc.vector.tensor_scalar(brk_all[:, 1:K * P], brk_all[:, 1:K * P], -BIG, None, ALU.mult))
            link(nc.vector.memset(msg[0:CH, 1, :, 0:1], -BIG))
            last_i = share[0:1, 0:TILES].bitcast(i32)
            last = share[0:1, TILES:2 * TILES]
            single = share[0:1, 2 * TILES:3 * TILES]
            cont = share[0:1, 3 * TILES:4 * TILES]
            link(nc.vector.tensor_copy(last, last_i))
            nc.vector.memset(cont[:, 0:1], 0.0)
            nc.vector.tensor_tensor(single, first, last, ALU.is_equal)
            link(nc.vector.tensor_tensor(cont[:, 1:TILES], first[:, 1:TILES], last[:, 0:TILES - 1], ALU.is_equal))
            link(nc.vector.tensor_tensor(single, single, cont, ALU.mult))
            link(nc.vector.tensor_scalar(single, single, 1.0, BIG, ALU.subtract, ALU.mult))
            link(nc.vector.tensor_scalar(cont, cont, 1.0, BIG, ALU.subtract, ALU.mult))
            link(nc.vector.memset(notfirst[:, :], 0.0))
            assert done[0] == STEP_TABLES, done
            link(nc.vector.memset(acc[:, :], 0.0))
            dve.wait_ge(setup_pe, 2)
            for l, k in ((1, 0), (2, 2), (3, 4)):
                H = HEADS[l]
                nc.vector.tensor_copy(wext[l][:, P:P + 2 * H].rearrange("p (a h) -> p a h", a=2),
                                      ps_e[:, k * HM:(k + 2) * HM].rearrange("p (a h) -> p a h", a=2)[:, :, 0:H])
            nc.vector.tensor_copy(wexp[:, :, :].rearrange("p a (h c) -> p a h c", h=4),
                                  ps_e[:, 0:2 * HM].rearrange("p (a h) -> p a h", a=2)[:, :, 0:4]
                                  .unsqueeze(3).to_broadcast([P, 2, 4, P // 4]))
            for k, h in enumerate((4, 8, 8)):
                nc.vector.tensor_copy(spread[0:h, k, :], ps[0:h, 6, k * P:(k + 1) * P])
            nc.vector.tensor_copy(brow[0:1, 0, P:2 * P], rowv[0:1, RW["L0_gnn_b1"], :])
            nc.vector.tensor_copy(brow[0:1, 1, 0:P], rowv[0:1, RW["L2_gnn_b_val"], :])
            dve.wait_ge(tables_in, 48)
            nc.vector.tensor_copy(brow[0:1, 1, P:P + 8], ps_e[0:1, 64:72]).then_inc(setup_copied, 1)

            count = [0]

            def node_loop(l, steps, body):
                start = count[0]
                with dve.Fori(0, NBLK) as k:
                    count[0] = start + steps * k
                    made = [0]

                    def then(ins):
                        made[0] += 1
                        ins.then_inc(nvec, 1)
                        dve.wait_ge(nvec, start + steps * k + made[0])

                    body(l, k, then)
                    assert made[0] == steps, (l, made)
                count[0] = start + steps * NBLK

            norms = [0]

            def stretch(a):
                return a.unsqueeze(2).to_broadcast([P, Q, P])

            def layer_norm(then, src, dst):
                for q in range(Q):
                    o = nc.vector.bn_stats(stats[:, q, :], src[:, q, :])
                then(o)
                dve.sem_inc(norm_paced, 1)
                for q in range(Q):
                    o = nc.vector.bn_aggr(mv[:, q, :], stats[:, q, :])
                then(o)
                nc.vector.tensor_scalar(varn[:, :], mv[:, :, 1], EPS_LN, None, ALU.add).then_inc(var_ready, 1)
                norms[0] = norms[0] + 1
                then(nc.vector.tensor_tensor(dst, src, stretch(mv[:, :, 0]), ALU.subtract))
                dve.wait_ge(rstd_ready, 1 + norms[0])
                return nc.vector.tensor_tensor(dst, dst, stretch(rstd[:, :]), ALU.mult)

            def node_block(l, k, then):
                tt, ts, stt = nc.vector.tensor_tensor, nc.vector.tensor_scalar, nc.vector.scalar_tensor_tensor
                norms[0] = norms_before(l, k)
                d = bass.ds(k * BLK, BLK)
                a_sum, a_wgt, a_max = acc[:, d], pn_n, pn_max
                n = blocks((l,), l, k)
                m = blocks(MID, l, k)
                if l < 3:
                    dve.wait_ge(wide_out, 1 + blocks((0, 1, 2), l, k) + 1)
                if l == 0:
                    then(ts(f5, a_wgt, 1.0, None, ALU.max))
                    then(nc.vector.reciprocal(f5, f5))
                    dve.wait_ge(agg_out, 1 + n)
                    then(tt(f1, a_sum, f5, ALU.mult))
                    ts(f2[0:1, :], a_wgt[0:1, :], 1.0, None, ALU.min).then_inc(agg_in, 1)
                    dve.wait_ge(upd_out, 1 + n + 1)
                    dve.wait_ge(feat_turned, 1 + m)
                    stt(feat, pn_c, col("L0_gnn_c2"), xt, ALU.add, ALU.add).then_inc(feat_ready, 1)
                if l == 1:
                    then(ts(f1, a_wgt, 0.0, -BIG, ALU.is_equal, ALU.mult))
                    then(tt(f1, f1, a_max, ALU.add))
                    dve.wait_ge(self_out, 1 + n + 1)
                    tt(f2, f1, pn_c, ALU.max)
                    then(nc.vector.tensor_copy(f3, pn_c))
                    tt(f1, f1, pn_d, ALU.add)
                    tt(f2, f2, pn_d, ALU.add)
                    then(tt(f3, f3, pn_d, ALU.add))
                    f123 = share[:, BLK:4 * BLK]
                    then(stt(f123, f123, SLOPE, f123, ALU.mult, ALU.max))
                    tt(f4, f1, f2, ALU.subtract)
                    tt(f5, f3, f2, ALU.subtract).then_inc(self_diff, 1)
                    dve.wait_ge(self_exp, 1 + n + 1)
                    tt(f1, a_sum, f4, ALU.mult)
                    tt(f2, pn_b, f5, ALU.mult)
                    then(tt(f3, a_wgt, f4, ALU.mult))
                    tt(f1, f1, f2, ALU.add)
                    then(stt(f3, f3, 1e-16, f5, ALU.add, ALU.add))
                    then(nc.vector.reciprocal(f3, f3))
                    then(tt(f1, f1, f3, ALU.mult))
                    dve.wait_ge(feat_turned, 1 + m)
                    stt(feat, pn_a, skipb[:, 0:1], f1, ALU.add, ALU.add).then_inc(feat_ready, 1)
                if l == 2:
                    then(ts(f1, a_wgt, 1e-30, None, ALU.max))
                    then(nc.vector.reciprocal(f1, f1))
                    dve.wait_ge(feat_turned, 1 + m)
                    tt(feat, a_sum, f1, ALU.mult).then_inc(feat_ready, 1)
                dve.wait_ge(feat_turned, 1 + m + 1)
                if l < 3:
                    ts(acc[:, d], acc[:, d], 0.0, None, ALU.mult)
                    ts(hacc[:, d], hacc[:, d], 0.0, None, ALU.mult)
                src, t3 = rowsof(pn_n), rowsof(tmp)
                dve.wait_ge(x_in, 1 + blocks(ALL, l, k) + 1)
                if l in SOME:
                    then(layer_norm(then, src, t3))
                    g, b_ = (bc[:, 2 * l + j, :].unsqueeze(1).to_broadcast([P, Q, P]) for j in range(2))
                    then(tt(t3, t3, g, ALU.mult))
                    then(tt(t3, t3, b_, ALU.add))
                    then(tt(t3, t3, rowsof(old), ALU.add))
                else:
                    then(tt(t3, src, rowsof(old), ALU.add))
                    if l == 3:
                        then(tt(t3, t3, rowsof(old), ALU.add))
                if l < 3:
                    dve.wait_ge(new_turned, 1 + blocks(MORE, l, k))
                    dve.wait_ge(new_kept, 1 + m)
                else:
                    dve.wait_ge(final, 1 + 16 * k)
                layer_norm(then, t3, rowsof(new)).then_inc(new_ready, 1)

            def batch_sums(l, k, then):
                d = bass.ds(k * BLK, BLK)
                dve.wait_ge(bn_wide, 1 + k + 1)
                then(nc.vector.tensor_scalar(f1, pn_n, 1e-16, 1e-30, ALU.add, ALU.max))
                then(nc.vector.reciprocal(f1, f1))
                then(nc.vector.tensor_tensor(f1, acc[:, d], f1, ALU.mult))
                then(nc.vector.tensor_scalar(acc[:, d], f1, col("L3_gnn_bias"), None, ALU.add))
                nc.vector.bn_stats(bnst[:, bass.ds(k, 1), :].rearrange("p o s -> p (o s)"),
                                   acc[:, d]).then_inc(bn_done, 1)

            def make_membership(l, i, b):
                dve.wait_ge(summed[b], 1 + uses(l, i))
                r = rel[:, bass.ds((2 * i + b) * K, K)].unsqueeze(2).to_broadcast([P, K, WIN])
                w = win_iota[:, :].unsqueeze(1).to_broadcast([P, K, WIN])
                nc.vector.tensor_tensor(memb[:, b, :].rearrange("p (k w) -> p k w", k=K), r, w,
                                        ALU.is_equal).then_inc(memb_ready, 1)

            def edge_mlp(l, i, b, prev):
                c = chunks(l, i, b)
                make_membership(l, i, b)
                if prev:
                    add_sums(l, *prev, first_nodes(*prev), 0, K)
                dve.wait_ge(gathered[l][b], 16 * K * (i + 1))
                for g in range(GR):
                    n = tiles_of(g)
                    dve.wait_ge(pre_ready[g][b], 1 + i + 1)
                    nc.vector.tensor_tensor(msg[:, b, 4 * g:4 * g + n, :], G[:, b, 4 * g:4 * g + n, 0:P],
                                            ps_pre[g][:, 0:n * P].rearrange("p (k f) -> p k f", k=n),
                                            ALU.add).then_inc(pre_added[g], 1)

            def edge_attention(l, i, b, prev):
                g_ = gchunks(l, i, b)
                H = HEADS[l]
                JH = K * H
                tt, ts, stt = nc.vector.tensor_tensor, nc.vector.tensor_scalar, nc.vector.scalar_tensor_tensor
                v0 = VEC * g_
                tiles = bass.ds((2 * i + b) * K, K)
                make_membership(l, i, b)
                ts(notfirst[:, :], rel[:, tiles], 0.0, -BIG, ALU.not_equal, ALU.mult).then_inc(vec, 1)
                if prev:
                    first = first_nodes(*prev)
                    add_sums(l, *prev, first, 0, 3)
                dve.wait_ge(brk_loaded[b], 1 + 16 * sum((HEADS[m] + 1) * PAIRS for m in range(1, l))
                            + 16 * (H + 1) * (i + 1))
                dve.wait_ge(sc_turned, 1 + g_ + 1)
                dve.wait_ge(seg_turned, 1 + g_)
                nc.vector.tensor_tensor_scan(segm[0:JH, :], brk[0:JH, b, :], ps_t[0:JH, 0:P], -BIG,
                                             ALU.add, ALU.max).then_inc(seg_fwd, 1)
                dve.wait_ge(seg_fwd, 1 + g_ + 1)
                dve.wait_ge(last_ready, 1 + g_)
                ts(lastm[0:JH, 0:H], row_head[H][0:JH, :], segm[0:JH, P - 1:P], None,
                   ALU.mult).then_inc(last_masked, 1)
                body = segm[0:JH, 0:P - 1][:, ::-1]
                nc.vector.tensor_tensor_scan(body, brk[0:JH, b, 1:P][:, ::-1], body, segm[0:JH, P - 1:P],
                                             ALU.add, ALU.max).then_inc(seg_all, 1)
                if prev:
                    add_sums(l, *prev, first, 3, 4)
                dve.wait_ge(last_ready, 1 + g_ + 1)
                dve.wait_ge(run_kept, 1 + g_ + l - 1)
                nc.vector.tensor_tensor_scan(runmax[0:H, 1:K + 1], join[0:H, b, 0, :], ps_last[0:H, :],
                                             runmax[0:H, 0:1], ALU.add, ALU.max).then_inc(run_ready, 1)
                dve.wait_ge(run_ready, 1 + g_ + 1)
                tt(carry[0:H, :], runmax[0:H, 0:K], join[0:H, b, 1, :], ALU.add).then_inc(carry_ready, 1)
                dve.wait_ge(carry_ready, 1 + g_ + 1)
                nc.vector.tensor_copy(runmax[0:H, 0:1], runmax[0:H, K:K + 1]).then_inc(run_kept, 1)
                dve.wait_ge(carry_spread, 1 + g_)
                tt(cdiag[0:H, 0:JH].rearrange("p (h k) -> p h k", h=H),
                   carry[0:H, :].unsqueeze(1).to_broadcast([H, H, K]),
                   ident[0:H, 0:H].unsqueeze(2).to_broadcast([H, H, K]), ALU.mult).then_inc(cdiag_ready, 1)

                def hk(a):
                    return a.rearrange("p (h k) -> p h k", h=H)

                if prev:
                    add_sums(l, *prev, first, 4, 8)
                s = [scores[:, c, 0:JH] for c in range(3)]
                dst = ps_e[:, O_DST:O_DST + JH].rearrange("p (k h) -> p h k", h=H)
                dve.wait_ge(carry_spread, 1 + g_ + 1)
                tt(hk(s[0]), hk(sflat[:, 0:JH]), dst, ALU.add).then_inc(vec, 1)
                dve.wait_ge(vec, 1 + v0 + 2)
                tt(hk(s[1]), hk(ps_e[:, O_CAR:O_CAR + JH]), notfirst[:, :].unsqueeze(1).to_broadcast([P, H, K]),
                   ALU.add).then_inc(vec, 1)
                dve.wait_ge(vec, 1 + v0 + 3)
                tt(s[2], s[1], ps_e[:, O_SEG:O_SEG + JH], ALU.max).then_inc(vec, 1)
                dve.wait_ge(vec, 1 + v0 + 4)
                if l == 1:
                    dve.wait_ge(brkT_ready, 1 + 2 * i + b + 1)
                    stt(prob[:, b, JH:2 * JH], ps_brk[:, 0:JH], -1.0 / BIG, s[2], ALU.mult, ALU.mult).then_inc(maxf_ready, 1)
                    dve.wait_ge(maxf_ready, 1 + 2 * i + b + 1)
                s12 = scores[:, 1:3, 0:JH].rearrange("p a (h k) -> p a h k", h=H)
                tt(s12, s12, dst.unsqueeze(1).to_broadcast([P, 2, H, K]), ALU.add).then_inc(vec, 1)
                dve.wait_ge(vec, 1 + v0 + 5)
                sall = scores[:, :, 0:JH]
                stt(sall, sall, SLOPE, sall, ALU.mult, ALU.max).then_inc(vec, 1)
                dve.wait_ge(vec, 1 + v0 + 6)
                dve.wait_ge(prob_ready, 1 + g_)
                tt(diff[:, :, 0:JH], scores[:, 0:2, 0:JH],
                   scores[:, 2:3, 0:JH].to_broadcast([P, 2, JH]), ALU.subtract).then_inc(diff_ready, 1)

                if prev:
                    add_sums(l, *prev, first, 8, 10)
                dve.wait_ge(prob_ready, 1 + g_ + 1)
                nc.vector.tensor_tensor(msg[:, b, :, :].rearrange("p k (h c) -> p k h c", h=H),
                                        G[:, b, :, 0:P].rearrange("p k (h c) -> p k h c", h=H),
                                        prob[:, b, 0:JH].rearrange("p (h k) -> p k h", h=H).unsqueeze(3)
                                        .to_broadcast([P, K, H, P // H]),
                                        ALU.mult).then_inc(messages[b], 1)
                if prev:
                    add_sums(l, *prev, first, 10, K)

            def edge_factors(l, i, b):
                g_ = gchunks(l, i, b)
                H = HEADS[l]
                JH = K * H
                dve.wait_ge(fac_spread, 1 + g_ + 1)
                dve.wait_ge(fac_ready, 1 + g_)
                nc.vector.tensor_tensor(facm[:, :, 0:JH].rearrange("p a (h k) -> p a h k", h=H),
                                        ps_e[:, O_FAC:O_FAC + JH].rearrange("p (h k) -> p h k", h=H)
                                        .unsqueeze(1).to_broadcast([P, 2, H, K]),
                                        masks[H][:, :, :].unsqueeze(3).to_broadcast([P, 2, H, K]),
                                        ALU.mult).then_inc(fac_masked, 1)
                dve.wait_ge(fac_masked, 1 + g_ + 1)
                nc.vector.tensor_reduce(fac[:, b, :, :], facm[:, :, 0:JH].rearrange("p a (h k) -> p a k h", h=H),
                                        AX.X, ALU.add).then_inc(fac_ready, 1)

            def first_nodes(i, b):
                return nc.values_load_multi_w_load_instructions(
                    base_i[0:1, bass.ds((2 * i + b) * K, K)], engines=(dve.engine,), min_val=0, max_val=N,
                    skip_runtime_bounds_check_because="targets are node numbers")[1]

            def add_sums(l, i, b, first, t0, t1):
                if t0 == 0:
                    dve.wait_ge(summed[b], 1 + uses(l, i) + 1)
                    if l:
                        dve.wait_ge(fac_ready, 1 + gchunks(l, i, b) + 1)
                R = ROWS[l]
                for t in range(t0, t1):
                    def after(done):
                        if t:
                            dve.wait_ge(done[b], 1 + K * uses(l, i) + t)
                        else:
                            dve.wait_ge(done[1 - b], 1 + K * (uses(l, i) + b))

                    w = slice(t * WIN, (t + 1) * WIN)
                    d = bass.ds(first[t], WIN)
                    node, wgt = acc[:, d], hacc[0:R, d]
                    after(added)
                    if l == 0:
                        nc.vector.tensor_tensor(node, node, ps_msg[b][:, w], ALU.add).then_inc(added[b], 1)
                    else:
                        nc.vector.scalar_tensor_tensor(node, node, fac[:, b, 0, t:t + 1], ps_msg[b][:, w],
                                                       ALU.mult, ALU.add).then_inc(added[b], 1)
                    after(weighed)
                    if l == 0:
                        nc.vector.tensor_tensor(wgt, wgt, ps_wgt[b][0:R, w], ALU.add).then_inc(weighed[b], 1)
                    else:
                        nc.vector.scalar_tensor_tensor(wgt, wgt, fac[0:R, b, 1, t:t + 1], ps_wgt[b][0:R, w],
                                                       ALU.mult, ALU.add).then_inc(weighed[b], 1)

            def front(l, i, b, prev):
                (edge_attention if l else edge_mlp)(l, i, b, prev)

            def factors(l, i, b):
                if l:
                    edge_factors(l, i, b)

            STEPS = {0: 13, 1: 19, 2: 6, 3: 5}
            for l in range(LAYERS):
                if l in (1, 3):
                    nc.vector.memset(wtab[:, :, :], 0.0).then_inc(wtab_clear, 1)
                if l:
                    node_loop(l - 1, STEPS[l - 1], node_block)
                    nc.vector.memset(runmax[:, :], -BIG).then_inc(run_kept, 1)
                front(l, 0, 0, None)
                factors(l, 0, 0)
                front(l, 0, 1, None)
                with dve.Fori(0, PAIRS - 1) as i:
                    factors(l, i, 1)
                    front(l, i + 1, 0, (i, 0))
                    factors(l, i + 1, 0)
                    front(l, i + 1, 1, (i, 1))
                factors(l, PAIRS - 1, 1)
                for b in range(2):
                    add_sums(l, PAIRS - 1, b, first_nodes(PAIRS - 1, b), 0, K)
            node_loop(3, 4, batch_sums)
            dve.wait_ge(bn_done, 1 + NBLK)
            start = count[0]
            left = N - (NBLK - 1) * BLK
            nth = [start]

            def then(ins):
                nth[0] += 1
                ins.then_inc(nvec, 1)
                dve.wait_ge(nvec, nth[0])

            then(nc.vector.bn_stats(bnst[:, NBLK - 1, :], acc[:, (NBLK - 1) * BLK:N]))
            then(nc.vector.bn_aggr(bnmv[:, :], bnst[:, :, :].rearrange("p k s -> p (k s)")))
            nc.vector.tensor_scalar(bnsc[:, 0:1], bnmv[:, 1:2], EPS_LN, None, ALU.add).then_inc(bn_var, 1)
            dve.wait_ge(bn_rstd, 1 + 1)
            then(nc.vector.tensor_tensor(bnsc[:, 0:1], bnsc[:, 0:1], col("L3_gnn_gamma"), ALU.mult))
            then(nc.vector.tensor_tensor(bnsc[:, 2:3], bnmv[:, 0:1], bnsc[:, 0:1], ALU.mult))
            nc.vector.tensor_tensor(bnsc[:, 1:2], col("L3_gnn_beta"), bnsc[:, 2:3], ALU.subtract).then_inc(bn_ready, 1)
            count[0] = nth[0]
            node_loop(3, STEPS[3], node_block)


def _lay(a, pad, value):
    import numpy as np
    return np.pad(a, [(0, pad)] + [(0, 0)] * (a.ndim - 1), constant_values=value)


def kernel(**inputs):
    import numpy as np
    import concourse.bacc as bacc
    from concourse.bass_utils import run_bass_kernel_spmd

    P, K = 128, 13
    a = {k: np.ascontiguousarray(v) for k, v in inputs.items()}
    n = a["x"].shape[0]
    edges = a["src"].shape[0]
    chunks = -(-edges // (P * K))
    pad = chunks * P * K - edges
    arrays = {}
    for name, v in a.items():
        if name.startswith("L1_gnn_att_") or name.startswith("L2_gnn_attn") or name.startswith("L3_gnn_att_"):
            v = v.reshape(-1)
        arrays[name] = v
    arrays["x"] = _lay(a["x"], -n % 512, 0)
    arrays["src"] = np.ascontiguousarray(_lay(a["src"], pad, 0).reshape(chunks, K, P).transpose(0, 2, 1))
    dst = _lay(a["dst"], pad, n)
    del arrays["dst"]
    arrays["dst_cols"] = np.ascontiguousarray(dst.reshape(chunks * K, P).T)
    arrays["dst_rows"] = np.ascontiguousarray(dst.reshape(chunks, K * P))
    arrays["edge_attr_64"] = np.ascontiguousarray(_lay(a["edge_attr_64"], pad, 0).T)

    nc = bacc.Bacc("TRN2", target_bir_lowering=False, num_devices=1, dynamic_dma_scratch_size=8192)
    aps, fed = {}, {}
    for name, v in arrays.items():
        aps[name] = nc.dram_tensor(f"in_{name}", v.shape, mybir.dt.from_np(v.dtype), kind="ExternalInput").ap()
        fed[f"in_{name}"] = v
    out = nc.dram_tensor("out", (n, P), mybir.dt.float32, kind="ExternalOutput").ap()
    gnn_program(nc, aps, out)
    r = run_bass_kernel_spmd(nc, [fed], core_ids=[0])
    return r.results[0]["out"]
```
